# Optimizing a Trainium2 kernel written in Bass

```python
import numpy as np
import jax
import jax.numpy as jnp

def _softmax(x, axis=-1):
    return jax.nn.softmax(x, axis=axis)

def _gelu(x):
    return jax.nn.gelu(x, approximate=True)

def _silu(x):
    return jax.nn.silu(x)

def _sigmoid(x):
    return jax.nn.sigmoid(x)

def _layernorm(x, axis=-1, eps=1e-05):
    m = jnp.mean(x, axis=axis, keepdims=True)
    v = jnp.var(x, axis=axis, keepdims=True)
    return (x - m) / jnp.sqrt(v + eps)

def _scatter_add(tgt, idx, src, axis=0):
    return tgt.at[idx].add(src)

def _segment_sum(src, seg, n):
    return jax.ops.segment_sum(src, seg, n)
kernel_name = 'mk_hybrid_d1_jaxref_r8_4a864f'

def setup_inputs(seed: int=0):
    np.random.seed(seed)
    _w = jnp.asarray

    def _L0_attn_a_setup():
        import jax, jax.numpy as jnp
        import numpy as np
        EPS = 1e-05

        def layer_norm(x, g, b):
            mu = jnp.mean(x, axis=-1, keepdims=True)
            var = jnp.mean((x - mu) ** 2, axis=-1, keepdims=True)
            return (x - mu) * jax.lax.rsqrt(var + EPS) * g + b

        def quantum_circuit(v):
            return jnp.cumprod(jnp.cos(v), axis=-1)
        key = jax.random.key(seed)
        ks = jax.random.split(key, 8)
        B, T, C, H = (4, 256, 128, 16)
        dk = C // H
        nq_ffn, ffn_dim = (16, 512)
        return {'x': jax.random.normal(ks[0], (B, T, C), dtype=jnp.float32) * 0.5, 'attn_circuit_params': jax.random.normal(ks[1], (H, dk), dtype=jnp.float32), 'ffn_circuit_params': jax.random.normal(ks[2], (nq_ffn,), dtype=jnp.float32), 'w1': jax.random.normal(ks[3], (ffn_dim, nq_ffn), dtype=jnp.float32) * 0.1, 'b1': jnp.zeros((ffn_dim,), dtype=jnp.float32), 'w2': jax.random.normal(ks[4], (C, ffn_dim), dtype=jnp.float32) * 0.02, 'b2': jnp.zeros((C,), dtype=jnp.float32), 'gamma1': jnp.ones((C,), dtype=jnp.float32), 'beta1': jnp.zeros((C,), dtype=jnp.float32), 'gamma2': jnp.ones((C,), dtype=jnp.float32), 'beta2': jnp.zeros((C,), dtype=jnp.float32)}
    _L0_attn_a_in = _L0_attn_a_setup()

    def _L0_attn_b_setup():
        import jax, jax.numpy as jnp
        import numpy as np
        B, N, D_IN, D_OUT, H = (2, 256, 128, 128, 16)
        HEAD_DIM = D_OUT // H
        key = jax.random.key(seed)
        ks = jax.random.split(key, 8)
        s = 0.02
        return {'x': jax.random.normal(ks[0], (B, N, D_IN), dtype=jnp.float32), 'Wq': jax.random.normal(ks[1], (D_IN, D_OUT), dtype=jnp.float32) * s, 'Wk': jax.random.normal(ks[2], (D_IN, D_OUT), dtype=jnp.float32) * s, 'Wv': jax.random.normal(ks[3], (D_IN, D_OUT), dtype=jnp.float32) * s, 'Wo': jax.random.normal(ks[4], (D_OUT, D_OUT), dtype=jnp.float32) * s, 'bo': jnp.zeros((D_OUT,), dtype=jnp.float32), 'w': jax.random.uniform(ks[5], (H,), dtype=jnp.float32), 'v': jax.random.uniform(ks[6], (H,), dtype=jnp.float32)}
    _L0_attn_b_in = _L0_attn_b_setup()

    def _L0_ffn_setup():
        import jax, jax.numpy as jnp
        import numpy as np
        D = 128
        H = 512
        E = 8
        B, N = (2, 256)
        key = jax.random.key(seed)
        ks = jax.random.split(key, 5)
        x = jax.random.normal(ks[0], (B, N, D), dtype=jnp.float32)
        W1 = jax.random.normal(ks[1], (E, D, H), dtype=jnp.float32) / np.sqrt(D)
        W2 = jax.random.normal(ks[2], (E, H, D), dtype=jnp.float32) / np.sqrt(H)
        Wg = jax.random.normal(ks[3], (D, E), dtype=jnp.float32) / np.sqrt(D)
        bg = jax.random.normal(ks[4], (E,), dtype=jnp.float32) * 0.01
        return {'x': x, 'W1': W1, 'W2': W2, 'Wg': Wg, 'bg': bg}
    _L0_ffn_in = _L0_ffn_setup()
    _d = {'L0_attn_a_x': _L0_attn_a_in['x'], 'L0_attn_a_attn_circuit_params': _L0_attn_a_in['attn_circuit_params'], 'L0_attn_a_ffn_circuit_params': _L0_attn_a_in['ffn_circuit_params'], 'L0_attn_a_w1': _L0_attn_a_in['w1'], 'L0_attn_a_b1': _L0_attn_a_in['b1'], 'L0_attn_a_w2': _L0_attn_a_in['w2'], 'L0_attn_a_b2': _L0_attn_a_in['b2'], 'L0_attn_a_gamma1': _L0_attn_a_in['gamma1'], 'L0_attn_a_beta1': _L0_attn_a_in['beta1'], 'L0_attn_a_gamma2': _L0_attn_a_in['gamma2'], 'L0_attn_a_beta2': _L0_attn_a_in['beta2'], 'L0_attn_b_Wq': _L0_attn_b_in['Wq'], 'L0_attn_b_Wk': _L0_attn_b_in['Wk'], 'L0_attn_b_Wv': _L0_attn_b_in['Wv'], 'L0_attn_b_Wo': _L0_attn_b_in['Wo'], 'L0_attn_b_bo': _L0_attn_b_in['bo'], 'L0_attn_b_w': _L0_attn_b_in['w'], 'L0_attn_b_v': _L0_attn_b_in['v'], 'L0_ffn_W1': _L0_ffn_in['W1'], 'L0_ffn_W2': _L0_ffn_in['W2'], 'L0_ffn_Wg': _L0_ffn_in['Wg'], 'L0_ffn_bg': _L0_ffn_in['bg']}
    _x0 = _d['L0_attn_a_x']
    _d['L0_attn_a_x'] = jax.random.normal(jax.random.fold_in(jax.random.key(seed), 1), (16, 256, 128), dtype=_x0.dtype)
    del _x0
    return _d

def reference(L0_attn_a_x, L0_attn_a_attn_circuit_params, L0_attn_a_ffn_circuit_params, L0_attn_a_w1, L0_attn_a_b1, L0_attn_a_w2, L0_attn_a_b2, L0_attn_a_gamma1, L0_attn_a_beta1, L0_attn_a_gamma2, L0_attn_a_beta2, L0_attn_b_Wq, L0_attn_b_Wk, L0_attn_b_Wv, L0_attn_b_Wo, L0_attn_b_bo, L0_attn_b_w, L0_attn_b_v, L0_ffn_W1, L0_ffn_W2, L0_ffn_Wg, L0_ffn_bg):

    def _L0_attn_a_ref(x, attn_circuit_params, ffn_circuit_params, w1, b1, w2, b2, gamma1, beta1, gamma2, beta2):
        import jax, jax.numpy as jnp
        import numpy as np
        EPS = 1e-05

        def layer_norm(x, g, b):
            mu = jnp.mean(x, axis=-1, keepdims=True)
            var = jnp.mean((x - mu) ** 2, axis=-1, keepdims=True)
            return (x - mu) * jax.lax.rsqrt(var + EPS) * g + b

        def quantum_circuit(v):
            return jnp.cumprod(jnp.cos(v), axis=-1)
        B, T, C = x.shape
        H, dk = attn_circuit_params.shape
        nq = ffn_circuit_params.shape[0]
        xh = x.reshape(B, T, H, dk)
        attn_out = quantum_circuit(xh).reshape(B, T, C)
        x1 = layer_norm(x + attn_out, gamma1, beta1)
        q = quantum_circuit(x1[..., :nq])
        h = jnp.einsum('btq,fq->btf', q, w1) + b1
        ffn_out = jnp.einsum('btf,cf->btc', jax.nn.relu(h), w2) + b2
        return layer_norm(x1 + ffn_out, gamma2, beta2)

    def _L0_attn_b_ref(x, Wq, Wk, Wv, Wo, bo, w, v):
        import jax, jax.numpy as jnp
        import numpy as np
        B, N, D_IN, D_OUT, H = (2, 256, 128, 128, 16)
        HEAD_DIM = D_OUT // H
        b, n, _ = x.shape
        h = w.shape[0]
        hd = Wq.shape[1] // h

        def proj(W):
            return (x @ W).reshape(b, n, h, hd).transpose(0, 2, 1, 3)
        q, k, val = (proj(Wq), proj(Wk), proj(Wv))
        pos = jnp.arange(n)
        R = jnp.abs(pos[:, None] - pos[None, :]).astype(x.dtype)
        wv = w[:, None, None]
        vv = v[:, None, None]
        R_hat = (1.0 + jnp.exp(vv)) / (1.0 + jnp.exp(vv - wv * R))
        scores = jax.nn.relu(jnp.einsum('bhqd,bhkd->bhqk', q, k)) * R_hat[None]
        causal = jnp.triu(jnp.ones((n, n), dtype=bool), k=1)
        scores = jnp.where(causal[None, None], -jnp.inf, scores)
        attn = jax.nn.softmax(scores / np.sqrt(hd).astype(x.dtype), axis=-1)
        ctx = jnp.einsum('bhqk,bhkd->bhqd', attn, val)
        ctx = ctx.transpose(0, 2, 1, 3).reshape(b, n, h * hd)
        return ctx @ Wo + bo

    def _L0_ffn_ref(x, W1, W2, Wg, bg):
        import jax, jax.numpy as jnp
        import numpy as np
        D = 128
        H = 512
        E = 8
        B, N = (2, 256)
        b, n, d = x.shape
        e = Wg.shape[1]
        xf = x.reshape(b * n, d)
        logits = xf @ Wg + bg
        one_hot = jax.nn.one_hot(jnp.argmax(logits, axis=-1), e, dtype=x.dtype)
        h = jax.nn.gelu(jnp.einsum('td,edh->eth', xf, W1), approximate=True)
        y = jnp.einsum('eth,ehd->etd', h, W2)
        out = jnp.einsum('etd,te->td', y, one_hot)
        return out.reshape(b, n, d)
    x = L0_attn_a_x
    x = x + _L0_attn_a_ref(_layernorm(x, axis=-1), L0_attn_a_attn_circuit_params, L0_attn_a_ffn_circuit_params, L0_attn_a_w1, L0_attn_a_b1, L0_attn_a_w2, L0_attn_a_b2, L0_attn_a_gamma1, L0_attn_a_beta1, L0_attn_a_gamma2, L0_attn_a_beta2)
    x = x + _L0_ffn_ref(_layernorm(x, axis=-1), L0_ffn_W1, L0_ffn_W2, L0_ffn_Wg, L0_ffn_bg)
    x = x + _L0_attn_b_ref(_layernorm(x, axis=-1), L0_attn_b_Wq, L0_attn_b_Wk, L0_attn_b_Wv, L0_attn_b_Wo, L0_attn_b_bo, L0_attn_b_w, L0_attn_b_v)
    x = x + _L0_ffn_ref(_layernorm(x, axis=-1), L0_ffn_W1, L0_ffn_W2, L0_ffn_Wg, L0_ffn_bg)
    return x

_drawn_inputs = setup_inputs


def setup_inputs(seed=0):
    import zlib

    import numpy as np

    out = dict(_drawn_inputs(seed))
    spreads = {'L0_attn_a_b1': (0.0, 0.1),
     'L0_attn_a_b2': (0.0, 0.1),
     'L0_attn_a_gamma1': (1.0, 0.2),
     'L0_attn_a_beta1': (0.0, 0.1),
     'L0_attn_a_gamma2': (1.0, 0.2),
     'L0_attn_a_beta2': (0.0, 0.1),
     'L0_attn_b_bo': (0.0, 0.1)}
    factors = {'L0_attn_b_Wq': 8.0,
     'L0_attn_b_Wk': 8.0,
     'L0_attn_b_Wv': 2.732,
     'L0_attn_b_Wo': 2.816,
     'L0_attn_b_w': 8.0,
     'L0_attn_b_v': 8.0}
    for name, (base, spread) in spreads.items():
        noise = np.random.default_rng([zlib.crc32(name.encode()), seed]).standard_normal(out[name].shape)
        drawn = base * np.exp(spread * noise) if base else spread * noise
        out[name] = jnp.asarray(drawn.astype(out[name].dtype))
    for name, factor in factors.items():
        out[name] = (out[name] * factor).astype(out[name].dtype)
    return out
```

```python
from contextlib import ExitStack
import concourse.bass as bass
import concourse.mybir as mybir
import numpy as np

FP32 = mybir.dt.float32
BF16 = mybir.dt.bfloat16
I32 = mybir.dt.int32
U32 = mybir.dt.uint32
ALU = mybir.AluOpType
ACT = mybir.ActivationFunctionType
AX = mybir.AxisListType

P = 128
BATCH, SEQ, C = 16, 256, 128
TOK = BATCH * SEQ
NT = TOK // P
NE, HID = 8, 512
NHC = HID // P
SLOT_TILES = NT + NE
EPS = 1e-5
ROUND = 1.5 * 2.0 ** 23
NQ, FFN = 16, 512
NFC = FFN // P
NH, HD = 16, 8


INV_2PI = 1.0 / (2.0 * np.pi)
TWO_PI = float(np.float32(2.0 * np.pi))
TWO_PI_HI = 6.28125
TWO_PI_LO = 2.0 * np.pi - TWO_PI_HI


class Steps:

    def __init__(self, eng, sem, run, per_run):
        self.eng, self.sem, self.base, self.per_run, self.n = eng, sem, run * per_run, per_run, 0

    def __call__(self, ins):
        self.n += 1
        ins.then_inc(self.sem, 1)
        self.eng.wait_ge(self.sem, self.base + self.n)

    def end(self):
        assert self.n == self.per_run


def block_a(nc, x, y, t1, t2, xb, w, const):
    CT = 4
    NCH = NT // CT
    N = CT * C
    with ExitStack() as stack:
        def sb(name, shape, dt=FP32):
            return stack.enter_context(nc.sbuf_tensor("a_" + name, shape, dt))

        def bank(name, shape):
            return stack.enter_context(nc.psum_tensor("a_" + name, shape, FP32))

        def sem(name):
            return stack.enter_context(nc.semaphore("a_" + name))

        NORMS = ("in", "mid", "out", "moe")
        stats = {n: sb("stats_" + n, [P, CT, 6]) for n in NORMS}
        mv = {n: sb("mv_" + n, [P, CT, 2]) for n in NORMS}
        vare = {n: sb("vare_" + n, [P, CT]) for n in NORMS}
        rstd = {n: sb("rstd_" + n, [P, CT]) for n in NORMS}
        ang = sb("ang", [P, CT * NQ])
        turns = sb("turns", [P, CT * NQ])
        qT = sb("qT", [NQ, CT * P])
        hT = sb("hT", [P, NFC, CT * P])
        xnT = sb("xnT", [P, CT * P])
        fresh = sb("fresh", [P, CT * C])
        qT_bank = bank("qT_bank", [P, CT * P])
        h_bank = [bank(f"h_bank{f}", [P, CT * P]) for f in range(NFC)]
        ffn_bank = bank("ffn_bank", [P, CT * C])
        xnT_bank = bank("xnT_bank", [P, CT * P])
        moments = {n: sem("moments_" + n) for n in NORMS}
        rstd_ready = {n: sem("rstd_" + n) for n in NORMS}
        steps = {n: sem("steps_" + n) for n in ("in", "y", "mid", "x1", "q", "z2", "x", "act_y", "act_q")}
        angle_y = sem("angle_y")
        cos_y = sem("cos_y")
        x1_ready = sem("x1_ready")
        angle_q = sem("angle_q")
        cos_q = sem("cos_q")
        x1b_ready = sem("x1b_ready")
        xb_ready = sem("xb_ready")
        q_ready = sem("q_ready")
        qT_psum = sem("qT_psum")
        qT_sbuf = sem("qT_sbuf")
        h_psum = sem("h_psum")
        h_sbuf = sem("h_sbuf")
        ffn_psum = sem("ffn_psum")
        z2_ready = sem("z2_ready")
        xn_ready = sem("xn_ready")
        xn_kept = sem("xn_kept")
        xnT_psum = sem("xnT_psum")
        xnT_sbuf = sem("xnT_sbuf")
        logits_psum = sem("logits_psum")
        block = stack.enter_context(nc.Block())

        def part(a, c, k=None, cols=None):
            if k is None:
                return a[:, c * N:(c + 1) * N]
            return a[:, c * N + k * C:c * N + (k + 1) * C]

        def in_steps(stages):
            for s in range(NCH + max(lag for _, lag in stages)):
                for f, lag in stages:
                    if 0 <= s - lag < NCH:
                        f(s - lag)

        @block.vector
        def _(dve):
            def stats_of(n, src, c, step):
                for k in range(CT):
                    last = nc.vector.bn_stats(stats[n][:, k, :], part(src, c, k))
                step(last)
                for k in range(CT):
                    last = nc.vector.bn_aggr(mv[n][:, k, :], stats[n][:, k, :])
                step(last)
                nc.vector.tensor_scalar(vare[n][:, :], mv[n][:, :, 1], EPS, None, ALU.add).then_inc(moments[n], 1)

            def norm_in(c):
                step = Steps(dve, steps["in"], c, 2)
                stats_of("in", x, c, step)
                step.end()

            def angles_of_y(c):
                step = Steps(dve, steps["y"], c, 3)
                dve.wait_ge(rstd_ready["in"], c + 1)
                for k in range(CT):
                    last = nc.vector.tensor_scalar(part(y, c, k), part(x, c, k), mv["in"][:, k, 0:1],
                                                   rstd["in"][:, k:k + 1], ALU.subtract, ALU.mult)
                step(last)
                step(nc.vector.tensor_scalar(part(t1, c), part(y, c), INV_2PI, ROUND, ALU.mult, ALU.add))
                step(nc.vector.tensor_scalar(part(t2, c), part(t1, c), ROUND, -TWO_PI, ALU.subtract, ALU.mult))
                nc.vector.tensor_tensor(part(t1, c), part(t2, c), part(y, c), ALU.add).then_inc(angle_y, 1)
                step.end()

            def products_of_y(c):
                step = Steps(dve, steps["mid"], c, HD - 1 + 3)
                dve.wait_ge(cos_y, c + 1)
                heads = part(t1, c).rearrange("p (g d) -> p g d", d=HD)
                for d in range(1, HD):
                    step(nc.vector.tensor_tensor(heads[:, :, d], heads[:, :, d], heads[:, :, d - 1], ALU.mult))
                step(nc.vector.tensor_tensor(part(t2, c), part(y, c), part(t1, c), ALU.add))
                stats_of("mid", t2, c, step)
                step.end()

            def x1_of(c):
                step = Steps(dve, steps["x1"], c, 4)
                dve.wait_ge(rstd_ready["mid"], c + 1)
                for k in range(CT):
                    last = nc.vector.scalar_tensor_tensor(out=part(t1, c, k), in0=part(t2, c, k), scalar=mv["mid"][:, k, 0:1],
                                                          in1=const["gamma1"][:, :], op0=ALU.subtract, op1=ALU.mult)
                step(last)
                for k in range(CT):
                    last = nc.vector.scalar_tensor_tensor(out=part(y, c, k), in0=part(t1, c, k), scalar=rstd["mid"][:, k:k + 1],
                                                          in1=const["beta1"][:, :], op0=ALU.mult, op1=ALU.add)
                last.then_inc(x1_ready, 1)
                dve.wait_ge(x1_ready, c + 1)
                q_cols = part(y, c).rearrange("p (t n) -> p t n", t=CT)[:, :, 0:NQ]
                ang3 = ang[:, :].rearrange("p (t n) -> p t n", t=CT)
                turns3 = turns[:, :].rearrange("p (t n) -> p t n", t=CT)
                step(nc.vector.tensor_scalar(ang3, q_cols, INV_2PI, ROUND, ALU.mult, ALU.add))
                step(nc.vector.tensor_scalar(turns[:, :], ang[:, :], ROUND, None, ALU.subtract))
                step(nc.vector.scalar_tensor_tensor(out=ang3, in0=turns3, scalar=-TWO_PI_HI, in1=q_cols,
                                                    op0=ALU.mult, op1=ALU.add))
                nc.vector.scalar_tensor_tensor(out=turns[:, :], in0=turns[:, :], scalar=-TWO_PI_LO, in1=ang[:, :],
                                               op0=ALU.mult, op1=ALU.add).then_inc(angle_q, 1)
                step.end()

            def products_of_q(c):
                step = Steps(dve, steps["q"], c, 3 + NQ // 4 - 2)
                dve.wait_ge(cos_q, c + 1)
                q4 = ang[:, :].rearrange("p (g d) -> p g d", d=4)
                for d in range(1, 4):
                    step(nc.vector.tensor_tensor(q4[:, :, d], q4[:, :, d], q4[:, :, d - 1], ALU.mult))
                qt = ang[:, :].rearrange("p (t n) -> p t n", n=NQ)
                for g in range(1, NQ // 4):
                    last = nc.vector.tensor_tensor(qt[:, :, 4 * g:4 * g + 4], qt[:, :, 4 * g:4 * g + 4],
                                                   qt[:, :, 4 * g - 1:4 * g].broadcast_to((P, CT, 4)), ALU.mult)
                    if g < NQ // 4 - 1:
                        step(last)
                last.then_inc(q_ready, 1)
                step.end()

            def norm_out(c):
                step = Steps(dve, steps["z2"], c, 3)
                dve.wait_ge(ffn_psum, c + 1)
                dve.wait_ge(x1b_ready, c + 1)
                step(nc.vector.tensor_tensor(part(t2, c), ffn_bank[:, :], part(t1, c), ALU.add))
                stats_of("out", t2, c, step)
                step.end()

            def x_of(c):
                step = Steps(dve, steps["x"], c, 4)
                dve.wait_ge(rstd_ready["out"], c + 1)
                for k in range(CT):
                    last = nc.vector.scalar_tensor_tensor(out=part(y, c, k), in0=part(t2, c, k), scalar=mv["out"][:, k, 0:1],
                                                          in1=const["gamma2"][:, :], op0=ALU.subtract, op1=ALU.mult)
                step(last)
                dve.wait_ge(xb_ready, c + 1)
                for k in range(CT):
                    last = nc.vector.scalar_tensor_tensor(out=part(x, c, k), in0=part(y, c, k), scalar=rstd["out"][:, k:k + 1],
                                                          in1=part(xb, c, k), op0=ALU.mult, op1=ALU.add)
                step(last)
                stats_of("moe", x, c, step)
                step.end()

            def xn_of(c):
                dve.wait_ge(rstd_ready["moe"], c + 1)
                if c >= 1:
                    dve.wait_ge(xnT_psum, c)
                    dve.wait_ge(xn_kept, c)
                for k in range(CT):
                    last = nc.vector.tensor_scalar(fresh[:, k * C:(k + 1) * C], part(x, c, k), mv["moe"][:, k, 0:1],
                                                   rstd["moe"][:, k:k + 1], ALU.subtract, ALU.mult)
                last.then_inc(xn_ready, 1)

            in_steps(((norm_in, 0), (xn_of, 3), (products_of_y, 1), (angles_of_y, 0), (norm_out, 2),
                                 (x1_of, 1), (x_of, 2), (products_of_q, 1)))

        @block.gpsimd
        def _(pool):
            def power(n):
                def stage(c):
                    pool.wait_ge(moments[n], c + 1)
                    nc.gpsimd.tensor_tensor(rstd[n][:, :], vare[n][:, :], const["minus_half"][:, 0:CT],
                                            ALU.pow).then_inc(rstd_ready[n], 1)
                return stage

            def tiles(a, c):
                return part(a, c).rearrange("p (t n) -> p t n", t=CT)

            def x_and_beta2(c):
                nc.gpsimd.tensor_tensor(tiles(xb, c), tiles(x, c),
                                        const["beta2"][:, :].unsqueeze(1).broadcast_to((P, CT, C)),
                                        ALU.add).then_inc(xb_ready, 1)

            def x1_and_b2(c):
                pool.wait_ge(x1_ready, c + 1)
                nc.gpsimd.tensor_tensor(tiles(t1, c), tiles(y, c),
                                        const["b2"][:, :].unsqueeze(1).broadcast_to((P, CT, C)),
                                        ALU.add).then_inc(x1b_ready, 1)

            def keep_xn(c):
                pool.wait_ge(xn_ready, c + 1)
                nc.gpsimd.tensor_copy(part(t2, c), fresh[:, :]).then_inc(xn_kept, 1)

            in_steps(((power("in"), 0), (keep_xn, 3), (x_and_beta2, 0), (power("mid"), 1), (power("out"), 2),
                                 (x1_and_b2, 1), (power("moe"), 2)))

        @block.scalar
        def _(act):
            def cosines_of_y(c):
                step = Steps(act, steps["act_y"], c, 1)
                act.wait_ge(angle_y, c + 1)
                step(nc.scalar.activation(part(t2, c), part(t1, c), ACT.Abs))
                nc.scalar.activation(part(t1, c), part(t2, c), ACT.Sin, bias=const["half_pi"][:, 0:1],
                                     scale=-1.0).then_inc(cos_y, 1)

            def cosines_of_q(c):
                step = Steps(act, steps["act_q"], c, 1)
                act.wait_ge(angle_q, c + 1)
                step(nc.scalar.activation(turns[:, :], turns[:, :], ACT.Abs))
                nc.scalar.activation(ang[:, :], turns[:, :], ACT.Sin, bias=const["half_pi"][:, 0:1],
                                     scale=-1.0).then_inc(cos_q, 1)

            def hidden(c):
                act.wait_ge(qT_psum, c + 1)
                nc.scalar.copy(qT[:, :], qT_bank[0:NQ, :]).then_inc(qT_sbuf, 1)
                for f in range(NFC):
                    act.wait_ge(h_psum, c * NFC + f + 1)
                    nc.scalar.activation(hT[:, f, :], h_bank[f][:, :], ACT.Relu,
                                         bias=const["b1"][:, f:f + 1]).then_inc(h_sbuf, 1)

            def xn_turned(c):
                act.wait_ge(xnT_psum, c + 1)
                nc.scalar.copy(xnT[:, :], xnT_bank[:, :]).then_inc(xnT_sbuf, 1)

            in_steps(((xn_turned, 3), (cosines_of_y, 0), (cosines_of_q, 1), (hidden, 1)))

        @block.tensor
        def _(pe):
            def ffn(c):
                pe.wait_ge(q_ready, c + 1)
                for k in range(CT):
                    last = nc.tensor.transpose(qT_bank[0:NQ, k * P:(k + 1) * P], ang[:, k * NQ:(k + 1) * NQ],
                                               const["ident"][:, :])
                last.then_inc(qT_psum, 1)
                pe.wait_ge(qT_sbuf, c + 1)
                for f in range(NFC):
                    nc.tensor.matmul(h_bank[f][:, :], const["w1T"][:, f * P:(f + 1) * P], qT[:, :],
                                     start=True, stop=True).then_inc(h_psum, 1)
                pe.wait_ge(h_sbuf, (c + 1) * NFC)
                for k in range(CT):
                    for f in range(NFC):
                        last = nc.tensor.matmul(ffn_bank[:, k * C:(k + 1) * C], hT[:, f, k * P:(k + 1) * P],
                                                const["w2T"][:, f, :], start=(f == 0), stop=(f == NFC - 1))
                last.then_inc(ffn_psum, 1)

            def logits(c):
                pe.wait_ge(xn_ready, c + 1)
                for k in range(CT):
                    last = nc.tensor.transpose(xnT_bank[:, k * P:(k + 1) * P], fresh[:, k * C:(k + 1) * C], const["ident"][:, :])
                last.then_inc(xnT_psum, 1)
                pe.wait_ge(xnT_sbuf, c + 1)
                for k in range(CT):
                    last = nc.tensor.matmul(const["logits_bank"][:, (c * CT + k) * NE:(c * CT + k + 1) * NE],
                                            xnT[:, k * P:(k + 1) * P], w["wg"][:, :], start=True, stop=True)
                last.then_inc(logits_psum, 1)

            in_steps(((logits, 3), (ffn, 1)))


def route(nc, tag, xn, const, slots_dram):
    with ExitStack() as stack:
        logits = stack.enter_context(nc.sbuf_tensor(tag + "logits", [P, NT, NE], FP32))
        best = stack.enter_context(nc.sbuf_tensor(tag + "best", [P, NT], FP32))
        isbest = stack.enter_context(nc.sbuf_tensor(tag + "isbest", [P, NT, NE], FP32))
        rankval = stack.enter_context(nc.sbuf_tensor(tag + "rankval", [P, NT, NE], FP32))
        onehot = stack.enter_context(nc.sbuf_tensor(tag + "onehot", [P, NE, NT], BF16))
        tot = stack.enter_context(nc.sbuf_tensor(tag + "tot", [P, NE, NT], FP32))
        cum = stack.enter_context(nc.sbuf_tensor(tag + "cum", [P, NE, NT], FP32))
        cnt = stack.enter_context(nc.sbuf_tensor(tag + "cnt", [P, NE], FP32))
        tiles_a = stack.enter_context(nc.sbuf_tensor(tag + "tiles_a", [P, NE], FP32))
        tiles_e = stack.enter_context(nc.sbuf_tensor(tag + "tiles_e", [P, NE], FP32))
        end_e = stack.enter_context(nc.sbuf_tensor(tag + "end_e", [P, NE], FP32))
        adj = stack.enter_context(nc.sbuf_tensor(tag + "adj", [P, NE], FP32))
        adj2 = stack.enter_context(nc.sbuf_tensor(tag + "adj2", [P, NE], FP32))
        pos = stack.enter_context(nc.sbuf_tensor(tag + "pos", [P, NE, NT], FP32))
        slotf = stack.enter_context(nc.sbuf_tensor(tag + "slotf", [P, NT], FP32))
        past = stack.enter_context(nc.sbuf_tensor(tag + "past", [P, SLOT_TILES, NE], FP32))
        tilef = stack.enter_context(nc.sbuf_tensor(tag + "tilef", [P, SLOT_TILES], FP32))
        pR = stack.enter_context(nc.psum_tensor(tag + "pR", [P, 2, NE * NT], FP32))
        onehot_ready = stack.enter_context(nc.semaphore(tag + "onehot_ready"))
        counts_psum = stack.enter_context(nc.semaphore(tag + "counts_psum"))
        slots_ready = stack.enter_context(nc.semaphore(tag + "slots_ready"))
        scattered = stack.enter_context(nc.semaphore(tag + "scattered"))
        dve_step = stack.enter_context(nc.semaphore(tag + "dve_step"))
        block = stack.enter_context(nc.Block())

        @block.vector
        def _(dve):
            done = [0]

            def step(ins):
                done[0] += 1
                ins.then_inc(dve_step, 1)
                dve.wait_ge(dve_step, done[0])

            step(nc.vector.tensor_tensor(logits[:, :, :], const["logits_bank"][:, :].rearrange("p (t e) -> p t e", e=NE),
                                         const["bg"][:, :].unsqueeze(1).broadcast_to((P, NT, NE)), ALU.add))
            step(nc.vector.tensor_reduce(best[:, :], logits[:, :, :], AX.X, ALU.max))
            step(nc.vector.tensor_tensor(isbest[:, :, :], logits[:, :, :],
                                         best[:, :].unsqueeze(2).broadcast_to((P, NT, NE)), ALU.is_equal))
            order = const["order"][:, :].unsqueeze(1).broadcast_to((P, NT, NE))
            step(nc.vector.tensor_tensor(rankval[:, :, :], isbest[:, :, :], order, ALU.mult))
            step(nc.vector.tensor_reduce(best[:, :], rankval[:, :, :], AX.X, ALU.max))
            nc.vector.tensor_tensor(onehot[:, :, :].rearrange("p e t -> p t e"), order,
                                    best[:, :].unsqueeze(2).broadcast_to((P, NT, NE)),
                                    ALU.is_equal).then_inc(onehot_ready, 1)
            dve.wait_ge(counts_psum, 1)
            step(nc.vector.tensor_copy(tot[:, :, :], pR[:, 1, :].rearrange("p (e t) -> p e t", e=NE)))
            flat = "p e t -> p (e t)"
            nc.vector.tensor_tensor_scan(cum[:, :, :].rearrange(flat), tot[:, :, :].rearrange(flat),
                                         const["zero"][:, 0:NE * NT], 0.0, ALU.add, ALU.add)
            step(nc.vector.tensor_reduce(cnt[:, :], tot[:, :, :], AX.X, ALU.add))
            step(nc.vector.tensor_scalar(tiles_a[:, :], cnt[:, :], 1.0 / P, (P - 1) / (2.0 * P), ALU.mult, ALU.add))
            step(nc.vector.tensor_scalar(tiles_e[:, :], tiles_a[:, :], ROUND, ROUND, ALU.add, ALU.subtract))
            step(nc.vector.tensor_tensor_scan(end_e[:, :], tiles_e[:, :], const["zero"][:, 0:NE], 0.0,
                                              ALU.add, ALU.add))
            step(nc.vector.tensor_tensor(adj[:, :], end_e[:, :], tiles_e[:, :], ALU.subtract))
            step(nc.vector.scalar_tensor_tensor(out=adj2[:, :], in0=adj[:, :], scalar=float(P), in1=tot[:, :, 0],
                                                op0=ALU.mult, op1=ALU.add))
            step(nc.vector.tensor_tensor(adj[:, :], adj2[:, :], cum[:, :, 0], ALU.subtract))
            step(nc.vector.tensor_tensor(pos[:, :, :], cum[:, :, :], tot[:, :, :], ALU.subtract))
            step(nc.vector.tensor_tensor(cum[:, :, :], pos[:, :, :], pR[:, 0, :].rearrange("p (e t) -> p e t", e=NE),
                                         ALU.add))
            step(nc.vector.tensor_tensor(pos[:, :, :], cum[:, :, :],
                                         adj[:, :].unsqueeze(2).broadcast_to((P, NE, NT)), ALU.add))
            step(nc.vector.tensor_tensor(cum[:, :, :], pos[:, :, :], onehot[:, :, :], ALU.mult))
            step(nc.vector.tensor_reduce(slotf[:, :], cum[:, :, :].rearrange("p e t -> p t e"), AX.X, ALU.add))
            nc.vector.tensor_copy(const["slot"][:, :], slotf[:, :]).then_inc(slots_ready, 1)
            step(nc.vector.tensor_tensor(past[:, :, :], end_e[:, :].unsqueeze(1).broadcast_to((P, SLOT_TILES, NE)),
                                         const["tileno"][:, :].unsqueeze(2).broadcast_to((P, SLOT_TILES, NE)),
                                         ALU.is_le))
            step(nc.vector.tensor_reduce(tilef[:, :], past[:, :, :], AX.X, ALU.add))
            step(nc.vector.tensor_scalar(const["tile_expert"][:, :], tilef[:, :], float(NE - 1), None, ALU.min))

        @block.gpsimd
        def _(pool):
            pool.wait_ge(slots_ready, 1)
            for t in range(NT):
                nc.gpsimd.indirect_dma_start(
                    out=slots_dram[:, :], out_offset=bass.IndirectOffsetOnAxis(ap=const["slot"][:, t:t + 1], axis=0),
                    in_=xn[:, t, :], in_offset=None).then_inc(scattered, 16)
            pool.wait_ge(scattered, 16 * NT)

        @block.tensor
        def _(pe):
            pe.wait_ge(onehot_ready, 1)
            oh = onehot[:, :, :].rearrange("p e t -> p (e t)")
            nc.tensor.matmul(pR[:, 0, :], const["before"][:, :], oh, start=True, stop=True)
            nc.tensor.matmul(pR[:, 1, :], const["ones"][:, :], oh, start=True, stop=True).then_inc(counts_psum, 1)


def expert_tiles(nc, tag, w, const, slots_dram, y_dram):
    U = 4
    assert SLOT_TILES % U == 0
    with ExitStack() as stack:
        xt = stack.enter_context(nc.sbuf_tensor(tag + "xt", [P, U, C], FP32))
        yt = stack.enter_context(nc.sbuf_tensor(tag + "yt", [P, U, C], FP32))
        xT = stack.enter_context(nc.sbuf_tensor(tag + "xT", [P, 2, P], FP32))
        hid = stack.enter_context(nc.sbuf_tensor(tag + "hid", [P, 2, HID], FP32))
        hidT = stack.enter_context(nc.sbuf_tensor(tag + "hidT", [P, 2, HID], FP32))
        xT_bank = [stack.enter_context(nc.psum_tensor(tag + f"xT_bank{b}", [P, 512], FP32)) for b in range(2)]
        hid_bank = [stack.enter_context(nc.psum_tensor(tag + f"hid_bank{b}", [P, HID], FP32)) for b in range(2)]
        hidT_bank = [stack.enter_context(nc.psum_tensor(tag + f"hidT_bank{b}", [P, HID], FP32)) for b in range(2)]
        y_bank = [stack.enter_context(nc.psum_tensor(tag + f"y_bank{b}", [P, 512], FP32)) for b in range(2)]
        loaded = [stack.enter_context(nc.semaphore(tag + f"loaded{u}")) for u in range(U)]
        stored = [stack.enter_context(nc.semaphore(tag + f"stored{u}")) for u in range(U)]
        xT_psum = stack.enter_context(nc.semaphore(tag + "xT_psum"))
        xT_sbuf = stack.enter_context(nc.semaphore(tag + "xT_sbuf"))
        hid_psum = stack.enter_context(nc.semaphore(tag + "hid_psum"))
        hid_sbuf = stack.enter_context(nc.semaphore(tag + "hid_sbuf"))
        hidT_psum = stack.enter_context(nc.semaphore(tag + "hidT_psum"))
        hidT_sbuf = stack.enter_context(nc.semaphore(tag + "hidT_sbuf"))
        y_psum = stack.enter_context(nc.semaphore(tag + "y_psum"))
        y_sbuf = stack.enter_context(nc.semaphore(tag + "y_sbuf"))
        block = stack.enter_context(nc.Block())

        def in_steps(eng, stages):
            FIRST = U + 3
            LOOPED = (SLOT_TILES - FIRST) // U * U

            def one(s):
                for f, lag in stages:
                    if 0 <= s - lag < SLOT_TILES:
                        f(s - lag, (s - lag) % U, (s - lag) // U)

            for s in range(FIRST):
                one(s)
            with eng.Fori(0, LOOPED // U) as i:
                for k in range(U):
                    for f, lag in stages:
                        j = FIRST + k - lag
                        f(i * U + j, j % U, i + j // U)
            for s in range(FIRST + LOOPED, SLOT_TILES + 3):
                one(s)

        def later(j, n):
            return not isinstance(j, int) or j >= n

        @block.sync
        def _(sp):
            for u in range(U):
                sp.dma_start(xt[:, u, :], slots_dram[u * P:(u + 1) * P, :]).then_inc(loaded[u], 16)
            with nc.sync.Fori(0, SLOT_TILES // U - 1) as i:
                for u in range(U):
                    sp.wait_ge(xT_psum, i * U + (u + 1))
                    sp.dma_start(xt[:, u, :], slots_dram[bass.ds(i * (U * P) + (U + u) * P, P), :]).then_inc(loaded[u], 16)

        @block.scalar
        def _(act):
            def gelu(j, u, turn):
                act.wait_ge(hid_psum, j + 1)
                if later(j, 2):
                    act.wait_ge(hidT_psum, j - 1)
                nc.scalar.activation(hid[:, u % 2, :], hid_bank[u % 2][:, :], ACT.Gelu_apprx_tanh).then_inc(hid_sbuf, 1)

            def copy_y(j, u, turn):
                act.wait_ge(y_psum, j + 1)
                if later(j, U):
                    act.wait_ge(stored[u], turn * 16)
                nc.scalar.copy(yt[:, u, :], y_bank[u % 2][:, 0:C]).then_inc(y_sbuf, 1)

            in_steps(nc.scalar, ((gelu, 1), (copy_y, 3)))

        @block.gpsimd
        def _(pool):
            with nc.gpsimd.Fori(0, SLOT_TILES // U) as i:
                for u in range(U):
                    pool.wait_ge(y_sbuf, i * U + (u + 1))
                    pool.dma_start(y_dram[bass.ds(i * (U * P) + u * P, P), :], yt[:, u, :]).then_inc(stored[u], 16)
            for u in range(U):
                pool.wait_ge(stored[u], 16 * SLOT_TILES // U)

        @block.vector
        def _(dve):
            def copy_x(j, u, turn):
                dve.wait_ge(xT_psum, j + 1)
                if later(j, 2):
                    dve.wait_ge(hid_psum, j - 1)
                nc.vector.tensor_copy(xT[:, u % 2, :], xT_bank[u % 2][:, 0:P]).then_inc(xT_sbuf, 1)

            def copy_hidden(j, u, turn):
                dve.wait_ge(hidT_psum, j + 1)
                if later(j, 2):
                    dve.wait_ge(y_psum, j - 1)
                nc.vector.tensor_copy(hidT[:, u % 2, :], hidT_bank[u % 2][:, :]).then_inc(hidT_sbuf, 1)

            in_steps(nc.vector, ((copy_x, 0), (copy_hidden, 2)))

        @block.tensor
        def _(pe):
            def turn_x(j, u, turn):
                pe.wait_ge(loaded[u], turn * 16 + 16)
                if later(j, 2):
                    pe.wait_ge(xT_sbuf, j - 1)
                nc.tensor.transpose(xT_bank[u % 2][:, 0:P], xt[:, u, :], const["ident"][:, :]).then_inc(xT_psum, 1)

            def up(j, u, turn):
                e = nc.tensor.value_load(const["tile_expert"][0:1, bass.ds(j, 1)], min_val=0, max_val=NE - 1)
                pe.wait_ge(xT_sbuf, j + 1)
                if later(j, 2):
                    pe.wait_ge(hid_sbuf, j - 1)
                nc.tensor.matmul(hid_bank[u % 2][:, :], xT[:, u % 2, :], w["w1"][:, bass.ds(e * HID, HID)],
                                 start=True, stop=True).then_inc(hid_psum, 1)

            def turn_hidden(j, u, turn):
                pe.wait_ge(hid_sbuf, j + 1)
                if later(j, 2):
                    pe.wait_ge(hidT_sbuf, j - 1)
                for k in range(NHC):
                    last = nc.tensor.transpose(hidT_bank[u % 2][:, k * P:(k + 1) * P],
                                               hid[:, u % 2, k * P:(k + 1) * P], const["ident"][:, :])
                last.then_inc(hidT_psum, 1)

            def down(j, u, turn):
                e = nc.tensor.value_load(const["tile_expert"][0:1, bass.ds(j, 1)], min_val=0, max_val=NE - 1)
                pe.wait_ge(hidT_sbuf, j + 1)
                if later(j, 2):
                    pe.wait_ge(y_sbuf, j - 1)
                for k in range(NHC):
                    last = nc.tensor.matmul(y_bank[u % 2][:, 0:C], hidT[:, u % 2, k * P:(k + 1) * P],
                                            w["w2"][:, bass.ds(e * (NHC * C) + k * C, C)],
                                            start=(k == 0), stop=(k == NHC - 1))
                last.then_inc(y_psum, 1)

            in_steps(nc.tensor, ((turn_x, 0), (up, 1), (turn_hidden, 2), (down, 3)))


def combine(nc, tag, x, y, const, y_dram):
    with ExitStack() as stack:
        gathered = stack.enter_context(nc.semaphore(tag + "gathered"))
        added = stack.enter_context(nc.semaphore(tag + "added"))
        block = stack.enter_context(nc.Block())
        @block.gpsimd
        def _(pool):
            for t in range(NT):
                nc.gpsimd.indirect_dma_start(
                    out=y[:, t, :], out_offset=None, in_=y_dram[:, :],
                    in_offset=bass.IndirectOffsetOnAxis(ap=const["slot"][:, t:t + 1], axis=0)).then_inc(gathered, 16)

        @block.vector
        def _(dve):
            dve.wait_ge(gathered, 16 * NT)
            for t in range(0, NT, 4):
                nc.vector.tensor_tensor(x[:, t:t + 4, :], x[:, t:t + 4, :], y[:, t:t + 4, :],
                                        ALU.add).then_inc(added, 1)
            dve.wait_ge(added, NT // 4)


PARTS = 3
STACK = PARTS * PARTS * HD
BIG = 1e30


def position_table(nc, ins, table):
    with ExitStack() as stack:
        def sb(name, shape, dt=FP32):
            return stack.enter_context(nc.sbuf_tensor("pt_" + name, shape, dt))

        def sem(name):
            return stack.enter_context(nc.semaphore("pt_" + name))

        dist = sb("dist", [P, SEQ])
        wb = sb("w", [P, NH])
        minus_w = sb("minus_w", [P, NH])
        vb = sb("v", [P, NH])
        ev = sb("ev", [P, NH])
        top = sb("top", [P, NH])
        grown = sb("grown", [P, NH, SEQ])
        loaded = sem("loaded")
        dist_made = sem("dist_made")
        grown_made = sem("grown_made")
        weights = sem("weights")
        dve_step = sem("dve_step")
        masked = sem("masked")
        block = stack.enter_context(nc.Block())

        @block.sync
        def _(sp):
            for dst, name in ((wb, "L0_attn_b_w"), (vb, "L0_attn_b_v")):
                sp.dma_start(dst[:, :], ins[name].unsqueeze(0).broadcast_to((P, NH))).then_inc(loaded, 16)

        @block.gpsimd
        def _(pool):
            nc.gpsimd.iota(dist[:, :], pattern=[[-1, SEQ]], base=P, channel_multiplier=1,
                           allow_small_or_imprecise_dtypes=True).then_inc(dist_made, 1)
            pool.wait_ge(weights, 1)
            nc.gpsimd.affine_select(out=table[:, :, :], in_=table[:, :, :], compare_op=ALU.is_ge, fill=-1.0,
                                    base=P, pattern=[[0, NH], [-1, SEQ]], channel_multiplier=1).then_inc(masked, 1)
            pool.wait_ge(masked, 1)

        @block.scalar
        def _(act):
            act.wait_ge(loaded, 32)
            nc.scalar.activation(ev[:, :], vb[:, :], ACT.Exp).then_inc(grown_made, 1)
            act.wait_ge(dve_step, 2)
            for h in range(NH):
                nc.scalar.activation(grown[:, h, :], dist[:, :], ACT.Exp, bias=vb[:, h:h + 1],
                                     scale=minus_w[:, h:h + 1]).then_inc(grown_made, 1)

        @block.vector
        def _(dve):
            step = Steps(dve, dve_step, 0, 5)
            dve.wait_ge(loaded, 32)
            step(nc.vector.tensor_scalar(minus_w[:, :], wb[:, :], -1.0, None, ALU.mult))
            dve.wait_ge(dist_made, 1)
            step(nc.vector.tensor_scalar(dist[:, :], dist[:, :], 0.0, None, ALU.max))
            dve.wait_ge(grown_made, 1 + NH)
            step(nc.vector.tensor_scalar(top[:, :], ev[:, :], 1.0, float(1.0 / np.sqrt(HD)), ALU.add, ALU.mult))
            step(nc.vector.tensor_scalar(grown[:, :, :], grown[:, :, :], 1.0, None, ALU.add))
            step(nc.vector.reciprocal(grown[:, :, :], grown[:, :, :]))
            nc.vector.tensor_tensor(table[:, :, :], grown[:, :, :],
                                    top[:, :].unsqueeze(2).broadcast_to((P, NH, SEQ)), ALU.mult).then_inc(weights, 1)
            step.end()


CT = 4
NCH = NT // CT


def staged(stages):
    for s in range(NCH + max(lag for _, lag in stages)):
        for f, lag in stages:
            if 0 <= s - lag < NCH:
                f(s - lag)


def part(a, c, k=None):
    first, n = (c * CT, CT) if k is None else (c * CT + k, 1)
    return a[:, first * C:(first + n) * C]


def layer_norm_stats(nc, stats, mv, vare, src, c, step, moments):
    for k in range(CT):
        last = nc.vector.bn_stats(stats[:, k, :], part(src, c, k))
    step(last)
    for k in range(CT):
        last = nc.vector.bn_aggr(mv[:, k, :], stats[:, k, :])
    step(last)
    nc.vector.tensor_scalar(vare[:, :], mv[:, :, 1], EPS, None, ALU.add).then_inc(moments, 1)


def project(nc, x, const, v_ones, q_dram, k_dram):
    with ExitStack() as stack:
        def sb(name, shape, dt=FP32):
            return stack.enter_context(nc.sbuf_tensor("p_" + name, shape, dt))

        def bank(name):
            return stack.enter_context(nc.psum_tensor("p_" + name, [P, CT * P], FP32))

        def sem(name):
            return stack.enter_context(nc.semaphore("p_" + name))

        stats, mv = sb("stats", [P, CT, 6]), sb("mv", [P, CT, 2])
        vare, rstd = sb("vare", [P, CT]), sb("rstd", [P, CT])
        fresh = sb("fresh", [P, CT * C])
        xnT = sb("xnT", [P, CT * P])
        whole = {s: sb("whole_" + s, [P, CT * P]) for s in "qk"}
        rest = {s: sb("rest_" + s, [P, CT * P]) for s in "qk"}
        split = {s: sb("split_" + s, [P, PARTS, CT * P], BF16) for s in "qk"}
        xnT_bank, v_bank = bank("xnT_bank"), bank("v_bank")
        qk_bank = {s: bank("bank_" + s) for s in "qk"}
        moments, rstd_ready, dve_step, pool_step = sem("moments"), sem("rstd"), sem("dve_step"), sem("pool_step")
        xn_ready, xnT_psum, xnT_sbuf = sem("xn_ready"), sem("xnT_psum"), sem("xnT_sbuf")
        qk_psum = {s: sem("psum_" + s) for s in "qk"}
        whole_ready = {s: sem("whole_ready_" + s) for s in "qk"}
        split_ready = {s: sem("split_ready_" + s) for s in "qk"}
        kept = {s: sem("kept_" + s) for s in "qk"}
        v_psum, v_sbuf, ones_set, x_plus = sem("v_psum"), sem("v_sbuf"), sem("ones_set"), sem("x_plus")
        block = stack.enter_context(nc.Block())

        @block.vector
        def _(dve):
            def norm(c):
                step = Steps(dve, dve_step, c, 2)
                layer_norm_stats(nc, stats, mv, vare, x, c, step, moments)
                step.end()

            def xn_of(c):
                dve.wait_ge(rstd_ready, c + 1)
                if c >= 1:
                    dve.wait_ge(xnT_psum, c)
                for k in range(CT):
                    last = nc.vector.tensor_scalar(fresh[:, k * C:(k + 1) * C], part(x, c, k), mv[:, k, 0:1],
                                                   rstd[:, k:k + 1], ALU.subtract, ALU.mult)
                last.then_inc(xn_ready, 1)

            def keep_values(c):
                dve.wait_ge(v_psum, c + 1)
                dve.wait_ge(ones_set, 1)
                nc.vector.tensor_copy(v_ones[:, c * CT * NH:(c + 1) * CT * NH, 0:HD],
                                      v_bank[:, :].rearrange("p (g d) -> p g d", d=HD)).then_inc(v_sbuf, 1)

            staged(((norm, 0), (keep_values, 1), (xn_of, 0)))

        @block.gpsimd
        def _(pool):
            nc.gpsimd.memset(v_ones[:, :, HD:HD + 1], 1.0).then_inc(ones_set, 1)

            def power(c):
                pool.wait_ge(moments, c + 1)
                nc.gpsimd.tensor_tensor(rstd[:, :], vare[:, :], const["minus_half"][:, 0:CT],
                                        ALU.pow).then_inc(rstd_ready, 1)

            def add_bo(c):
                pool.wait_ge(xn_ready, c + 1)
                xc = part(x, c).rearrange("p (t n) -> p t n", t=CT)
                nc.gpsimd.tensor_tensor(xc, xc, const["bo"][:, :].unsqueeze(1).broadcast_to((P, CT, C)),
                                        ALU.add).then_inc(x_plus, 1)

            def split_of(c):
                step = Steps(pool, pool_step, c, 4)
                for s in "qk":
                    pool.wait_ge(whole_ready[s], c + 1)
                    step(nc.gpsimd.tensor_tensor(rest[s][:, :], whole[s][:, :], split[s][:, 0, :], ALU.subtract))
                    step(nc.gpsimd.tensor_copy(split[s][:, 1, :], rest[s][:, :]))
                    nc.gpsimd.tensor_tensor(split[s][:, 2, :], rest[s][:, :], split[s][:, 1, :],
                                            ALU.subtract).then_inc(split_ready[s], 1)
                step.end()

            staged(((power, 0), (add_bo, 0), (split_of, 1)))
            pool.wait_ge(x_plus, NCH)

        @block.scalar
        def _(act):
            def xn_turned(c):
                act.wait_ge(xnT_psum, c + 1)
                nc.scalar.copy(xnT[:, :], xnT_bank[:, :]).then_inc(xnT_sbuf, 1)

            def first_part(c):
                for s in "qk":
                    act.wait_ge(qk_psum[s], c + 1)
                    if c >= 1:
                        act.wait_ge(split_ready[s], c)
                        act.wait_ge(kept[s], 16 * (CT * P // SEQ) * c)
                    nc.scalar.copy(whole[s][:, :], qk_bank[s][:, :])
                    nc.scalar.copy(split[s][:, 0, :], qk_bank[s][:, :]).then_inc(whole_ready[s], 1)

            staged(((xn_turned, 0), (first_part, 0)))

        @block.sync
        def _(sp):
            for c in range(NCH):
                for s, dram in (("q", q_dram), ("k", k_dram)):
                    sp.wait_ge(split_ready[s], c + 1)
                    for b in range(CT * P // SEQ):
                        sp.dma_start(dram[c * (CT * P // SEQ) + b].rearrange("r p n -> p r n"),
                                     split[s][:, :, b * SEQ:(b + 1) * SEQ]).then_inc(kept[s], 16)
            sp.wait_ge(kept["q"], 16 * BATCH)
            sp.wait_ge(kept["k"], 16 * BATCH)

        @block.tensor
        def _(pe):
            def turn(c):
                pe.wait_ge(xn_ready, c + 1)
                for k in range(CT):
                    last = nc.tensor.transpose(xnT_bank[:, k * P:(k + 1) * P], fresh[:, k * C:(k + 1) * C],
                                               const["ident"][:, :])
                last.then_inc(xnT_psum, 1)

            def products(c):
                pe.wait_ge(xnT_sbuf, c + 1)
                for s in "qk":
                    if c >= 1:
                        pe.wait_ge(whole_ready[s], c)
                    nc.tensor.matmul(qk_bank[s][:, :], const["w" + s][:, :], xnT[:, :],
                                     start=True, stop=True).then_inc(qk_psum[s], 1)
                if c >= 1:
                    pe.wait_ge(v_sbuf, c)
                for k in range(CT):
                    last = nc.tensor.matmul(v_bank[:, k * C:(k + 1) * C], xnT[:, k * P:(k + 1) * P], const["wv"][:, :],
                                            start=True, stop=True)
                last.then_inc(v_psum, 1)

            staged(((turn, 0), (products, 0)))


def attend(nc, const, v_ones, table, q_dram, k_dram, ctx_out):
    GAP = 32
    PER = P // GAP
    UNIT = 8 * P
    per_batch = [(0, 8 * g, 8) for g in range(2)] + [(1, 4 * g, 4) for g in range(4)]
    UNITS = [(b, tile, head, heads) for b in range(2) for tile, head, heads in per_batch]
    NU = len(UNITS)
    TOTAL = NU * BATCH // 2
    with ExitStack() as stack:
        def sb(name, shape, dt=FP32):
            return stack.enter_context(nc.sbuf_tensor("t_" + name, shape, dt))

        def bank(name, n=1):
            return stack.enter_context(nc.psum_tensor("t_" + name, [P, 512 * n], FP32))

        def sem(name):
            return stack.enter_context(nc.semaphore("t_" + name))

        qs = [sb(f"qs{b}", [STACK, NH, SEQ], BF16) for b in range(2)]
        ks = [sb(f"ks{b}", [STACK, NH, SEQ], BF16) for b in range(2)]
        values = [sb(f"values{b}", [P, 2 * NH * (HD + 1)]) for b in range(2)]
        weighted = [sb(f"weighted{p}", [P, UNIT]) for p in range(3)]
        tops = [sb(f"top{p}", [P, 8]) for p in range(3)]
        ctxT = [sb(f"ctxT{p}", [P, NH // PER * P]) for p in range(2)]
        probs = [sb(f"probs{p}", [P, UNIT]) for p in range(2)]
        recs = [sb(f"rec{p}", [P, NH]) for p in range(2)]
        score_banks = [bank(f"score{p}", 2) for p in range(2)]
        turned_bank = [bank(f"turned{p}") for p in range(2)]
        ctxT_bank, ctx_bank = bank("ctxT_bank"), bank("ctx_bank")
        stacked = [sem(f"stacked{b}") for b in range(2)]
        values_here = [sem(f"values_here{b}") for b in range(2)]
        scored, weights_done, max_done, shifted, turned, exped, averaged = (sem(n) for n in (
            "scored", "weights_done", "max_done", "shifted", "turned", "exped", "averaged"))
        bank_blank, ctxT_sbuf, turned_back, rec_done, ctx_done = (sem(n) for n in (
            "bank_blank", "ctxT_sbuf", "turned_back", "rec_done", "ctx_done"))
        block = stack.enter_context(nc.Block())

        def in_steps(eng, stages):
            lags = max(lag for _, lag in stages)
            for s in range(NU):
                for f, lag in stages:
                    if s >= lag:
                        f(s - lag, s - lag, 0)
            with eng.Fori(1, BATCH // 2) as i:
                for s in range(NU):
                    for f, lag in stages:
                        f(i * NU + (s - lag), (s - lag) % NU, i if s >= lag else i - 1)
            for s in range(TOTAL, TOTAL + lags):
                for f, lag in stages:
                    if s - lag < TOTAL:
                        f(s - lag, (s - lag) % NU, BATCH // 2 - 1)

        def first(g, n):
            return isinstance(g, int) and g < n

        group = [2 * b + tile for b, tile, _, _ in UNITS]
        ends = [u + 1 == NU or group[u + 1] != group[u] for u in range(NU)]
        begins = [u == 0 or group[u - 1] != group[u] for u in range(NU)]

        @block.sync
        def _(sp):
            def load(pair, b):
                n = pair * 2 + b
                for c in range(PARTS * PARTS):
                    rows = slice(c * HD, (c + 1) * HD)
                    for dst, dram, r in ((qs[b], q_dram, c // PARTS), (ks[b], k_dram, c % PARTS)):
                        sp.dma_start(dst[rows, :, :], dram[bass.ds(n, 1), r].rearrange("a (h d) n -> d (a h) n", d=HD)
                                     ).then_inc(stacked[b], 16)

            def load_values(pair, b):
                wide = 2 * NH * (HD + 1)
                sp.dma_start(values[b][:, :], v_ones[:, bass.ds((pair * 2 + b) * wide, wide)]
                             ).then_inc(values_here[b], 16)

            for b in range(2):
                load(0, b)
                load_values(0, b)
            with nc.sync.Fori(1, BATCH // 2) as i:
                for b in range(2):
                    sp.wait_ge(scored, i * NU + (NU // 2) * (b - 1))
                    load(i, b)
                    sp.wait_ge(averaged, i * NU + (NU // 2) * (b - 1))
                    load_values(i, b)

        @block.tensor
        def _(pe):
            def scores(g, u, pair):
                b, tile, head, heads = UNITS[u]
                keys = (tile + 1) * P
                out = score_banks[u % 2]
                if u % (NU // 2) == 0:
                    pe.wait_ge(stacked[b], (pair + 1) * (16 * 2 * PARTS * PARTS))
                if not first(g, 2):
                    pe.wait_ge(weights_done, g - 1)
                for half in range(2):
                    per = heads // 2
                    own = out[:, half * 512:(half + 1) * 512].rearrange("p (h k) -> p h k", h=per)
                    nc.tensor.matmul(own[:, :, keys - P:keys], const["ident16"][:, :],
                                     const["after"][:, :].unsqueeze(1).broadcast_to((P, per, P)),
                                     start=True, stop=False, skip_group_check=True)
                    for k in range(per):
                        h = head + half * per + k
                        last = nc.tensor.matmul(own[:, k, :], qs[b][:, h, tile * P:(tile + 1) * P],
                                                ks[b][:, h, 0:keys], start=False, stop=True, skip_group_check=True)
                last.then_inc(scored, 1)

            def turn(g, u, pair):
                pe.wait_ge(shifted, g + 1)
                for half in range(2):
                    if not first(g, 1):
                        pe.wait_ge(exped, g * 2 + (half - 1))
                    for j in range(4):
                        last = nc.tensor.transpose(turned_bank[half][:, j * P:(j + 1) * P],
                                                   weighted[u % 3][:, (half * 4 + j) * P:(half * 4 + j + 1) * P],
                                                   const["ident"][:, :])
                    last.then_inc(turned, 1)

            def average(g, u, pair):
                b, tile, head, heads = UNITS[u]
                blocks = tile + 1
                if u % (NU // 2) == 0:
                    pe.wait_ge(values_here[b], (pair + 1) * 16)
                if first(g, 1):
                    pe.wait_ge(bank_blank, 1)
                elif begins[u]:
                    pe.wait_ge(ctxT_sbuf, pair * 4 + group[u])
                pe.wait_ge(exped, g * 2 + 2)
                for quad in range(heads // PER):
                    for j in range(blocks):
                        for k in range(PER):
                            h = head + quad * PER + k
                            n = (quad * PER + k) * blocks + j
                            last = nc.tensor.matmul(
                                ctxT_bank[k * GAP:k * GAP + HD + 1, h // PER * P:(h // PER + 1) * P],
                                values[b][:, (j * NH + h) * (HD + 1):(j * NH + h + 1) * (HD + 1)],
                                probs[u % 2][:, n * P:(n + 1) * P], start=(j == 0), stop=(j == blocks - 1),
                                skip_group_check=True)
                last.then_inc(averaged, 1)

            def turn_back(g, u, pair):
                if not ends[u]:
                    return
                done = pair * 4 + group[u]
                pe.wait_ge(ctxT_sbuf, done + 1)
                if not first(done, 1):
                    pe.wait_ge(ctx_done, done)
                for n in range(NH // PER):
                    last = nc.tensor.transpose(ctx_bank[:, n * P:(n + 1) * P], ctxT[group[u] % 2][:, n * P:(n + 1) * P],
                                               const["ident"][:, :])
                last.then_inc(turned_back, 1)

            in_steps(nc.tensor, ((scores, 0), (turn, 3), (average, 4), (turn_back, 5)))

        @block.vector
        def _(dve):
            def weigh(g, u, pair):
                b, tile, head, heads = UNITS[u]
                keys = (tile + 1) * P
                dve.wait_ge(scored, g + 1)
                if not first(g, 3):
                    dve.wait_ge(turned, g * 2 - 4)
                view = weighted[u % 3][:, :].rearrange("p (h k) -> p h k", k=keys)
                nc.vector.scalar_tensor_tensor(
                    out=view, in0=score_banks[u % 2][:, :].rearrange("p (h k) -> p h k", k=keys), scalar=0.0,
                    in1=table[:, head:head + heads, SEQ - keys:SEQ], op0=ALU.max, op1=ALU.mult).then_inc(weights_done, 1)
                dve.wait_ge(weights_done, g + 1)
                nc.vector.tensor_reduce(tops[u % 3][:, 0:heads], view, AX.X, ALU.max).then_inc(max_done, 1)

            def divide(g, u, pair):
                if not ends[u]:
                    return
                done = pair * 4 + group[u]
                ctx = ctx_bank[:, :].rearrange("p (h d) -> p h d", d=GAP)
                rec = recs[group[u] % 2]
                dve.wait_ge(turned_back, done + 1)
                nc.vector.reciprocal(rec[:, :], ctx[:, :, HD]).then_inc(rec_done, 1)
                dve.wait_ge(rec_done, done + 1)
                nc.vector.tensor_tensor(ctx_out[:, bass.ds(done * C, C)].rearrange("p (h d) -> p h d", h=NH),
                                        ctx[:, :, 0:HD], rec[:, :].unsqueeze(2).broadcast_to((P, NH, HD)),
                                        ALU.mult).then_inc(ctx_done, 1)

            nc.vector.memset(ctxT_bank[:, :], 0.0).then_inc(bank_blank, 1)
            in_steps(nc.vector, ((weigh, 0), (divide, 6)))

        @block.gpsimd
        def _(pool):
            def shift(g, u, pair):
                b, tile, head, heads = UNITS[u]
                view = weighted[u % 3][:, :].rearrange("p (h k) -> p h k", h=heads)
                pool.wait_ge(max_done, g + 1)
                nc.gpsimd.tensor_tensor(view, view, tops[u % 3][:, 0:heads].unsqueeze(2).broadcast_to(
                    (P, heads, (tile + 1) * P)), ALU.subtract).then_inc(shifted, 1)

            in_steps(nc.gpsimd, ((shift, 0),))

        @block.scalar
        def _(act):
            def exp(g, u, pair):
                if not first(g, 2):
                    act.wait_ge(averaged, g - 1)
                for half in range(2):
                    act.wait_ge(turned, g * 2 + (half + 1))
                    nc.scalar.activation(probs[u % 2][:, half * 512:(half + 1) * 512], turned_bank[half][:, :],
                                         ACT.Exp).then_inc(exped, 1)

            def keep_ctxT(g, u, pair):
                if not ends[u]:
                    return
                done = pair * 4 + group[u]
                act.wait_ge(averaged, g + 1)
                if not first(done, 2):
                    act.wait_ge(turned_back, done - 1)
                nc.scalar.copy(ctxT[group[u] % 2][:, :], ctxT_bank[:, :]).then_inc(ctxT_sbuf, 1)

            in_steps(nc.scalar, ((exp, 3), (keep_ctxT, 4)))


def attention_out(nc, x, ctx, kept_xn, w, const, logits_bank):
    with ExitStack() as stack:
        def sb(name, shape, dt=FP32):
            return stack.enter_context(nc.sbuf_tensor("o_" + name, shape, dt))

        def bank(name):
            return stack.enter_context(nc.psum_tensor("o_" + name, [P, CT * P], FP32))

        def sem(name):
            return stack.enter_context(nc.semaphore("o_" + name))

        stats, mv = sb("stats", [P, CT, 6]), sb("mv", [P, CT, 2])
        vare, rstd = sb("vare", [P, CT]), sb("rstd", [P, CT])
        ctxT, xnT = sb("ctxT", [P, CT * P]), sb("xnT", [P, CT * P])
        ctxT_bank, out_bank, xnT_bank = bank("ctxT_bank"), bank("out_bank"), bank("xnT_bank")
        moments, rstd_ready, dve_step = sem("moments"), sem("rstd"), sem("dve_step")
        ctxT_psum, ctxT_sbuf, out_psum, x_done = sem("ctxT_psum"), sem("ctxT_sbuf"), sem("out_psum"), sem("x_done")
        xn_ready, xnT_psum, xnT_sbuf, logits_psum = sem("xn_ready"), sem("xnT_psum"), sem("xnT_sbuf"), sem("logits")
        block = stack.enter_context(nc.Block())

        @block.vector
        def _(dve):
            def add_and_norm(c):
                step = Steps(dve, dve_step, c, 3)
                dve.wait_ge(out_psum, c + 1)
                step(nc.vector.tensor_tensor(part(x, c), out_bank[:, :], part(x, c), ALU.add))
                layer_norm_stats(nc, stats, mv, vare, x, c, step, moments)
                step.end()

            def xn_of(c):
                dve.wait_ge(rstd_ready, c + 1)
                for k in range(CT):
                    last = nc.vector.tensor_scalar(part(kept_xn, c, k), part(x, c, k), mv[:, k, 0:1],
                                                   rstd[:, k:k + 1], ALU.subtract, ALU.mult)
                last.then_inc(xn_ready, 1)

            staged(((add_and_norm, 0), (xn_of, 0)))

        @block.gpsimd
        def _(pool):
            for c in range(NCH):
                pool.wait_ge(moments, c + 1)
                nc.gpsimd.tensor_tensor(rstd[:, :], vare[:, :], const["minus_half"][:, 0:CT],
                                        ALU.pow).then_inc(rstd_ready, 1)

        @block.scalar
        def _(act):
            def ctx_turned(c):
                act.wait_ge(ctxT_psum, c + 1)
                nc.scalar.copy(ctxT[:, :], ctxT_bank[:, :]).then_inc(ctxT_sbuf, 1)

            def xn_turned(c):
                act.wait_ge(xnT_psum, c + 1)
                nc.scalar.copy(xnT[:, :], xnT_bank[:, :]).then_inc(xnT_sbuf, 1)

            staged(((ctx_turned, 0), (xn_turned, 1)))

        @block.tensor
        def _(pe):
            def out(c):
                for k in range(CT):
                    last = nc.tensor.transpose(ctxT_bank[:, k * P:(k + 1) * P], part(ctx, c, k), const["ident"][:, :])
                last.then_inc(ctxT_psum, 1)
                pe.wait_ge(ctxT_sbuf, c + 1)
                if c >= 1:
                    pe.wait_ge(dve_step, 3 * (c - 1) + 1)
                for k in range(CT):
                    last = nc.tensor.matmul(out_bank[:, k * C:(k + 1) * C], ctxT[:, k * P:(k + 1) * P],
                                            const["wo"][:, :], start=True, stop=True)
                last.then_inc(out_psum, 1)

            def logits(c):
                pe.wait_ge(xn_ready, c + 1)
                for k in range(CT):
                    last = nc.tensor.transpose(xnT_bank[:, k * P:(k + 1) * P], part(kept_xn, c, k), const["ident"][:, :])
                last.then_inc(xnT_psum, 1)
                pe.wait_ge(xnT_sbuf, c + 1)
                for k in range(CT):
                    t = c * CT + k
                    last = nc.tensor.matmul(logits_bank[:, t * NE:(t + 1) * NE], xnT[:, k * P:(k + 1) * P],
                                            w["wg"][:, :], start=True, stop=True)
                last.then_inc(logits_psum, 1)

            staged(((out, 0), (logits, 1)))


INPUTS = ["L0_attn_a_x", "L0_attn_a_w1", "L0_attn_a_b1", "L0_attn_a_w2", "L0_attn_a_b2", "L0_attn_a_gamma1",
          "L0_attn_a_beta1", "L0_attn_a_gamma2", "L0_attn_a_beta2", "L0_attn_b_Wq", "L0_attn_b_Wk", "L0_attn_b_Wv",
          "L0_attn_b_Wo", "L0_attn_b_bo", "L0_attn_b_w", "L0_attn_b_v", "L0_ffn_W1", "L0_ffn_W2", "L0_ffn_Wg",
          "L0_ffn_bg"]
STAGE = 9


def program(nc, ins, out):
    slots_dram = nc.dram_tensor("slots", [SLOT_TILES * P, C], FP32, kind="Internal").ap()
    y_dram = nc.dram_tensor("expert_out", [SLOT_TILES * P, C], FP32, kind="Internal").ap()
    q_dram = nc.dram_tensor("query_parts", [BATCH, PARTS, P, SEQ], BF16, kind="Internal").ap()
    k_dram = nc.dram_tensor("key_parts", [BATCH, PARTS, P, SEQ], BF16, kind="Internal").ap()
    with ExitStack() as stack:
        def sb(name, shape, dt=FP32):
            return stack.enter_context(nc.sbuf_tensor(name, shape, dt))

        x = sb("x", [P, NT * C])
        w = dict(w1=sb("w1", [P, NE * HID]), w2=sb("w2", [P, NE * HID]), wg=sb("wg", [P, NE]))
        const = dict(
            ident=sb("ident", [P, P]), before=sb("before", [P, P], BF16), ones=sb("ones", [P, P], BF16),
            zero=sb("zero", [P, NE * NT]), order=sb("order", [P, NE]), tileno=sb("tileno", [P, SLOT_TILES]),
            minus_half=sb("minus_half", [P, 8]), half_pi=sb("half_pi", [P, 1]),
            slot=sb("slot", [P, NT], U32), tile_expert=sb("tile_expert", [P, SLOT_TILES], I32),
            ident16=sb("ident16", [P, P], BF16), after=sb("after", [P, P], BF16),
            wq=sb("wq", [P, C]), wk=sb("wk", [P, C]), wv=sb("wv", [P, C]), wo=sb("wo", [P, C]),
            w1T=sb("w1T", [NQ, FFN]), w2T=sb("w2T", [P, NFC, C]), b1=sb("b1", [P, NFC]))
        rows = {"b2": "L0_attn_a_b2", "gamma1": "L0_attn_a_gamma1", "beta1": "L0_attn_a_beta1",
                "gamma2": "L0_attn_a_gamma2", "beta2": "L0_attn_a_beta2", "bo": "L0_attn_b_bo", "bg": "L0_ffn_bg"}
        for name, source in rows.items():
            const[name] = sb(name, [P, ins[source].shape[0]])
        t2 = sb("t2", [P, NT * C])
        setup(nc, ins, x, t2, w, const, rows, slots_dram)
        view = "p (t c) -> p t c"
        x3, t23 = x[:, :].rearrange(view, c=C), t2[:, :].rearrange(view, c=C)
        with ExitStack() as inner:
            const["logits_bank"] = inner.enter_context(nc.psum_tensor("logits_bank", [P, NT * NE], FP32))
            with ExitStack() as scratch:
                y, t1, xb = (scratch.enter_context(nc.sbuf_tensor(n, [P, NT * C], FP32)) for n in ("y", "t1", "xb"))
                block_a(nc, x, y, t1, t2, xb, w, const)
            if STAGE >= 2:
                route(nc, "r1_", t23, const, slots_dram)
        if STAGE >= 2:
            expert_tiles(nc, "e1_", w, const, slots_dram, y_dram)
            combine(nc, "c1_", x3, t23, const, y_dram)
        if STAGE >= 3:
            with ExitStack() as inner:
                table = inner.enter_context(nc.sbuf_tensor("table", [P, NH, SEQ], FP32))
                v_ones = inner.enter_context(nc.sbuf_tensor("v_ones", [P, NT * NH * (HD + 1)], FP32))
                position_table(nc, ins, table)
                project(nc, x, const, v_ones[:, :].rearrange("p (g d) -> p g d", d=HD + 1), q_dram, k_dram)
                attend(nc, const, v_ones, table, q_dram, k_dram, t2)
            with ExitStack() as inner:
                const["logits_bank"] = inner.enter_context(nc.psum_tensor("logits_bank2", [P, NT * NE], FP32))
                xn2 = inner.enter_context(nc.sbuf_tensor("xn2", [P, NT * C], FP32))
                attention_out(nc, x, t2, xn2, w, const, const["logits_bank"])
                if STAGE >= 4:
                    route(nc, "r2_", xn2[:, :].rearrange(view, c=C), const, slots_dram)
        if STAGE >= 4:
            expert_tiles(nc, "e2_", w, const, slots_dram, y_dram)
            combine(nc, "c2_", x3, t23, const, y_dram)
        with nc.semaphore("stored") as stored, nc.Block() as block:
            @block.sync
            def _(sp):
                sp.dma_start(out.rearrange("(t p) c -> p t c", p=P), x3).then_inc(stored, 16)
                sp.wait_ge(stored, 16)


def setup(nc, ins, x, blank, w, const, rows, slots_dram):
    with ExitStack() as stack:
        loads = stack.enter_context(nc.semaphore("loads"))
        zeroed = stack.enter_context(nc.semaphore("zeroed"))
        pool_made = stack.enter_context(nc.semaphore("pool_made"))
        blanked = stack.enter_context(nc.semaphore("blanked"))
        block = stack.enter_context(nc.Block())

        @block.sync
        def _(sp):
            n = [0]

            def load(dst, src):
                n[0] += 16
                sp.dma_start(dst, src).then_inc(loads, 16)

            load(x[:, :].rearrange("p (t c) -> p t c", c=C),
                 ins["L0_attn_a_x"].rearrange("b s c -> (b s) c").rearrange("(t p) c -> p t c", p=P))
            load(const["w1T"][:, :], ins["L0_attn_a_w1"])
            load(const["w2T"][:, :, :], ins["L0_attn_a_w2"].rearrange("(f p) c -> p f c", p=P))
            load(const["b1"][:, :], ins["L0_attn_a_b1"])
            for name, source in rows.items():
                src = ins[source]
                load(const[name][:, :], src.unsqueeze(0).broadcast_to((P, src.shape[0])))
            load(w["wg"][:, :], ins["L0_ffn_Wg"])
            for s in "qkvo":
                load(const["w" + s][:, :], ins["L0_attn_b_W" + s])
            load(w["w1"][:, :].rearrange("p (e h) -> p e h", e=NE), ins["L0_ffn_W1"].rearrange("e d h -> d e h"))
            load(w["w2"][:, :].rearrange("p (e k c) -> p e k c", e=NE, k=NHC),
                 ins["L0_ffn_W2"].rearrange("e (k p) c -> p e k c", p=P))
            sp.wait_ge(blanked, 1)
            empty = slots_dram.rearrange("(t p) c -> p t c", p=P)
            src = blank[:, :].rearrange("p (t c) -> p t c", c=C)
            sp.dma_start(empty[:, 0:NT, :], src).then_inc(zeroed, 16)
            sp.dma_start(empty[:, NT:, :], src[:, 0:SLOT_TILES - NT, :]).then_inc(zeroed, 16)
            sp.wait_ge(loads, n[0])
            sp.wait_ge(zeroed, 32)

        @block.vector
        def _(dve):
            nc.vector.memset(blank[:, :], 0.0).then_inc(blanked, 1)

        @block.gpsimd
        def _(pool):
            nc.gpsimd.memset(const["zero"][:, :], 0.0)
            nc.gpsimd.memset(const["ident"][:, :], 0.0)
            nc.gpsimd.memset(const["before"][:, :], 1.0)
            nc.gpsimd.memset(const["ident16"][:, :], 0.0)
            nc.gpsimd.memset(const["after"][:, :], 0.0)
            nc.gpsimd.memset(const["ones"][:, :], 1.0)
            nc.gpsimd.memset(const["minus_half"][:, :], -0.5)
            nc.gpsimd.memset(const["half_pi"][:, :], np.pi / 2)
            nc.gpsimd.iota(const["order"][:, :], pattern=[[-1, NE]], base=NE, channel_multiplier=0,
                           allow_small_or_imprecise_dtypes=True)
            nc.gpsimd.iota(const["tileno"][:, :], pattern=[[1, SLOT_TILES]], base=0, channel_multiplier=0,
                           allow_small_or_imprecise_dtypes=True).then_inc(pool_made, 1)
            pool.wait_ge(pool_made, 1)
            nc.gpsimd.affine_select(out=const["ident"][:, :], in_=const["ident"][:, :], compare_op=ALU.not_equal,
                                    fill=1.0, base=0, pattern=[[-1, P]], channel_multiplier=1)
            nc.gpsimd.affine_select(out=const["ident16"][:, :], in_=const["ident16"][:, :], compare_op=ALU.not_equal,
                                    fill=1.0, base=0, pattern=[[-1, P]], channel_multiplier=1)
            nc.gpsimd.affine_select(out=const["after"][:, :], in_=const["after"][:, :], compare_op=ALU.is_ge,
                                    fill=BIG, base=0, pattern=[[-1, P]], channel_multiplier=1)
            nc.gpsimd.affine_select(out=const["before"][:, :], in_=const["before"][:, :], compare_op=ALU.is_gt,
                                    fill=0.0, base=0, pattern=[[1, P]], channel_multiplier=-1).then_inc(pool_made, 1)
            pool.wait_ge(pool_made, 2)


def kernel(**inputs):
    import numpy as _np
    import concourse.bacc as _bacc
    from concourse import mybir as _mybir
    from concourse.bass_utils import run_bass_kernel_spmd as _run

    nc = _bacc.Bacc("TRN2", target_bir_lowering=False, num_devices=1)
    arrays, args = {}, {}
    for name in INPUTS:
        a = _np.asarray(inputs[name])
        if name in ("L0_attn_a_w1", "L0_attn_a_w2"):
            a = a.T
        if name == "L0_attn_a_b1":
            a = a.reshape(NFC, P).T
        a = _np.ascontiguousarray(a)
        arrays["in_" + name] = a
        args[name] = nc.dram_tensor("in_" + name, a.shape, _mybir.dt.from_np(a.dtype), kind="ExternalInput").ap()
    out = nc.dram_tensor("out_0", (TOK, C), _mybir.dt.float32, kind="ExternalOutput").ap()
    program(nc, args, out)
    r = _run(nc, [arrays], core_ids=[0])
    return _np.asarray(r.results[0]["out_0"]).reshape(BATCH, SEQ, C)
```

```python
from contextlib import ExitStack
import concourse.bass as bass
import concourse.mybir as mybir
import numpy as np

FP32 = mybir.dt.float32
BF16 = mybir.dt.bfloat16
I32 = mybir.dt.int32
U32 = mybir.dt.uint32
ALU = mybir.AluOpType
ACT = mybir.ActivationFunctionType
AX = mybir.AxisListType

P = 128
BATCH, SEQ, C = 16, 256, 128
TOK = BATCH * SEQ
NT = TOK // P
NE, HID = 8, 512
NHC = HID // P
SLOT_TILES = NT + NE
EPS = 1e-5
ROUND = 1.5 * 2.0 ** 23
NQ, FFN = 16, 512
NFC = FFN // P
NH, HD = 16, 8
CT = 4
NCH = NT // CT
SLOTS_EMPTY = 2 * 16


INV_2PI = 1.0 / (2.0 * np.pi)
TWO_PI = float(np.float32(2.0 * np.pi))
TWO_PI_HI = 6.28125
TWO_PI_LO = 2.0 * np.pi - TWO_PI_HI


class Steps:

    def __init__(self, eng, sem, run, per_run):
        self.eng, self.sem, self.base, self.per_run, self.n = eng, sem, run * per_run, per_run, 0

    def __call__(self, ins):
        self.n += 1
        ins.then_inc(self.sem, 1)
        self.eng.wait_ge(self.sem, self.base + self.n)

    def end(self):
        assert self.n == self.per_run


def block_a(nc, x, y, t1, t2, xb, w, const, x_here):
    N = CT * C
    with ExitStack() as stack:
        def sb(name, shape, dt=FP32):
            return stack.enter_context(nc.sbuf_tensor("a_" + name, shape, dt))

        def bank(name, shape):
            return stack.enter_context(nc.psum_tensor("a_" + name, shape, FP32))

        def sem(name):
            return stack.enter_context(nc.semaphore("a_" + name))

        NORMS = ("in", "mid", "out", "moe")
        stats = {n: sb("stats_" + n, [P, CT, 6]) for n in NORMS}
        mv = {n: sb("mv_" + n, [P, CT, 2]) for n in NORMS}
        vare = {n: sb("vare_" + n, [P, CT]) for n in NORMS}
        rstd = {n: [sb(f"rstd_{n}{b}", [P, CT]) for b in range(2)] for n in NORMS}
        minus_mean = {n: sb("minus_mean_" + n, [P, CT]) for n in NORMS}
        offset = {n: [sb(f"offset_{n}{b}", [P, CT]) for b in range(2)] for n in NORMS}
        ang = sb("ang", [P, CT * NQ])
        turns = sb("turns", [P, CT * NQ])
        qT = sb("qT", [NQ, CT * P])
        hT = sb("hT", [P, NFC, CT * P])
        xnT = sb("xnT", [P, CT * P])
        qT_bank = bank("qT_bank", [P, CT * P])
        h_bank = [bank(f"h_bank{b}", [P, CT * P]) for b in range(2)]
        ffn_bank = [bank(f"ffn_bank{b}", [P, CT * C]) for b in range(2)]
        xnT_bank = bank("xnT_bank", [P, CT * P])
        moments = {n: sem("moments_" + n) for n in NORMS}
        scales = {n: sem("scales_" + n) for n in NORMS}
        steps = {n: sem("steps_" + n) for n in ("in", "y", "mid", "x1", "q", "z2", "x", "act_y", "act_q")}
        y_ready = sem("y_ready")
        angle_y = sem("angle_y")
        cos_y = sem("cos_y")
        x1_ready = sem("x1_ready")
        angle_q = sem("angle_q")
        cos_q = sem("cos_q")
        x1b_ready = sem("x1b_ready")
        xb_ready = sem("xb_ready")
        q_ready = sem("q_ready")
        qT_psum = sem("qT_psum")
        qT_sbuf = sem("qT_sbuf")
        h_psum = sem("h_psum")
        h_sbuf = sem("h_sbuf")
        ffn_psum = sem("ffn_psum")
        normed_mid, normed_out, scaled_out = sem("normed_mid"), sem("normed_out"), sem("scaled_out")
        xn_ready = sem("xn_ready")
        xnT_psum = sem("xnT_psum")
        xnT_sbuf = sem("xnT_sbuf")
        logits_psum = sem("logits_psum")
        block = stack.enter_context(nc.Block())

        def part(a, c, k=None, cols=None):
            if k is None:
                return a[:, c * N:(c + 1) * N]
            return a[:, c * N + k * C:c * N + (k + 1) * C]

        def in_steps(stages):
            for s in range(NCH + max(lag for _, lag in stages)):
                for f, lag in stages:
                    if 0 <= s - lag < NCH:
                        f(s - lag)

        def tiles(a, c):
            return part(a, c).rearrange("p (t n) -> p t n", t=CT)

        def each_tile(name):
            return const[name][:, :].unsqueeze(1).broadcast_to((P, CT, C))

        @block.vector
        def _(dve):
            def stats_of(n, src, c, step):
                for k in range(CT):
                    last = nc.vector.bn_stats(stats[n][:, k, :], part(src, c, k))
                step(last)
                for k in range(CT):
                    last = nc.vector.bn_aggr(mv[n][:, k, :], stats[n][:, k, :])
                step(last)
                nc.vector.tensor_scalar(minus_mean[n][:, :], mv[n][:, :, 0], -1.0, None, ALU.mult)
                nc.vector.tensor_scalar(vare[n][:, :], mv[n][:, :, 1], EPS, None, ALU.add).then_inc(moments[n], 1)

            def norm_in(c):
                step = Steps(dve, steps["in"], c, 2)
                dve.wait_ge(x_here[c], 16)
                stats_of("in", x, c, step)
                step.end()

            def products_of_y(c):
                step = Steps(dve, steps["mid"], c, HD - 1 + 3)
                dve.wait_ge(cos_y, c + 1)
                heads = part(t1, c).rearrange("p (g d) -> p g d", d=HD)
                for d in range(1, HD):
                    step(nc.vector.tensor_tensor(heads[:, :, d], heads[:, :, d], heads[:, :, d - 1], ALU.mult))
                step(nc.vector.tensor_tensor(part(t2, c), part(y, c), part(t1, c), ALU.add))
                stats_of("mid", t2, c, step)
                step.end()

            def x1_of(c):
                step = Steps(dve, steps["x1"], c, 4)
                dve.wait_ge(normed_mid, c + 1)
                step(nc.vector.tensor_tensor(tiles(t1, c), tiles(t1, c), each_tile("gamma1"), ALU.mult))
                nc.vector.tensor_tensor(tiles(y, c), tiles(t1, c), each_tile("beta1"), ALU.add).then_inc(x1_ready, 1)
                dve.wait_ge(x1_ready, c + 1)
                if c >= 1:
                    dve.wait_ge(qT_psum, c)
                q_cols = part(y, c).rearrange("p (t n) -> p t n", t=CT)[:, :, 0:NQ]
                ang3 = ang[:, :].rearrange("p (t n) -> p t n", t=CT)
                turns3 = turns[:, :].rearrange("p (t n) -> p t n", t=CT)
                step(nc.vector.tensor_scalar(ang3, q_cols, INV_2PI, ROUND, ALU.mult, ALU.add))
                step(nc.vector.tensor_scalar(turns[:, :], ang[:, :], ROUND, None, ALU.subtract))
                step(nc.vector.scalar_tensor_tensor(out=ang3, in0=turns3, scalar=-TWO_PI_HI, in1=q_cols,
                                                    op0=ALU.mult, op1=ALU.add))
                nc.vector.scalar_tensor_tensor(out=turns[:, :], in0=turns[:, :], scalar=-TWO_PI_LO, in1=ang[:, :],
                                               op0=ALU.mult, op1=ALU.add).then_inc(angle_q, 1)
                step.end()

            def products_of_q(c):
                step = Steps(dve, steps["q"], c, 3 + NQ // 4 - 2)
                dve.wait_ge(cos_q, c + 1)
                q4 = ang[:, :].rearrange("p (g d) -> p g d", d=4)
                for d in range(1, 4):
                    step(nc.vector.tensor_tensor(q4[:, :, d], q4[:, :, d], q4[:, :, d - 1], ALU.mult))
                qt = ang[:, :].rearrange("p (t n) -> p t n", n=NQ)
                for g in range(1, NQ // 4):
                    last = nc.vector.tensor_tensor(qt[:, :, 4 * g:4 * g + 4], qt[:, :, 4 * g:4 * g + 4],
                                                   qt[:, :, 4 * g - 1:4 * g].broadcast_to((P, CT, 4)), ALU.mult)
                    if g < NQ // 4 - 1:
                        step(last)
                last.then_inc(q_ready, 1)
                step.end()

            def norm_out(c):
                step = Steps(dve, steps["z2"], c, 3)
                dve.wait_ge(ffn_psum, c + 1)
                dve.wait_ge(x1b_ready, c + 1)
                step(nc.vector.tensor_tensor(part(t2, c), ffn_bank[c % 2][:, :], part(t1, c), ALU.add))
                stats_of("out", t2, c, step)
                step.end()

            def x_of(c):
                step = Steps(dve, steps["x"], c, 3)
                dve.wait_ge(scaled_out, c + 1)
                dve.wait_ge(xb_ready, c + 1)
                step(nc.vector.tensor_tensor(part(x, c), part(y, c), part(xb, c), ALU.add))
                stats_of("moe", x, c, step)
                step.end()

            in_steps(((products_of_q, 2), (norm_out, 3), (products_of_y, 1), (norm_in, 0), (x_of, 3), (x1_of, 1)))

        @block.gpsimd
        def _(pool):
            def power(n):
                def stage(c):
                    pool.wait_ge(moments[n], c + 1)
                    nc.gpsimd.tensor_tensor(rstd[n][c % 2][:, :], vare[n][:, :], const["minus_half"][:, 0:CT],
                                            ALU.pow).then_inc(scales[n], 1)
                    pool.wait_ge(scales[n], 2 * c + 1)
                    nc.gpsimd.tensor_tensor(offset[n][c % 2][:, :], minus_mean[n][:, :], rstd[n][c % 2][:, :],
                                            ALU.mult).then_inc(scales[n], 1)
                return stage

            def x_and_beta2(c):
                pool.wait_ge(x_here[c], 16)
                nc.gpsimd.tensor_tensor(tiles(xb, c), tiles(x, c), each_tile("beta2"), ALU.add).then_inc(xb_ready, 1)

            def x1_and_b2(c):
                pool.wait_ge(x1_ready, c + 1)
                nc.gpsimd.tensor_tensor(tiles(t1, c), tiles(y, c), each_tile("b2"), ALU.add).then_inc(x1b_ready, 1)

            def scale_out(c):
                pool.wait_ge(normed_out, c + 1)
                nc.gpsimd.tensor_tensor(tiles(y, c), tiles(y, c), each_tile("gamma2"), ALU.mult).then_inc(scaled_out, 1)

            def angles_of_y(c):
                step = Steps(pool, steps["y"], c, 2)
                pool.wait_ge(y_ready, c + 1)
                step(nc.gpsimd.tensor_scalar(part(t1, c), part(y, c), INV_2PI, ROUND, ALU.mult, ALU.add))
                step(nc.gpsimd.tensor_scalar(part(t2, c), part(t1, c), -ROUND, -TWO_PI, ALU.add, ALU.mult))
                nc.gpsimd.tensor_tensor(part(t1, c), part(t2, c), part(y, c), ALU.add).then_inc(angle_y, 1)
                step.end()

            in_steps(((power("out"), 3), (x_and_beta2, 0), (scale_out, 3), (power("mid"), 1), (power("in"), 0),
                      (angles_of_y, 0), (power("moe"), 3), (x1_and_b2, 1)))

        @block.scalar
        def _(act):
            def cosines_of_y(c):
                step = Steps(act, steps["act_y"], c, 1)
                act.wait_ge(angle_y, c + 1)
                step(nc.scalar.activation(part(t2, c), part(t1, c), ACT.Abs))
                nc.scalar.activation(part(t1, c), part(t2, c), ACT.Sin, bias=const["half_pi"][:, 0:1],
                                     scale=-1.0).then_inc(cos_y, 1)

            def cosines_of_q(c):
                step = Steps(act, steps["act_q"], c, 1)
                act.wait_ge(angle_q, c + 1)
                step(nc.scalar.activation(turns[:, :], turns[:, :], ACT.Abs))
                nc.scalar.activation(ang[:, :], turns[:, :], ACT.Sin, bias=const["half_pi"][:, 0:1],
                                     scale=-1.0).then_inc(cos_q, 1)

            def q_turned(c):
                act.wait_ge(qT_psum, c + 1)
                nc.scalar.copy(qT[:, :], qT_bank[0:NQ, :]).then_inc(qT_sbuf, 1)

            def hidden(*fs):
                def stage(c):
                    for f in fs:
                        act.wait_ge(h_psum, c * NFC + f + 1)
                        nc.scalar.activation(hT[:, f, :], h_bank[f % 2][:, :], ACT.Relu,
                                             bias=const["b1"][:, f:f + 1]).then_inc(h_sbuf, 1)
                return stage

            def xn_turned(c):
                act.wait_ge(xnT_psum, c + 1)
                nc.scalar.copy(xnT[:, :], xnT_bank[:, :]).then_inc(xnT_sbuf, 1)

            def normed(n, dst, src, ready):
                def stage(c):
                    act.wait_ge(scales[n], 2 * c + 2)
                    for k in range(CT):
                        last = nc.scalar.activation(part(dst, c, k), part(src, c, k), ACT.Identity,
                                                    bias=offset[n][c % 2][:, k:k + 1], scale=rstd[n][c % 2][:, k:k + 1])
                    last.then_inc(ready, 1)
                return stage

            in_steps(((q_turned, 2), (normed("out", y, t2, normed_out), 3), (hidden(0, 1, 2), 2),
                      (normed("mid", t1, t2, normed_mid), 1), (hidden(3), 2), (normed("in", y, x, y_ready), 0),
                      (cosines_of_q, 1), (normed("moe", t2, x, xn_ready), 4), (xn_turned, 4), (cosines_of_y, 0)))

        @block.tensor
        def _(pe):
            def ffn(c):
                pe.wait_ge(q_ready, c + 1)
                for k in range(CT):
                    last = nc.tensor.transpose(qT_bank[0:NQ, k * P:(k + 1) * P], ang[:, k * NQ:(k + 1) * NQ],
                                               const["ident"][:, :])
                last.then_inc(qT_psum, 1)
                pe.wait_ge(qT_sbuf, c + 1)
                for f in range(NFC):
                    if c * NFC + f >= 2:
                        pe.wait_ge(h_sbuf, c * NFC + f - 1)
                    nc.tensor.matmul(h_bank[f % 2][:, :], const["w1T"][:, f * P:(f + 1) * P], qT[:, :],
                                     start=True, stop=True).then_inc(h_psum, 1)
                if c >= 2:
                    pe.wait_ge(steps["z2"], 3 * (c - 2) + 1)
                for f in range(NFC):
                    pe.wait_ge(h_sbuf, c * NFC + f + 1)
                    for k in range(CT):
                        last = nc.tensor.matmul(ffn_bank[c % 2][:, k * C:(k + 1) * C], hT[:, f, k * P:(k + 1) * P],
                                                const["w2T"][:, f, :], start=(f == 0 and k == 0), stop=(f == NFC - 1),
                                                skip_group_check=True)
                last.then_inc(ffn_psum, 1)

            def turn_xn(c):
                pe.wait_ge(xn_ready, c + 1)
                if c >= 1:
                    pe.wait_ge(xnT_sbuf, c)
                for k in range(CT):
                    last = nc.tensor.transpose(xnT_bank[:, k * P:(k + 1) * P], part(t2, c, k), const["ident"][:, :])
                last.then_inc(xnT_psum, 1)

            def logits(c):
                pe.wait_ge(xnT_sbuf, c + 1)
                for k in range(CT):
                    last = nc.tensor.matmul(const["logits_bank"][:, (c * CT + k) * NE:(c * CT + k + 1) * NE],
                                            xnT[:, k * P:(k + 1) * P], w["wg"][:, :], start=True, stop=True)
                last.then_inc(logits_psum, 1)

            in_steps(((ffn, 2), (turn_xn, 4), (logits, 4)))


def route(nc, tag, xn, const, slots_dram, slots_empty, table=None, big_weights=None):
    with ExitStack() as stack:
        logits = stack.enter_context(nc.sbuf_tensor(tag + "logits", [P, NT, NE], FP32))
        best = stack.enter_context(nc.sbuf_tensor(tag + "best", [P, NT], FP32))
        isbest = stack.enter_context(nc.sbuf_tensor(tag + "isbest", [P, NT, NE], FP32))
        rankval = stack.enter_context(nc.sbuf_tensor(tag + "rankval", [P, NT, NE], FP32))
        onehot = stack.enter_context(nc.sbuf_tensor(tag + "onehot", [P, NE, NT], BF16))
        tot = stack.enter_context(nc.sbuf_tensor(tag + "tot", [P, NE, NT], FP32))
        cum = stack.enter_context(nc.sbuf_tensor(tag + "cum", [P, NE, NT], FP32))
        cnt = stack.enter_context(nc.sbuf_tensor(tag + "cnt", [P, NE], FP32))
        tiles_a = stack.enter_context(nc.sbuf_tensor(tag + "tiles_a", [P, NE], FP32))
        tiles_e = stack.enter_context(nc.sbuf_tensor(tag + "tiles_e", [P, NE], FP32))
        end_e = stack.enter_context(nc.sbuf_tensor(tag + "end_e", [P, NE], FP32))
        adj = stack.enter_context(nc.sbuf_tensor(tag + "adj", [P, NE], FP32))
        adj2 = stack.enter_context(nc.sbuf_tensor(tag + "adj2", [P, NE], FP32))
        pos = stack.enter_context(nc.sbuf_tensor(tag + "pos", [P, NE, NT], FP32))
        slotf = stack.enter_context(nc.sbuf_tensor(tag + "slotf", [P, NT], FP32))
        past = stack.enter_context(nc.sbuf_tensor(tag + "past", [P, SLOT_TILES, NE], FP32))
        tilef = stack.enter_context(nc.sbuf_tensor(tag + "tilef", [P, SLOT_TILES], FP32))
        pR = stack.enter_context(nc.psum_tensor(tag + "pR", [P, 2, NE * NT], FP32))
        onehot_ready = stack.enter_context(nc.semaphore(tag + "onehot_ready"))
        counts_psum = stack.enter_context(nc.semaphore(tag + "counts_psum"))
        slots_ready = stack.enter_context(nc.semaphore(tag + "slots_ready"))
        scattered = stack.enter_context(nc.semaphore(tag + "scattered"))
        dve_step = stack.enter_context(nc.semaphore(tag + "dve_step"))
        if table is not None:
            dist = stack.enter_context(nc.sbuf_tensor("pt_dist", [P, SEQ], FP32))
            minus_w, ev, top = (stack.enter_context(nc.sbuf_tensor("pt_" + n, [P, NH], FP32))
                                for n in ("minus_w", "ev", "top"))
            grown = stack.enter_context(nc.sbuf_tensor("pt_grown", [P, NH, SEQ], FP32))
            dist_made, dist_ready, grown_made, grown_step, weights, masked = (
                stack.enter_context(nc.semaphore("pt_" + n))
                for n in ("dist_made", "dist_ready", "grown_made", "grown_step", "weights", "masked"))
        block = stack.enter_context(nc.Block())

        @block.vector
        def _(dve):
            done = [0]

            def step(ins):
                done[0] += 1
                ins.then_inc(dve_step, 1)
                dve.wait_ge(dve_step, done[0])

            step(nc.vector.tensor_tensor(logits[:, :, :], const["logits_bank"][:, :].rearrange("p (t e) -> p t e", e=NE),
                                         const["bg"][:, :].unsqueeze(1).broadcast_to((P, NT, NE)), ALU.add))
            step(nc.vector.tensor_reduce(best[:, :], logits[:, :, :], AX.X, ALU.max))
            step(nc.vector.tensor_tensor(isbest[:, :, :], logits[:, :, :],
                                         best[:, :].unsqueeze(2).broadcast_to((P, NT, NE)), ALU.is_equal))
            order = const["order"][:, :].unsqueeze(1).broadcast_to((P, NT, NE))
            step(nc.vector.tensor_tensor(rankval[:, :, :], isbest[:, :, :], order, ALU.mult))
            step(nc.vector.tensor_reduce(best[:, :], rankval[:, :, :], AX.X, ALU.max))
            nc.vector.tensor_tensor(onehot[:, :, :].rearrange("p e t -> p t e"), order,
                                    best[:, :].unsqueeze(2).broadcast_to((P, NT, NE)),
                                    ALU.is_equal).then_inc(onehot_ready, 1)
            if table is not None:
                nc.vector.tensor_scalar(minus_w[:, :], const["w"][:, :], -1.0, None, ALU.mult)
                dve.wait_ge(dist_made, 1)
                nc.vector.tensor_scalar(dist[:, :], dist[:, :], 0.0, None, ALU.max).then_inc(dist_ready, 1)
            dve.wait_ge(counts_psum, 1)
            step(nc.vector.tensor_copy(tot[:, :, :], pR[:, 1, :].rearrange("p (e t) -> p e t", e=NE)))
            flat = "p e t -> p (e t)"
            nc.vector.tensor_tensor_scan(cum[:, :, :].rearrange(flat), tot[:, :, :].rearrange(flat),
                                         const["zero"][:, 0:NE * NT], 0.0, ALU.add, ALU.add)
            step(nc.vector.tensor_reduce(cnt[:, :], tot[:, :, :], AX.X, ALU.add))
            step(nc.vector.tensor_scalar(tiles_a[:, :], cnt[:, :], 1.0 / P, (P - 1) / (2.0 * P), ALU.mult, ALU.add))
            step(nc.vector.tensor_scalar(tiles_e[:, :], tiles_a[:, :], ROUND, ROUND, ALU.add, ALU.subtract))
            step(nc.vector.tensor_tensor_scan(end_e[:, :], tiles_e[:, :], const["zero"][:, 0:NE], 0.0,
                                              ALU.add, ALU.add))
            step(nc.vector.tensor_tensor(adj[:, :], end_e[:, :], tiles_e[:, :], ALU.subtract))
            step(nc.vector.scalar_tensor_tensor(out=adj2[:, :], in0=adj[:, :], scalar=float(P), in1=tot[:, :, 0],
                                                op0=ALU.mult, op1=ALU.add))
            step(nc.vector.tensor_tensor(adj[:, :], adj2[:, :], cum[:, :, 0], ALU.subtract))
            step(nc.vector.tensor_tensor(pos[:, :, :], cum[:, :, :], tot[:, :, :], ALU.subtract))
            step(nc.vector.tensor_tensor(cum[:, :, :], pos[:, :, :], pR[:, 0, :].rearrange("p (e t) -> p e t", e=NE),
                                         ALU.add))
            step(nc.vector.tensor_tensor(pos[:, :, :], cum[:, :, :],
                                         adj[:, :].unsqueeze(2).broadcast_to((P, NE, NT)), ALU.add))
            step(nc.vector.tensor_tensor(cum[:, :, :], pos[:, :, :], onehot[:, :, :], ALU.mult))
            step(nc.vector.tensor_reduce(slotf[:, :], cum[:, :, :].rearrange("p e t -> p t e"), AX.X, ALU.add))
            nc.vector.tensor_copy(const["slot"][:, :], slotf[:, :]).then_inc(slots_ready, 1)
            step(nc.vector.tensor_tensor(past[:, :, :], end_e[:, :].unsqueeze(1).broadcast_to((P, SLOT_TILES, NE)),
                                         const["tileno"][:, :].unsqueeze(2).broadcast_to((P, SLOT_TILES, NE)),
                                         ALU.is_le))
            step(nc.vector.tensor_reduce(tilef[:, :], past[:, :, :], AX.X, ALU.add))
            step(nc.vector.tensor_scalar(const["tile_expert"][:, :], tilef[:, :], float(NE - 1), None, ALU.min))
            if table is not None:
                dve.wait_ge(grown_made, 1 + NH)
                nc.vector.tensor_scalar(top[:, :], ev[:, :], 1.0, float(1.0 / np.sqrt(HD)), ALU.add, ALU.mult)
                nc.vector.tensor_scalar(grown[:, :, :], grown[:, :, :], 1.0, None, ALU.add).then_inc(grown_step, 1)
                dve.wait_ge(grown_step, 1)
                nc.vector.reciprocal(grown[:, :, :], grown[:, :, :]).then_inc(grown_step, 1)
                dve.wait_ge(grown_step, 2)
                dve.wait_ge(slots_empty, SLOTS_EMPTY)
                nc.vector.tensor_tensor(table[:, :, :], grown[:, :, :],
                                        top[:, :].unsqueeze(2).broadcast_to((P, NH, SEQ)), ALU.mult).then_inc(weights, 1)

        if table is not None:
            @block.scalar
            def _(act):
                nc.scalar.activation(ev[:, :], const["v"][:, :], ACT.Exp).then_inc(grown_made, 1)
                act.wait_ge(dist_ready, 1)
                for h in range(NH):
                    nc.scalar.activation(grown[:, h, :], dist[:, :], ACT.Exp, bias=const["v"][:, h:h + 1],
                                         scale=minus_w[:, h:h + 1]).then_inc(grown_made, 1)

            @block.sync
            def _(sp):
                sp.wait_ge(*big_weights)

        @block.gpsimd
        def _(pool):
            if table is not None:
                nc.gpsimd.iota(dist[:, :], pattern=[[-1, SEQ]], base=P, channel_multiplier=1,
                               allow_small_or_imprecise_dtypes=True).then_inc(dist_made, 1)
            pool.wait_ge(slots_empty, SLOTS_EMPTY)
            pool.wait_ge(slots_ready, 1)
            for t in range(NT):
                nc.gpsimd.indirect_dma_start(
                    out=slots_dram[:, :], out_offset=bass.IndirectOffsetOnAxis(ap=const["slot"][:, t:t + 1], axis=0),
                    in_=xn[:, t, :], in_offset=None).then_inc(scattered, 16)
            if table is not None:
                pool.wait_ge(weights, 1)
                nc.gpsimd.affine_select(out=table[:, :, :], in_=table[:, :, :], compare_op=ALU.is_ge, fill=-1.0,
                                        base=P, pattern=[[0, NH], [-1, SEQ]], channel_multiplier=1).then_inc(masked, 1)
                pool.wait_ge(masked, 1)
            pool.wait_ge(scattered, 16 * NT)

        @block.tensor
        def _(pe):
            pe.wait_ge(onehot_ready, 1)
            oh = onehot[:, :, :].rearrange("p e t -> p (e t)")
            nc.tensor.matmul(pR[:, 0, :], const["before"][:, :], oh, start=True, stop=True)
            nc.tensor.matmul(pR[:, 1, :], const["ones"][:, :], oh, start=True, stop=True).then_inc(counts_psum, 1)


def expert_tiles(nc, tag, w, const, slots_dram, y_dram):
    U = 4
    assert SLOT_TILES % U == 0
    with ExitStack() as stack:
        xt = stack.enter_context(nc.sbuf_tensor(tag + "xt", [P, U, C], FP32))
        yt = stack.enter_context(nc.sbuf_tensor(tag + "yt", [P, U, C], FP32))
        xT = stack.enter_context(nc.sbuf_tensor(tag + "xT", [P, 2, P], FP32))
        hid = stack.enter_context(nc.sbuf_tensor(tag + "hid", [P, 2, HID], FP32))
        hidT = stack.enter_context(nc.sbuf_tensor(tag + "hidT", [P, 2, HID], FP32))
        xT_bank = [stack.enter_context(nc.psum_tensor(tag + f"xT_bank{b}", [P, 512], FP32)) for b in range(2)]
        hid_bank = [stack.enter_context(nc.psum_tensor(tag + f"hid_bank{b}", [P, HID], FP32)) for b in range(2)]
        hidT_bank = [stack.enter_context(nc.psum_tensor(tag + f"hidT_bank{b}", [P, HID], FP32)) for b in range(2)]
        y_bank = [stack.enter_context(nc.psum_tensor(tag + f"y_bank{b}", [P, 512], FP32)) for b in range(2)]
        loaded = [stack.enter_context(nc.semaphore(tag + f"loaded{u}")) for u in range(U)]
        stored = [stack.enter_context(nc.semaphore(tag + f"stored{u}")) for u in range(U)]
        xT_psum = stack.enter_context(nc.semaphore(tag + "xT_psum"))
        xT_sbuf = stack.enter_context(nc.semaphore(tag + "xT_sbuf"))
        hid_psum = stack.enter_context(nc.semaphore(tag + "hid_psum"))
        hid_sbuf = stack.enter_context(nc.semaphore(tag + "hid_sbuf"))
        hidT_psum = stack.enter_context(nc.semaphore(tag + "hidT_psum"))
        hidT_sbuf = stack.enter_context(nc.semaphore(tag + "hidT_sbuf"))
        y_psum = stack.enter_context(nc.semaphore(tag + "y_psum"))
        y_sbuf = stack.enter_context(nc.semaphore(tag + "y_sbuf"))
        block = stack.enter_context(nc.Block())

        FIRST = U + 3
        LOOPED = (SLOT_TILES - FIRST) // U * U

        def in_steps(eng, stages, begin=None):

            def one(s):
                for f, lag in stages:
                    if 0 <= s - lag < SLOT_TILES:
                        f(s - lag, (s - lag) % U, (s - lag) // U)

            for s in range(FIRST):
                one(s)
            with eng.Fori(0, LOOPED // U) as i:
                if begin is not None:
                    begin(i)
                for k in range(U):
                    for f, lag in stages:
                        j = FIRST + k - lag
                        f(i * U + j, j % U, i + j // U)
            for s in range(FIRST + LOOPED, SLOT_TILES + 3):
                one(s)

        def later(j, n):
            return not isinstance(j, int) or j >= n

        @block.sync
        def _(sp):
            for u in range(U):
                sp.dma_start(xt[:, u, :], slots_dram[u * P:(u + 1) * P, :]).then_inc(loaded[u], 16)
            with nc.sync.Fori(0, SLOT_TILES // U - 1) as i:
                for u in range(U):
                    sp.wait_ge(xT_psum, i * U + (u + 1))
                    sp.dma_start(xt[:, u, :], slots_dram[bass.ds(i * (U * P) + (U + u) * P, P), :]).then_inc(loaded[u], 16)

        @block.scalar
        def _(act):
            def gelu(j, u, turn):
                act.wait_ge(hid_psum, j + 1)
                if later(j, 2):
                    act.wait_ge(hidT_psum, j - 1)
                nc.scalar.activation(hid[:, u % 2, :], hid_bank[u % 2][:, :], ACT.Gelu_apprx_tanh).then_inc(hid_sbuf, 1)

            def copy_y(j, u, turn):
                act.wait_ge(y_psum, j + 1)
                if later(j, U):
                    act.wait_ge(stored[u], turn * 16)
                nc.scalar.copy(yt[:, u, :], y_bank[u % 2][:, 0:C]).then_inc(y_sbuf, 1)

            in_steps(nc.scalar, ((gelu, 1), (copy_y, 3)))

        @block.gpsimd
        def _(pool):
            with nc.gpsimd.Fori(0, SLOT_TILES // U) as i:
                for u in range(U):
                    pool.wait_ge(y_sbuf, i * U + (u + 1))
                    pool.dma_start(y_dram[bass.ds(i * (U * P) + u * P, P), :], yt[:, u, :]).then_inc(stored[u], 16)
            for u in range(U):
                pool.wait_ge(stored[u], 16 * SLOT_TILES // U)

        @block.vector
        def _(dve):
            def copy_x(j, u, turn):
                dve.wait_ge(xT_psum, j + 1)
                if later(j, 2):
                    dve.wait_ge(hid_psum, j - 1)
                nc.vector.tensor_copy(xT[:, u % 2, :], xT_bank[u % 2][:, 0:P]).then_inc(xT_sbuf, 1)

            def copy_hidden(j, u, turn):
                dve.wait_ge(hidT_psum, j + 1)
                if later(j, 2):
                    dve.wait_ge(y_psum, j - 1)
                nc.vector.tensor_copy(hidT[:, u % 2, :], hidT_bank[u % 2][:, :]).then_inc(hidT_sbuf, 1)

            in_steps(nc.vector, ((copy_x, 0), (copy_hidden, 2)))

        @block.tensor
        def _(pe):
            experts = {}

            def load_experts(i):
                _, values = nc.values_load_multi_w_load_instructions(
                    const["tile_expert"][0:1, bass.ds(i * U + (FIRST - 3), U + 2)],
                    engines=[mybir.EngineType.PE], min_val=0, max_val=NE - 1)
                experts.update(enumerate(values))

            def expert(j, u):
                if isinstance(j, int):
                    return nc.tensor.value_load(const["tile_expert"][0:1, bass.ds(j, 1)], min_val=0, max_val=NE - 1)
                return experts[u]

            def turn_x(j, u, turn):
                pe.wait_ge(loaded[u], turn * 16 + 16)
                if later(j, 2):
                    pe.wait_ge(xT_sbuf, j - 1)
                nc.tensor.transpose(xT_bank[u % 2][:, 0:P], xt[:, u, :], const["ident"][:, :]).then_inc(xT_psum, 1)

            def up(j, u, turn):
                e = expert(j, 2 + (u - (FIRST - 1)) % U)
                pe.wait_ge(xT_sbuf, j + 1)
                if later(j, 2):
                    pe.wait_ge(hid_sbuf, j - 1)
                nc.tensor.matmul(hid_bank[u % 2][:, :], xT[:, u % 2, :], w["w1"][:, bass.ds(e * HID, HID)],
                                 start=True, stop=True).then_inc(hid_psum, 1)

            def turn_hidden(j, u, turn):
                pe.wait_ge(hid_sbuf, j + 1)
                if later(j, 2):
                    pe.wait_ge(hidT_sbuf, j - 1)
                for k in range(NHC):
                    last = nc.tensor.transpose(hidT_bank[u % 2][:, k * P:(k + 1) * P],
                                               hid[:, u % 2, k * P:(k + 1) * P], const["ident"][:, :])
                last.then_inc(hidT_psum, 1)

            def down(j, u, turn):
                e = expert(j, (u - (FIRST - 3)) % U)
                pe.wait_ge(hidT_sbuf, j + 1)
                if later(j, 2):
                    pe.wait_ge(y_sbuf, j - 1)
                for k in range(NHC):
                    last = nc.tensor.matmul(y_bank[u % 2][:, 0:C], hidT[:, u % 2, k * P:(k + 1) * P],
                                            w["w2"][:, bass.ds(e * (NHC * C) + k * C, C)],
                                            start=(k == 0), stop=(k == NHC - 1))
                last.then_inc(y_psum, 1)

            in_steps(nc.tensor, ((turn_x, 0), (up, 1), (turn_hidden, 2), (down, 3)), load_experts)


def combine_and_store(nc, x, y, const, y_dram, gathered, out):
    with ExitStack() as stack:
        added = stack.enter_context(nc.semaphore("c_added"))
        stored = stack.enter_context(nc.semaphore("c_stored"))
        block = stack.enter_context(nc.Block())
        rows = out.rearrange("(t p) c -> p t c", p=P)

        @block.gpsimd
        def _(pool):
            for t in range(NT):
                nc.gpsimd.indirect_dma_start(
                    out=y[:, t, :], out_offset=None, in_=y_dram[:, :],
                    in_offset=bass.IndirectOffsetOnAxis(ap=const["slot"][:, t:t + 1], axis=0)
                ).then_inc(gathered[t // CT], 16)

        @block.vector
        def _(dve):
            for c in range(NCH):
                tiles = slice(c * CT, (c + 1) * CT)
                dve.wait_ge(gathered[c], 2 * 16 * CT)
                nc.vector.tensor_tensor(x[:, tiles, :], x[:, tiles, :], y[:, tiles, :], ALU.add).then_inc(added, 1)

        @block.sync
        def _(sp):
            for c in range(NCH):
                tiles = slice(c * CT, (c + 1) * CT)
                sp.wait_ge(added, c + 1)
                sp.dma_start(rows[:, tiles, :], x[:, tiles, :]).then_inc(stored, 16)
            sp.wait_ge(stored, 16 * NCH)


PARTS = 3
STACK = PARTS * PARTS * HD
BIG = 1e30


def staged(stages):
    for s in range(NCH + max(lag for _, lag in stages)):
        for f, lag in stages:
            if 0 <= s - lag < NCH:
                f(s - lag)


def part(a, c, k=None):
    first, n = (c * CT, CT) if k is None else (c * CT + k, 1)
    return a[:, first * C:(first + n) * C]


def layer_norm_stats(nc, stats, mv, vare, src, c, step, moments):
    for k in range(CT):
        last = nc.vector.bn_stats(stats[:, k, :], part(src, c, k))
    step(last)
    for k in range(CT):
        last = nc.vector.bn_aggr(mv[:, k, :], stats[:, k, :])
    step(last)
    nc.vector.tensor_scalar(vare[:, :], mv[:, :, 1], EPS, None, ALU.add).then_inc(moments, 1)


def load_stack(eng, b, n, qs, ks, stacked, q_dram, k_dram, pairs=range(PARTS * PARTS)):
    for c in pairs:
        rows = slice(c * HD, (c + 1) * HD)
        for dst, dram, r in ((qs[b], q_dram, c // PARTS), (ks[b], k_dram, c % PARTS)):
            eng.dma_start(dst[rows, :, :], dram[bass.ds(n, 1), r].rearrange("a (h d) n -> d (a h) n", d=HD)
                          ).then_inc(stacked[b], 16)


def load_values(eng, b, n, values, v_ones, values_here):
    wide = 2 * NH * (HD + 1)
    eng.dma_start(values[b][:, :], v_ones[:, bass.ds(n * wide, wide)]).then_inc(values_here[b], 16)


def project(nc, x, y, const, y_dram, gathered, v_ones, q_dram, k_dram, places):
    CHUNK_BATCHES = CT * P // SEQ
    with ExitStack() as stack:
        def sb(name, shape, dt=FP32, n=2):
            return [stack.enter_context(nc.sbuf_tensor(f"p_{name}{p}", shape, dt)) for p in range(n)]

        def banks(name):
            return [stack.enter_context(nc.psum_tensor(f"p_{name}{p}", [P, CT * P], FP32)) for p in range(2)]

        def sem(name):
            return stack.enter_context(nc.semaphore("p_" + name))

        stats, mv = sb("stats", [P, CT, 6]), sb("mv", [P, CT, 2])
        vare, rstd = sb("vare", [P, CT]), sb("rstd", [P, CT])
        fresh = sb("fresh", [P, CT * C])
        xnT = sb("xnT", [P, CT * P])
        rest = {s: sb("rest_" + s, [P, CT * P]) for s in "qk"}
        split = {s: sb("split_" + s, [P, PARTS, CT * P], BF16, 3) for s in "qk"}
        xnT_bank, v_bank = banks("xnT_bank"), banks("v_bank")
        qk_bank = {s: banks("bank_" + s) for s in "qk"}
        moments, rstd_ready, dve_step = sem("moments"), sem("rstd"), sem("dve_step")
        xn_ready, xnT_psum, xnT_sbuf = sem("xn_ready"), sem("xnT_psum"), sem("xnT_sbuf")
        qk_psum, part0_ready, rest_ready, part1_ready, split_ready = (
            sem(n) for n in ("qk_psum", "part0", "rest", "part1", "split_ready"))
        kept = [sem(f"kept{p}") for p in range(3)]
        v_psum, v_sbuf, ones_set = sem("v_psum"), sem("v_sbuf"), sem("ones_set")
        block = stack.enter_context(nc.Block())

        @block.gpsimd
        def _(pool):
            nc.gpsimd.memset(v_ones[:, :, HD:HD + 1], 1.0).then_inc(ones_set, 1)

            def gather(c):
                for t in range(c * CT, (c + 1) * CT):
                    nc.gpsimd.indirect_dma_start(
                        out=y[:, t, :], out_offset=None, in_=y_dram[:, :],
                        in_offset=bass.IndirectOffsetOnAxis(ap=const["slot"][:, t:t + 1], axis=0)
                    ).then_inc(gathered[c], 16)

            def power(c):
                pool.wait_ge(moments, c + 1)
                nc.gpsimd.tensor_tensor(rstd[c % 2][:, :], vare[c % 2][:, :], const["minus_half"][:, 0:CT],
                                        ALU.pow).then_inc(rstd_ready, 1)

            staged(((gather, 0), (power, 2)))

        @block.vector
        def _(dve):
            def add_and_norm(c):
                step = Steps(dve, dve_step, c, 3)
                dve.wait_ge(gathered[c], 16 * CT)
                step(nc.vector.tensor_tensor(part(x, c), part(x, c),
                                             y[:, c * CT:(c + 1) * CT, :].rearrange("p t c -> p (t c)"), ALU.add))
                layer_norm_stats(nc, stats[c % 2], mv[c % 2], vare[c % 2], x, c, step, moments)
                step.end()

            def xn_of(c):
                dve.wait_ge(rstd_ready, c + 1)
                if c >= 2:
                    dve.wait_ge(xnT_psum, c - 1)
                for k in range(CT):
                    last = nc.vector.tensor_scalar(fresh[c % 2][:, k * C:(k + 1) * C], part(x, c, k),
                                                   mv[c % 2][:, k, 0:1], rstd[c % 2][:, k:k + 1],
                                                   ALU.subtract, ALU.mult)
                last.then_inc(xn_ready, 1)

            def rest_of(c):
                for n, s in enumerate("qk"):
                    dve.wait_ge(part0_ready, 2 * c + 1 + n)
                    nc.vector.tensor_tensor(rest[s][c % 2][:, :], qk_bank[s][c % 2][:, :], split[s][c % 3][:, 0, :],
                                            ALU.subtract).then_inc(rest_ready, 1)

            def part2_of(c):
                for n, s in enumerate("qk"):
                    dve.wait_ge(part1_ready, 2 * c + 1 + n)
                    nc.vector.tensor_tensor(split[s][c % 3][:, 2, :], rest[s][c % 2][:, :], split[s][c % 3][:, 1, :],
                                            ALU.subtract).then_inc(split_ready, 1)

            def keep_values(c):
                dve.wait_ge(v_psum, c + 1)
                dve.wait_ge(ones_set, 1)
                nc.vector.tensor_copy(v_ones[:, c * CT * NH:(c + 1) * CT * NH, 0:HD],
                                      v_bank[c % 2][:, :].rearrange("p (g d) -> p g d", d=HD)).then_inc(v_sbuf, 1)

            staged(((rest_of, 3), (add_and_norm, 0), (xn_of, 1), (keep_values, 2), (part2_of, 3)))

        @block.scalar
        def _(act):
            def part1_of(c):
                for n, s in enumerate("qk"):
                    act.wait_ge(rest_ready, 2 * c + 1 + n)
                    nc.scalar.copy(split[s][c % 3][:, 1, :], rest[s][c % 2][:, :]).then_inc(part1_ready, 1)

            def xn_turned(c):
                act.wait_ge(xnT_psum, c + 1)
                if c >= 2:
                    act.wait_ge(v_psum, c - 1)
                nc.scalar.copy(xnT[c % 2][:, :], xnT_bank[c % 2][:, :]).then_inc(xnT_sbuf, 1)

            def part0_of(c):
                for n, s in enumerate("qk"):
                    act.wait_ge(qk_psum, 2 * c + 1 + n)
                    if c >= 3:
                        act.wait_ge(kept[c % 3], 2 * 16 * CHUNK_BATCHES * (c // 3))
                    nc.scalar.copy(split[s][c % 3][:, 0, :], qk_bank[s][c % 2][:, :]).then_inc(part0_ready, 1)

            staged(((part1_of, 3), (xn_turned, 1), (part0_of, 1)))

        @block.sync
        def _(sp):
            for c in range(NCH):
                for n, (s, dram) in enumerate((("q", q_dram), ("k", k_dram))):
                    sp.wait_ge(split_ready, 2 * c + 1 + n)
                    for b in range(CHUNK_BATCHES):
                        sp.dma_start(dram[c * CHUNK_BATCHES + b].rearrange("r p n -> p r n"),
                                     split[s][c % 3][:, :, b * SEQ:(b + 1) * SEQ]).then_inc(kept[c % 3], 16)
                if c == 1:
                    sp.wait_ge(kept[0], 2 * 16 * CHUNK_BATCHES)
                    sp.wait_ge(v_sbuf, 1)
                    for b in range(2):
                        load_values(sp, b, b, places["values"], places["v_flat"], places["values_here"])
                if 1 <= c <= 2 * PARTS:
                    b, first = divmod((c - 1) * PARTS, PARTS * PARTS)
                    load_stack(sp, b, b, places["qs"], places["ks"], places["stacked"], q_dram, k_dram,
                               range(first, first + PARTS))
            for p in range(3):
                sp.wait_ge(kept[p], 2 * 16 * CHUNK_BATCHES * len(range(p, NCH, 3)))

        @block.tensor
        def _(pe):
            def turn(c):
                pe.wait_ge(xn_ready, c + 1)
                if c >= 2:
                    pe.wait_ge(xnT_sbuf, c - 1)
                for k in range(CT):
                    last = nc.tensor.transpose(xnT_bank[c % 2][:, k * P:(k + 1) * P], fresh[c % 2][:, k * C:(k + 1) * C],
                                               const["ident"][:, :])
                last.then_inc(xnT_psum, 1)

            def products(c):
                pe.wait_ge(xnT_sbuf, c + 1)
                for n, s in enumerate("qk"):
                    if c >= 2:
                        pe.wait_ge(rest_ready, 2 * (c - 2) + 1 + n)
                    nc.tensor.matmul(qk_bank[s][c % 2][:, :], const["w" + s][:, :], xnT[c % 2][:, :],
                                     start=True, stop=True).then_inc(qk_psum, 1)
                if c >= 2:
                    pe.wait_ge(v_sbuf, c - 1)
                for k in range(CT):
                    last = nc.tensor.matmul(v_bank[c % 2][:, k * C:(k + 1) * C], xnT[c % 2][:, k * P:(k + 1) * P],
                                            const["wv"][:, :], start=True, stop=True)
                last.then_inc(v_psum, 1)

            staged(((turn, 1), (products, 1)))


def attend(nc, const, v_ones, table, q_dram, k_dram, places, ctx_out):
    GAP = 32
    PER = P // GAP
    W = 4
    UNIT = 8 * P
    per_batch = [(0, 8 * g, 8) for g in range(2)] + [(1, 4 * g, 4) for g in range(4)]
    UNITS = [(b, tile, head, heads) for b in range(2) for tile, head, heads in per_batch]
    NU = len(UNITS)
    TOTAL = NU * BATCH // 2
    with ExitStack() as stack:
        def sb(name, shape, dt=FP32):
            return stack.enter_context(nc.sbuf_tensor("t_" + name, shape, dt))

        def bank(name, n=1):
            return stack.enter_context(nc.psum_tensor("t_" + name, [P, 512 * n], FP32))

        def sem(name):
            return stack.enter_context(nc.semaphore("t_" + name))

        qs, ks, values = places["qs"], places["ks"], places["values"]
        stacked, values_here = places["stacked"], places["values_here"]
        relus = [sb(f"relu{p}", [P, UNIT]) for p in range(2)]
        weighted = [sb(f"weighted{p}", [P, UNIT]) for p in range(W)]
        tops = [sb(f"top{p}", [P, 8]) for p in range(W)]
        gate = sb("gate", [P, W])
        ctxT = [sb(f"ctxT{p}", [P, NH // PER * P]) for p in range(2)]
        probs = [sb(f"probs{p}", [P, UNIT]) for p in range(2)]
        recs = [sb(f"rec{p}", [P, NH]) for p in range(2)]
        score_banks = [bank(f"score{p}", 2) for p in range(2)]
        turned_bank = [bank(f"turned{p}") for p in range(2)]
        ctxT_bank, ctx_bank = bank("ctxT_bank"), bank("ctx_bank")
        scored, relu_done, weighted_done, shifted, turned, exped, averaged = (sem(n) for n in (
            "scored", "relu_done", "weighted_done", "shifted", "turned", "exped", "averaged"))
        bank_blank, ctxT_sbuf, turned_back, rec_done, ctx_done = (sem(n) for n in (
            "bank_blank", "ctxT_sbuf", "turned_back", "rec_done", "ctx_done"))
        block = stack.enter_context(nc.Block())

        def in_steps(eng, stages):
            lags = max(lag for _, lag in stages)
            for s in range(NU):
                for f, lag in stages:
                    if s >= lag:
                        f(s - lag, s - lag, 0)
            with eng.Fori(1, BATCH // 2) as i:
                for s in range(NU):
                    for f, lag in stages:
                        f(i * NU + (s - lag), (s - lag) % NU, i if s >= lag else i - 1)
            for s in range(TOTAL, TOTAL + lags):
                for f, lag in stages:
                    if s - lag < TOTAL:
                        f(s - lag, (s - lag) % NU, BATCH // 2 - 1)

        def first(g, n):
            return isinstance(g, int) and g < n

        group = [2 * b + tile for b, tile, _, _ in UNITS]
        ends = [u + 1 == NU or group[u + 1] != group[u] for u in range(NU)]
        begins = [u == 0 or group[u - 1] != group[u] for u in range(NU)]

        @block.sync
        def _(sp):
            with nc.sync.Fori(1, BATCH // 2) as i:
                for b in range(2):
                    sp.wait_ge(scored, i * NU + (NU // 2) * (b - 1))
                    load_stack(sp, b, i * 2 + b, qs, ks, stacked, q_dram, k_dram)
                    sp.wait_ge(averaged, i * NU + (NU // 2) * (b - 1))
                    load_values(sp, b, i * 2 + b, values, v_ones, values_here)

        @block.tensor
        def _(pe):
            def scores(g, u, pair):
                b, tile, head, heads = UNITS[u]
                keys = (tile + 1) * P
                out = score_banks[u % 2]
                if u % (NU // 2) == 0:
                    pe.wait_ge(stacked[b], (pair + 1) * (16 * 2 * PARTS * PARTS))
                if not first(g, 2):
                    pe.wait_ge(relu_done, g - 1)
                for half in range(2):
                    per = heads // 2
                    own = out[:, half * 512:(half + 1) * 512].rearrange("p (h k) -> p h k", h=per)
                    nc.tensor.matmul(own[:, :, keys - P:keys], const["ident16"][:, :],
                                     const["after"][:, :].unsqueeze(1).broadcast_to((P, per, P)),
                                     start=True, stop=False, skip_group_check=True)
                    for k in range(per):
                        h = head + half * per + k
                        last = nc.tensor.matmul(own[:, k, :], qs[b][:, h, tile * P:(tile + 1) * P],
                                                ks[b][:, h, 0:keys], start=False, stop=True, skip_group_check=True)
                last.then_inc(scored, 1)

            def turn(g, u, pair):
                pe.wait_ge(shifted, g + 1)
                for half in range(2):
                    if not first(g, 1):
                        pe.wait_ge(exped, g * 2 + (half - 1))
                    for j in range(4):
                        last = nc.tensor.transpose(turned_bank[half][:, j * P:(j + 1) * P],
                                                   weighted[u % W][:, (half * 4 + j) * P:(half * 4 + j + 1) * P],
                                                   const["ident"][:, :])
                    last.then_inc(turned, 1)

            def average(g, u, pair):
                b, tile, head, heads = UNITS[u]
                blocks = tile + 1
                if u % (NU // 2) == 0:
                    pe.wait_ge(values_here[b], (pair + 1) * 16)
                if first(g, 1):
                    pe.wait_ge(bank_blank, 1)
                elif begins[u]:
                    pe.wait_ge(ctxT_sbuf, pair * 4 + group[u])
                pe.wait_ge(exped, g * 2 + 2)
                for quad in range(heads // PER):
                    for j in range(blocks):
                        for k in range(PER):
                            h = head + quad * PER + k
                            n = (quad * PER + k) * blocks + j
                            last = nc.tensor.matmul(
                                ctxT_bank[k * GAP:k * GAP + HD + 1, h // PER * P:(h // PER + 1) * P],
                                values[b][:, (j * NH + h) * (HD + 1):(j * NH + h + 1) * (HD + 1)],
                                probs[u % 2][:, n * P:(n + 1) * P], start=(j == 0), stop=(j == blocks - 1),
                                skip_group_check=True)
                last.then_inc(averaged, 1)

            def turn_back(g, u, pair):
                if not ends[u]:
                    return
                done = pair * 4 + group[u]
                pe.wait_ge(ctxT_sbuf, done + 1)
                if not first(done, 1):
                    pe.wait_ge(ctx_done, done)
                for n in range(NH // PER):
                    last = nc.tensor.transpose(ctx_bank[:, n * P:(n + 1) * P], ctxT[group[u] % 2][:, n * P:(n + 1) * P],
                                               const["ident"][:, :])
                last.then_inc(turned_back, 1)

            in_steps(nc.tensor, ((scores, 0), (turn, 4), (average, 5), (turn_back, 6)))

        @block.vector
        def _(dve):
            def weigh(g, u, pair):
                b, tile, head, heads = UNITS[u]
                keys = (tile + 1) * P
                dve.wait_ge(relu_done, g + 1)
                if not first(g, W):
                    dve.wait_ge(turned, (g - W) * 2 + 2)
                nc.vector.memset(gate[:, u % W:u % W + 1], 0.0)
                for k in range(heads):
                    own = slice(k * keys, (k + 1) * keys)
                    last = nc.vector.tensor_tensor_reduce(
                        out=weighted[u % W][:, own], in0=relus[u % 2][:, own], in1=table[:, head + k, SEQ - keys:SEQ],
                        scale=1.0, scalar=0.0, op0=ALU.mult, op1=ALU.max, accum_out=tops[u % W][:, k:k + 1])
                last.then_inc(weighted_done, 1)

            def divide(g, u, pair):
                if not ends[u]:
                    return
                done = pair * 4 + group[u]
                ctx = ctx_bank[:, :].rearrange("p (h d) -> p h d", d=GAP)
                rec = recs[group[u] % 2]
                dve.wait_ge(turned_back, done + 1)
                nc.vector.reciprocal(rec[:, :], ctx[:, :, HD]).then_inc(rec_done, 1)
                dve.wait_ge(rec_done, done + 1)
                nc.vector.tensor_tensor(ctx_out[:, bass.ds(done * C, C)].rearrange("p (h d) -> p h d", h=NH),
                                        ctx[:, :, 0:HD], rec[:, :].unsqueeze(2).broadcast_to((P, NH, HD)),
                                        ALU.mult).then_inc(ctx_done, 1)

            nc.vector.memset(ctxT_bank[:, :], 0.0).then_inc(bank_blank, 1)
            in_steps(nc.vector, ((weigh, 0), (divide, 7)))

        @block.gpsimd
        def _(pool):
            def shift(g, u, pair):
                b, tile, head, heads = UNITS[u]
                view = weighted[u % W][:, :].rearrange("p (h k) -> p h k", h=heads)
                pool.wait_ge(weighted_done, g + 1)
                nc.gpsimd.tensor_tensor(view, view, tops[u % W][:, 0:heads].unsqueeze(2).broadcast_to(
                    (P, heads, (tile + 1) * P)), ALU.subtract).then_inc(shifted, 1)

            in_steps(nc.gpsimd, ((shift, 0),))

        @block.scalar
        def _(act):
            def relu(g, u, pair):
                act.wait_ge(scored, g + 1)
                if not first(g, 2):
                    act.wait_ge(weighted_done, g - 1)
                nc.scalar.activation(relus[u % 2][:, :], score_banks[u % 2][:, :], ACT.Relu).then_inc(relu_done, 1)

            def exp(g, u, pair):
                if not first(g, 2):
                    act.wait_ge(averaged, g - 1)
                for half in range(2):
                    act.wait_ge(turned, g * 2 + (half + 1))
                    nc.scalar.activation(probs[u % 2][:, half * 512:(half + 1) * 512], turned_bank[half][:, :],
                                         ACT.Exp).then_inc(exped, 1)

            def keep_ctxT(g, u, pair):
                if not ends[u]:
                    return
                done = pair * 4 + group[u]
                act.wait_ge(averaged, g + 1)
                if not first(done, 2):
                    act.wait_ge(turned_back, done - 1)
                nc.scalar.copy(ctxT[group[u] % 2][:, :], ctxT_bank[:, :]).then_inc(ctxT_sbuf, 1)

            in_steps(nc.scalar, ((relu, 0), (exp, 4), (keep_ctxT, 5)))


def attention_out(nc, x, ctx, kept_xn, w, const, logits_bank):
    with ExitStack() as stack:
        def sb(name, shape, dt=FP32):
            return [stack.enter_context(nc.sbuf_tensor(f"o_{name}{p}", shape, dt)) for p in range(2)]

        def banks(name):
            return [stack.enter_context(nc.psum_tensor(f"o_{name}{p}", [P, CT * P], FP32)) for p in range(2)]

        def sem(name):
            return stack.enter_context(nc.semaphore("o_" + name))

        stats, mv = sb("stats", [P, CT, 6]), sb("mv", [P, CT, 2])
        vare, rstd = sb("vare", [P, CT]), sb("rstd", [P, CT])
        ctxT, xnT = sb("ctxT", [P, CT * P]), sb("xnT", [P, CT * P])
        ctxT_bank, out_bank, xnT_bank = banks("ctxT_bank"), banks("out_bank"), banks("xnT_bank")
        moments, rstd_ready, dve_step, x_plus = sem("moments"), sem("rstd"), sem("dve_step"), sem("x_plus")
        ctxT_psum, ctxT_sbuf, out_psum = sem("ctxT_psum"), sem("ctxT_sbuf"), sem("out_psum")
        xn_ready, xnT_psum, xnT_sbuf, logits_psum = sem("xn_ready"), sem("xnT_psum"), sem("xnT_sbuf"), sem("logits")
        block = stack.enter_context(nc.Block())

        @block.vector
        def _(dve):
            def add_and_norm(c):
                step = Steps(dve, dve_step, c, 3)
                dve.wait_ge(x_plus, c + 1)
                dve.wait_ge(out_psum, c + 1)
                step(nc.vector.tensor_tensor(part(x, c), out_bank[c % 2][:, :], part(x, c), ALU.add))
                layer_norm_stats(nc, stats[c % 2], mv[c % 2], vare[c % 2], x, c, step, moments)
                step.end()

            def xn_of(c):
                dve.wait_ge(rstd_ready, c + 1)
                for k in range(CT):
                    last = nc.vector.tensor_scalar(part(kept_xn, c, k), part(x, c, k), mv[c % 2][:, k, 0:1],
                                                   rstd[c % 2][:, k:k + 1], ALU.subtract, ALU.mult)
                last.then_inc(xn_ready, 1)

            staged(((add_and_norm, 1), (xn_of, 2)))

        @block.gpsimd
        def _(pool):
            def add_bo(c):
                xc = part(x, c).rearrange("p (t n) -> p t n", t=CT)
                nc.gpsimd.tensor_tensor(xc, xc, const["bo"][:, :].unsqueeze(1).broadcast_to((P, CT, C)),
                                        ALU.add).then_inc(x_plus, 1)

            def power(c):
                pool.wait_ge(moments, c + 1)
                nc.gpsimd.tensor_tensor(rstd[c % 2][:, :], vare[c % 2][:, :], const["minus_half"][:, 0:CT],
                                        ALU.pow).then_inc(rstd_ready, 1)

            staged(((add_bo, 0), (power, 1)))

        @block.scalar
        def _(act):
            def ctx_turned(c):
                act.wait_ge(ctxT_psum, c + 1)
                if c >= 2:
                    act.wait_ge(out_psum, c - 1)
                nc.scalar.copy(ctxT[c % 2][:, :], ctxT_bank[c % 2][:, :]).then_inc(ctxT_sbuf, 1)

            def xn_turned(c):
                act.wait_ge(xnT_psum, c + 1)
                if c >= 2:
                    act.wait_ge(logits_psum, c - 1)
                nc.scalar.copy(xnT[c % 2][:, :], xnT_bank[c % 2][:, :]).then_inc(xnT_sbuf, 1)

            staged(((ctx_turned, 0), (xn_turned, 4)))

        @block.tensor
        def _(pe):
            def turn_ctx(c):
                if c >= 2:
                    pe.wait_ge(ctxT_sbuf, c - 1)
                for k in range(CT):
                    last = nc.tensor.transpose(ctxT_bank[c % 2][:, k * P:(k + 1) * P], part(ctx, c, k),
                                               const["ident"][:, :])
                last.then_inc(ctxT_psum, 1)

            def out(c):
                pe.wait_ge(ctxT_sbuf, c + 1)
                if c >= 2:
                    pe.wait_ge(dve_step, 3 * (c - 2) + 1)
                for k in range(CT):
                    last = nc.tensor.matmul(out_bank[c % 2][:, k * C:(k + 1) * C], ctxT[c % 2][:, k * P:(k + 1) * P],
                                            const["wo"][:, :], start=True, stop=True)
                last.then_inc(out_psum, 1)

            def turn_xn(c):
                pe.wait_ge(xn_ready, c + 1)
                if c >= 2:
                    pe.wait_ge(xnT_sbuf, c - 1)
                for k in range(CT):
                    last = nc.tensor.transpose(xnT_bank[c % 2][:, k * P:(k + 1) * P], part(kept_xn, c, k),
                                               const["ident"][:, :])
                last.then_inc(xnT_psum, 1)

            def logits(c):
                pe.wait_ge(xnT_sbuf, c + 1)
                for k in range(CT):
                    t = c * CT + k
                    last = nc.tensor.matmul(logits_bank[:, t * NE:(t + 1) * NE], xnT[c % 2][:, k * P:(k + 1) * P],
                                            w["wg"][:, :], start=True, stop=True)
                last.then_inc(logits_psum, 1)

            staged(((turn_ctx, 0), (turn_xn, 4), (out, 1), (logits, 4)))


INPUTS = ["L0_attn_a_x", "L0_attn_a_w1", "L0_attn_a_b1", "L0_attn_a_w2", "L0_attn_a_b2", "L0_attn_a_gamma1",
          "L0_attn_a_beta1", "L0_attn_a_gamma2", "L0_attn_a_beta2", "L0_attn_b_Wq", "L0_attn_b_Wk", "L0_attn_b_Wv",
          "L0_attn_b_Wo", "L0_attn_b_bo", "L0_attn_b_w", "L0_attn_b_v", "L0_ffn_W1", "L0_ffn_W2", "L0_ffn_Wg",
          "L0_ffn_bg"]


def program(nc, ins, out):
    slots_dram = nc.dram_tensor("slots", [SLOT_TILES * P, C], FP32, kind="Internal").ap()
    y_dram = nc.dram_tensor("expert_out", [SLOT_TILES * P, C], FP32, kind="Internal").ap()
    q_dram = nc.dram_tensor("query_parts", [BATCH, PARTS, P, SEQ], BF16, kind="Internal").ap()
    k_dram = nc.dram_tensor("key_parts", [BATCH, PARTS, P, SEQ], BF16, kind="Internal").ap()
    with ExitStack() as stack:
        def sb(name, shape, dt=FP32):
            return stack.enter_context(nc.sbuf_tensor(name, shape, dt))

        x = sb("x", [P, NT * C])
        w = dict(w1=sb("w1", [P, NE * HID]), w2=sb("w2", [P, NE * HID]), wg=sb("wg", [P, NE]))
        const = dict(
            ident=sb("ident", [P, P]), before=sb("before", [P, P], BF16), ones=sb("ones", [P, P], BF16),
            zero=sb("zero", [P, NE * NT]), order=sb("order", [P, NE]), tileno=sb("tileno", [P, SLOT_TILES]),
            minus_half=sb("minus_half", [P, 8]), half_pi=sb("half_pi", [P, 1]),
            slot=sb("slot", [P, NT], U32), tile_expert=sb("tile_expert", [P, SLOT_TILES], I32),
            ident16=sb("ident16", [P, P], BF16), after=sb("after", [P, P], BF16),
            wq=sb("wq", [P, C]), wk=sb("wk", [P, C]), wv=sb("wv", [P, C]), wo=sb("wo", [P, C]),
            w1T=sb("w1T", [NQ, FFN]), w2T=sb("w2T", [P, NFC, C]), b1=sb("b1", [P, NFC]))
        rows = {"b2": "L0_attn_a_b2", "gamma1": "L0_attn_a_gamma1", "beta1": "L0_attn_a_beta1",
                "gamma2": "L0_attn_a_gamma2", "beta2": "L0_attn_a_beta2", "bo": "L0_attn_b_bo", "bg": "L0_ffn_bg",
                "w": "L0_attn_b_w", "v": "L0_attn_b_v"}
        for name, source in rows.items():
            const[name] = sb(name, [P, ins[source].shape[0]])
        t2 = sb("t2", [P, NT * C])
        table = sb("table", [P, NH, SEQ])
        x_here = [stack.enter_context(nc.semaphore(f"x_here{c}")) for c in range(NCH)]
        gathered = [stack.enter_context(nc.semaphore(f"gathered{c}")) for c in range(NCH)]
        slots_empty = stack.enter_context(nc.semaphore("slots_empty"))
        big_here = stack.enter_context(nc.semaphore("big_here"))
        big_weights = (big_here, setup(nc, ins, x, table, w, const, rows, slots_dram, x_here, slots_empty, big_here))
        view = "p (t c) -> p t c"
        x3, t23 = x[:, :].rearrange(view, c=C), t2[:, :].rearrange(view, c=C)
        with ExitStack() as inner:
            const["logits_bank"] = inner.enter_context(nc.psum_tensor("logits_bank", [P, NT * NE], FP32))
            with ExitStack() as scratch:
                y, t1, xb = (scratch.enter_context(nc.sbuf_tensor(n, [P, NT * C], FP32)) for n in ("y", "t1", "xb"))
                block_a(nc, x, y, t1, t2, xb, w, const, x_here)
            route(nc, "r1_", t23, const, slots_dram, slots_empty, table, big_weights)
        expert_tiles(nc, "e1_", w, const, slots_dram, y_dram)
        with ExitStack() as inner:
            def inner_sb(name, shape, dt=FP32):
                return inner.enter_context(nc.sbuf_tensor(name, shape, dt))

            v_ones = inner_sb("v_ones", [P, NT * NH * (HD + 1)])
            places = dict(qs=[inner_sb(f"qs{b}", [STACK, NH, SEQ], BF16) for b in range(2)],
                          ks=[inner_sb(f"ks{b}", [STACK, NH, SEQ], BF16) for b in range(2)],
                          values=[inner_sb(f"values{b}", [P, 2 * NH * (HD + 1)]) for b in range(2)],
                          v_flat=v_ones,
                          stacked=[inner.enter_context(nc.semaphore(f"stacked{b}")) for b in range(2)],
                          values_here=[inner.enter_context(nc.semaphore(f"values_here{b}")) for b in range(2)])
            project(nc, x, t23, const, y_dram, gathered, v_ones[:, :].rearrange("p (g d) -> p g d", d=HD + 1),
                    q_dram, k_dram, places)
            attend(nc, const, v_ones, table, q_dram, k_dram, places, t2)
        with ExitStack() as inner:
            const["logits_bank"] = inner.enter_context(nc.psum_tensor("logits_bank2", [P, NT * NE], FP32))
            xn2 = inner.enter_context(nc.sbuf_tensor("xn2", [P, NT * C], FP32))
            attention_out(nc, x, t2, xn2, w, const, const["logits_bank"])
            route(nc, "r2_", xn2[:, :].rearrange(view, c=C), const, slots_dram, slots_empty)
        expert_tiles(nc, "e2_", w, const, slots_dram, y_dram)
        combine_and_store(nc, x3, t23, const, y_dram, gathered, out)


def setup(nc, ins, x, blank, w, const, rows, slots_dram, x_here, slots_empty, big_here):
    with ExitStack() as stack:
        loads = stack.enter_context(nc.semaphore("loads"))
        pool_made = stack.enter_context(nc.semaphore("pool_made"))
        blanked = stack.enter_context(nc.semaphore("blanked"))
        block = stack.enter_context(nc.Block())
        token_tiles = ins["L0_attn_a_x"].rearrange("b s c -> (b s) c").rearrange("(t p) c -> p t c", p=P)
        xt = x[:, :].rearrange("p (t c) -> p t c", c=C)
        big = 0

        @block.scalar
        def _(act):
            for c in range(NCH):
                tiles = slice(c * CT, (c + 1) * CT)
                act.dma_start(xt[:, tiles, :], token_tiles[:, tiles, :]).then_inc(x_here[c], 16)

        @block.sync
        def _(sp):
            nonlocal big
            small = [(const["w1T"][:, :], ins["L0_attn_a_w1"]),
                     (const["w2T"][:, :, :], ins["L0_attn_a_w2"].rearrange("(f p) c -> p f c", p=P)),
                     (const["b1"][:, :], ins["L0_attn_a_b1"]), (w["wg"][:, :], ins["L0_ffn_Wg"])]
            for name, source in rows.items():
                src = ins[source]
                small.append((const[name][:, :], src.unsqueeze(0).broadcast_to((P, src.shape[0]))))
            for dst, src in small:
                sp.dma_start(dst, src).then_inc(loads, 16)
            sp.wait_ge(blanked, 1)
            empty = slots_dram.rearrange("(t p) c -> p t c", p=P)
            src = blank[:, :, :].rearrange("p h k -> p (h k)").rearrange("p (t c) -> p t c", c=C)
            sp.dma_start(empty[:, 0:NT, :], src).then_inc(slots_empty, 16)
            sp.dma_start(empty[:, NT:, :], src[:, 0:SLOT_TILES - NT, :]).then_inc(slots_empty, 16)
            large = [(const["w" + s][:, :], ins["L0_attn_b_W" + s]) for s in "qkvo"]
            large.append((w["w1"][:, :].rearrange("p (e h) -> p e h", e=NE), ins["L0_ffn_W1"].rearrange("e d h -> d e h")))
            large.append((w["w2"][:, :].rearrange("p (e k c) -> p e k c", e=NE, k=NHC),
                          ins["L0_ffn_W2"].rearrange("e (k p) c -> p e k c", p=P)))
            for dst, src in large:
                sp.dma_start(dst, src).then_inc(big_here, 16)
            big = 16 * len(large)
            sp.wait_ge(loads, 16 * len(small))

        @block.vector
        def _(dve):
            nc.vector.memset(blank[:, :, :], 0.0).then_inc(blanked, 1)

        @block.gpsimd
        def _(pool):
            nc.gpsimd.memset(const["zero"][:, :], 0.0)
            nc.gpsimd.memset(const["ident"][:, :], 0.0)
            nc.gpsimd.memset(const["before"][:, :], 1.0)
            nc.gpsimd.memset(const["ident16"][:, :], 0.0)
            nc.gpsimd.memset(const["after"][:, :], 0.0)
            nc.gpsimd.memset(const["ones"][:, :], 1.0)
            nc.gpsimd.memset(const["minus_half"][:, :], -0.5)
            nc.gpsimd.memset(const["half_pi"][:, :], np.pi / 2)
            nc.gpsimd.iota(const["order"][:, :], pattern=[[-1, NE]], base=NE, channel_multiplier=0,
                           allow_small_or_imprecise_dtypes=True)
            nc.gpsimd.iota(const["tileno"][:, :], pattern=[[1, SLOT_TILES]], base=0, channel_multiplier=0,
                           allow_small_or_imprecise_dtypes=True).then_inc(pool_made, 1)
            pool.wait_ge(pool_made, 1)
            nc.gpsimd.affine_select(out=const["ident"][:, :], in_=const["ident"][:, :], compare_op=ALU.not_equal,
                                    fill=1.0, base=0, pattern=[[-1, P]], channel_multiplier=1)
            nc.gpsimd.affine_select(out=const["ident16"][:, :], in_=const["ident16"][:, :], compare_op=ALU.not_equal,
                                    fill=1.0, base=0, pattern=[[-1, P]], channel_multiplier=1)
            nc.gpsimd.affine_select(out=const["after"][:, :], in_=const["after"][:, :], compare_op=ALU.is_ge,
                                    fill=BIG, base=0, pattern=[[-1, P]], channel_multiplier=1)
            nc.gpsimd.affine_select(out=const["before"][:, :], in_=const["before"][:, :], compare_op=ALU.is_gt,
                                    fill=0.0, base=0, pattern=[[1, P]], channel_multiplier=-1).then_inc(pool_made, 1)
            pool.wait_ge(pool_made, 2)
    return big


def kernel(**inputs):
    import numpy as _np
    import concourse.bacc as _bacc
    from concourse import mybir as _mybir
    from concourse.bass_utils import run_bass_kernel_spmd as _run

    nc = _bacc.Bacc("TRN2", target_bir_lowering=False, num_devices=1)
    arrays, args = {}, {}
    for name in INPUTS:
        a = _np.asarray(inputs[name])
        if name in ("L0_attn_a_w1", "L0_attn_a_w2"):
            a = a.T
        if name == "L0_attn_a_b1":
            a = a.reshape(NFC, P).T
        a = _np.ascontiguousarray(a)
        arrays["in_" + name] = a
        args[name] = nc.dram_tensor("in_" + name, a.shape, _mybir.dt.from_np(a.dtype), kind="ExternalInput").ap()
    out = nc.dram_tensor("out_0", (TOK, C), _mybir.dt.float32, kind="ExternalOutput").ap()
    program(nc, args, out)
    r = _run(nc, [arrays], core_ids=[0])
    return _np.asarray(r.results[0]["out_0"]).reshape(BATCH, SEQ, C)
```

```python
from contextlib import ExitStack
import concourse.bass as bass
import concourse.mybir as mybir
import numpy as np

FP32 = mybir.dt.float32
BF16 = mybir.dt.bfloat16
I32 = mybir.dt.int32
U32 = mybir.dt.uint32
ALU = mybir.AluOpType
ACT = mybir.ActivationFunctionType
AX = mybir.AxisListType

P = 128
BATCH, SEQ, C = 16, 256, 128
TOK = BATCH * SEQ
NT = TOK // P
NE, HID = 8, 512
NHC = HID // P
SIX = 6
ROW = C + 1
SLOT_TILES = NT + NE - 1
EPS = 1e-5
ROUND = 1.5 * 2.0 ** 23
NQ, FFN = 16, 512
NFC = FFN // P
NH, HD = 16, 8
CT = 4
NCH = NT // CT
SMALL_LOADS = 13 * 16
BIG_LOADS = 6 * 16
SLOTS_EMPTY = 2 * 16


INV_2PI = 1.0 / (2.0 * np.pi)
TWO_PI = float(np.float32(2.0 * np.pi))
TWO_PI_HI = 6.28125
TWO_PI_LO = 2.0 * np.pi - TWO_PI_HI


class Steps:

    def __init__(self, eng, sem, run, per_run):
        self.eng, self.sem, self.base, self.per_run, self.n = eng, sem, run * per_run, per_run, 0

    def __call__(self, ins):
        self.n += 1
        ins.then_inc(self.sem, 1)
        self.eng.wait_ge(self.sem, self.base + self.n)

    def passed(self):
        self.n += 1
        self.eng.wait_ge(self.sem, self.base + self.n)

    def end(self):
        assert self.n == self.per_run


def block_a(nc, x, y, t1, t2, xb, w, const, x_here, loads, load_later, routed):
    N = CT * C
    with ExitStack() as stack:
        def sb(name, shape, dt=FP32):
            return stack.enter_context(nc.sbuf_tensor("a_" + name, shape, dt))

        def bank(name, shape):
            return stack.enter_context(nc.psum_tensor("a_" + name, shape, FP32))

        def sem(name):
            return stack.enter_context(nc.semaphore("a_" + name))

        NORMS = ("in", "mid", "out", "moe")
        stats = {n: sb("stats_" + n, [P, CT, 6]) for n in NORMS}
        mv = {n: sb("mv_" + n, [P, CT, 2]) for n in NORMS}
        vare = {n: sb("vare_" + n, [P, CT]) for n in NORMS}
        rstd = {n: [sb(f"rstd_{n}{b}", [P, CT]) for b in range(2)] for n in NORMS}
        minus_mean = {n: sb("minus_mean_" + n, [P, CT]) for n in NORMS}
        offset = {n: [sb(f"offset_{n}{b}", [P, CT]) for b in range(2)] for n in NORMS}
        ang = sb("ang", [P, CT * NQ])
        turns = sb("turns", [P, CT * NQ])
        qT = sb("qT", [NQ, CT * P])
        hT = sb("hT", [P, NFC, CT * P])
        xnT = sb("xnT", [P, CT * P])
        qT_bank = bank("qT_bank", [P, CT * P])
        h_bank = [bank(f"h_bank{b}", [P, CT * P]) for b in range(2)]
        ffn_bank = [bank(f"ffn_bank{b}", [P, CT * C]) for b in range(2)]
        xnT_bank = bank("xnT_bank", [P, CT * P])
        moments = {n: sem("moments_" + n) for n in NORMS}
        scales = {n: sem("scales_" + n) for n in NORMS}
        steps = {n: sem("steps_" + n) for n in ("in", "y", "mid", "x1", "q", "z2", "x", "act_y", "act_q")}
        y_ready = sem("y_ready")
        angle_y = sem("angle_y")
        cos_y = sem("cos_y")
        x1_ready = sem("x1_ready")
        angle_q = sem("angle_q")
        cos_q = sem("cos_q")
        x1b_ready = sem("x1b_ready")
        xb_ready = sem("xb_ready")
        q_ready = sem("q_ready")
        qT_psum = sem("qT_psum")
        qT_sbuf = sem("qT_sbuf")
        h_psum = sem("h_psum")
        h_sbuf = sem("h_sbuf")
        ffn_psum = sem("ffn_psum")
        normed_mid, normed_out, scaled_out = sem("normed_mid"), sem("normed_out"), sem("scaled_out")
        xn_ready = sem("xn_ready")
        xnT_psum = sem("xnT_psum")
        xnT_sbuf = sem("xnT_sbuf")
        logits_psum = sem("logits_psum")
        block = stack.enter_context(nc.Block())

        def part(a, c, k=None, cols=None):
            if k is None:
                return a[:, c * N:(c + 1) * N]
            return a[:, c * N + k * C:c * N + (k + 1) * C]

        def in_steps(stages):
            for s in range(NCH + max(lag for _, lag in stages)):
                for f, lag in stages:
                    if 0 <= s - lag < NCH:
                        f(s - lag)

        @block.sync
        def _(sp):
            load_later(sp)

        def tiles(a, c):
            return part(a, c).rearrange("p (t n) -> p t n", t=CT)

        def each_tile(name):
            return const[name][:, :].unsqueeze(1).broadcast_to((P, CT, C))

        @block.vector
        def _(dve):
            def stats_of(n, src, c, step):
                for k in range(CT):
                    last = nc.vector.bn_stats(stats[n][:, k, :], part(src, c, k))
                step(last)
                moments_of(n, step)

            def moments_of(n, step):
                for k in range(CT):
                    last = nc.vector.bn_aggr(mv[n][:, k, :], stats[n][:, k, :])
                step(last)
                nc.vector.tensor_scalar(minus_mean[n][:, :], mv[n][:, :, 0], -1.0, None, ALU.mult)
                nc.vector.tensor_scalar(vare[n][:, :], mv[n][:, :, 1], EPS, None, ALU.add).then_inc(moments[n], 1)

            def stats_in(c, k):
                if k == 0:
                    dve.wait_ge(x_here[c], 16)
                ins = nc.vector.bn_stats(stats["in"][:, k, :], part(x, c, k))
                if k == CT - 1:
                    ins.then_inc(steps["in"], 1)

            def norm_in(c):
                if c == 0:
                    for k in range(CT):
                        stats_in(0, k)
                dve.wait_ge(steps["in"], 2 * c + 1)
                moments_of("in", lambda last: (last.then_inc(steps["in"], 1), dve.wait_ge(steps["in"], 2 * c + 2)))

            def products_of_y(c):
                step = Steps(dve, steps["mid"], c, HD - 1 + 3)
                dve.wait_ge(cos_y, c + 1)
                heads = part(t1, c).rearrange("p (g d) -> p g d", d=HD)
                for d in range(1, HD):
                    nc.vector.tensor_tensor(heads[:, :, d], heads[:, :, d], heads[:, :, d - 1],
                                            ALU.mult).then_inc(steps["mid"], 1)
                    if d <= CT and c + 1 < NCH:
                        stats_in(c + 1, d - 1)
                    step.passed()
                step(nc.vector.tensor_tensor(part(t2, c), part(y, c), part(t1, c), ALU.add))
                stats_of("mid", t2, c, step)
                step.end()

            def x1_of(c):
                step = Steps(dve, steps["x1"], c, 4)
                if c == 0:
                    dve.wait_ge(loads, SMALL_LOADS)
                dve.wait_ge(normed_mid, c + 1)
                step(nc.vector.tensor_tensor(tiles(t1, c), tiles(t1, c), each_tile("gamma1"), ALU.mult))
                nc.vector.tensor_tensor(tiles(y, c), tiles(t1, c), each_tile("beta1"), ALU.add).then_inc(x1_ready, 1)
                dve.wait_ge(x1_ready, c + 1)
                if c >= 1:
                    dve.wait_ge(qT_psum, c)
                q_cols = part(y, c).rearrange("p (t n) -> p t n", t=CT)[:, :, 0:NQ]
                ang3 = ang[:, :].rearrange("p (t n) -> p t n", t=CT)
                turns3 = turns[:, :].rearrange("p (t n) -> p t n", t=CT)
                step(nc.vector.tensor_scalar(ang3, q_cols, INV_2PI, ROUND, ALU.mult, ALU.add))
                step(nc.vector.tensor_scalar(turns[:, :], ang[:, :], ROUND, None, ALU.subtract))
                step(nc.vector.scalar_tensor_tensor(out=ang3, in0=turns3, scalar=-TWO_PI_HI, in1=q_cols,
                                                    op0=ALU.mult, op1=ALU.add))
                nc.vector.scalar_tensor_tensor(out=turns[:, :], in0=turns[:, :], scalar=-TWO_PI_LO, in1=ang[:, :],
                                               op0=ALU.mult, op1=ALU.add).then_inc(angle_q, 1)
                step.end()

            def products_of_q(c):
                step = Steps(dve, steps["q"], c, 3 + NQ // 4 - 2)
                dve.wait_ge(cos_q, c + 1)
                q4 = ang[:, :].rearrange("p (g d) -> p g d", d=4)
                for d in range(1, 4):
                    step(nc.vector.tensor_tensor(q4[:, :, d], q4[:, :, d], q4[:, :, d - 1], ALU.mult))
                qt = ang[:, :].rearrange("p (t n) -> p t n", n=NQ)
                for g in range(1, NQ // 4):
                    last = nc.vector.tensor_tensor(qt[:, :, 4 * g:4 * g + 4], qt[:, :, 4 * g:4 * g + 4],
                                                   qt[:, :, 4 * g - 1:4 * g].broadcast_to((P, CT, 4)), ALU.mult)
                    if g < NQ // 4 - 1:
                        step(last)
                last.then_inc(q_ready, 1)
                step.end()

            def norm_out(c):
                step = Steps(dve, steps["z2"], c, 3)
                dve.wait_ge(ffn_psum, c + 1)
                dve.wait_ge(x1b_ready, c + 1)
                step(nc.vector.tensor_tensor(part(t2, c), ffn_bank[c % 2][:, :], part(t1, c), ALU.add))
                stats_of("out", t2, c, step)
                step.end()

            def x_of(c):
                step = Steps(dve, steps["x"], c, 3)
                dve.wait_ge(scaled_out, c + 1)
                dve.wait_ge(xb_ready, c + 1)
                step(nc.vector.tensor_tensor(part(x, c), part(y, c), part(xb, c), ALU.add))
                stats_of("moe", x, c, step)
                step.end()

            in_steps(((products_of_q, 2), (norm_out, 3), (products_of_y, 1), (norm_in, 0), (x_of, 3), (x1_of, 1)))

        @block.gpsimd
        def _(pool):
            def power(n):
                def stage(c):
                    pool.wait_ge(moments[n], c + 1)
                    nc.gpsimd.tensor_tensor(rstd[n][c % 2][:, :], vare[n][:, :], const["minus_half"][:, 0:CT],
                                            ALU.pow).then_inc(scales[n], 1)
                    pool.wait_ge(scales[n], 2 * c + 1)
                    nc.gpsimd.tensor_tensor(offset[n][c % 2][:, :], minus_mean[n][:, :], rstd[n][c % 2][:, :],
                                            ALU.mult).then_inc(scales[n], 1)
                return stage

            def x_and_beta2(c):
                pool.wait_ge(x_here[c], 16)
                if c == 0:
                    pool.wait_ge(loads, SMALL_LOADS)
                nc.gpsimd.tensor_tensor(tiles(xb, c), tiles(x, c), each_tile("beta2"), ALU.add).then_inc(xb_ready, 1)

            def x1_and_b2(c):
                pool.wait_ge(x1_ready, c + 1)
                nc.gpsimd.tensor_tensor(tiles(t1, c), tiles(y, c), each_tile("b2"), ALU.add).then_inc(x1b_ready, 1)

            def scale_out(c):
                pool.wait_ge(normed_out, c + 1)
                nc.gpsimd.tensor_tensor(tiles(y, c), tiles(y, c), each_tile("gamma2"), ALU.mult).then_inc(scaled_out, 1)

            def angles_of_y(c):
                step = Steps(pool, steps["y"], c, 2)
                pool.wait_ge(y_ready, c + 1)
                step(nc.gpsimd.tensor_scalar(part(t1, c), part(y, c), INV_2PI, ROUND, ALU.mult, ALU.add))
                step(nc.gpsimd.tensor_scalar(part(t2, c), part(t1, c), -ROUND, -TWO_PI, ALU.add, ALU.mult))
                nc.gpsimd.tensor_tensor(part(t1, c), part(t2, c), part(y, c), ALU.add).then_inc(angle_y, 1)
                step.end()

            number_tokens(nc, routed)
            in_steps(((power("out"), 3), (x_and_beta2, 0), (scale_out, 3), (power("mid"), 1), (power("in"), 0),
                      (power("moe"), 3), (angles_of_y, 0), (x1_and_b2, 1)))

        @block.scalar
        def _(act):
            def cosines_of_y(c):
                step = Steps(act, steps["act_y"], c, 1)
                act.wait_ge(angle_y, c + 1)
                step(nc.scalar.activation(part(t2, c), part(t1, c), ACT.Abs))
                nc.scalar.activation(part(t1, c), part(t2, c), ACT.Sin, bias=const["half_pi"][:, 0:1],
                                     scale=-1.0).then_inc(cos_y, 1)

            def cosines_of_q(c):
                step = Steps(act, steps["act_q"], c, 1)
                act.wait_ge(angle_q, c + 1)
                step(nc.scalar.activation(turns[:, :], turns[:, :], ACT.Abs))
                nc.scalar.activation(ang[:, :], turns[:, :], ACT.Sin, bias=const["half_pi"][:, 0:1],
                                     scale=-1.0).then_inc(cos_q, 1)

            def q_turned(c):
                act.wait_ge(qT_psum, c + 1)
                nc.scalar.copy(qT[:, :], qT_bank[0:NQ, :]).then_inc(qT_sbuf, 1)

            def hidden(*fs):
                def stage(c):
                    for f in fs:
                        if c == 0:
                            act.wait_ge(loads, SMALL_LOADS)
                        act.wait_ge(h_psum, c * NFC + f + 1)
                        nc.scalar.activation(hT[:, f, :], h_bank[f % 2][:, :], ACT.Relu,
                                             bias=const["b1"][:, f:f + 1]).then_inc(h_sbuf, 1)
                return stage

            def xn_turned(c):
                act.wait_ge(xnT_psum, c + 1)
                nc.scalar.copy(xnT[:, :], xnT_bank[:, :]).then_inc(xnT_sbuf, 1)

            def normed(n, dst, src, ready):
                def stage(c):
                    act.wait_ge(scales[n], 2 * c + 2)
                    for k in range(CT):
                        to = part(dst, c, k) if dst is not routed else routed[:, c * CT + k, 0:C]
                        last = nc.scalar.activation(to, part(src, c, k), ACT.Identity,
                                                    bias=offset[n][c % 2][:, k:k + 1], scale=rstd[n][c % 2][:, k:k + 1])
                    last.then_inc(ready, 1)
                return stage

            in_steps(((q_turned, 2), (cosines_of_y, 1), (xn_turned, 4), (hidden(0, 1), 2),
                      (normed("out", y, t2, normed_out), 3), (hidden(2), 2),
                      (normed("mid", t1, t2, normed_mid), 1), (hidden(3), 2), (normed("in", y, x, y_ready), 0),
                      (cosines_of_q, 1), (normed("moe", routed, x, xn_ready), 3)))

        @block.tensor
        def _(pe):
            def turn_q(c):
                pe.wait_ge(q_ready, c + 1)
                for k in range(CT):
                    last = nc.tensor.transpose(qT_bank[0:NQ, k * P:(k + 1) * P], ang[:, k * NQ:(k + 1) * NQ],
                                               const["ident"][:, :])
                last.then_inc(qT_psum, 1)

            def ffn(c):
                pe.wait_ge(qT_sbuf, c + 1)
                if c == 0:
                    pe.wait_ge(loads, SMALL_LOADS)
                for f in range(NFC):
                    if c * NFC + f >= 2:
                        pe.wait_ge(h_sbuf, c * NFC + f - 1)
                    nc.tensor.matmul(h_bank[f % 2][:, :], const["w1T"][:, f * P:(f + 1) * P], qT[:, :],
                                     start=True, stop=True).then_inc(h_psum, 1)
                if c >= 2:
                    pe.wait_ge(steps["z2"], 3 * (c - 2) + 1)
                for f in range(NFC):
                    if f == NFC - 1 and c >= 2:
                        logits(c - 2)
                    pe.wait_ge(h_sbuf, c * NFC + f + 1)
                    for k in range(CT):
                        last = nc.tensor.matmul(ffn_bank[c % 2][:, k * C:(k + 1) * C], hT[:, f, k * P:(k + 1) * P],
                                                const["w2T"][:, f, :], start=(f == 0 and k == 0), stop=(f == NFC - 1),
                                                skip_group_check=True)
                last.then_inc(ffn_psum, 1)

            def turn_xn(c):
                pe.wait_ge(xn_ready, c + 1)
                if c >= 1:
                    pe.wait_ge(xnT_sbuf, c)
                for k in range(CT):
                    last = nc.tensor.transpose(xnT_bank[:, k * P:(k + 1) * P], routed[:, c * CT + k, 0:C], const["ident"][:, :])
                last.then_inc(xnT_psum, 1)

            def logits(c):
                pe.wait_ge(xnT_sbuf, c + 1)
                for k in range(CT):
                    last = nc.tensor.matmul(const["logits_bank"][:, (c * CT + k) * NE:(c * CT + k + 1) * NE],
                                            xnT[:, k * P:(k + 1) * P], w["wg"][:, :], start=True, stop=True)
                last.then_inc(logits_psum, 1)

            def logits_alone(c):
                if c + 2 >= NCH:
                    logits(c)

            in_steps(((turn_q, 2), (turn_xn, 4), (ffn, 2), (logits_alone, 4)))


def number_tokens(nc, routed):
    nc.gpsimd.iota(routed[:, :, C:ROW], pattern=[[P, NT], [0, 1]], base=0, channel_multiplier=1,
                   allow_small_or_imprecise_dtypes=True)


def route(nc, tag, routed, const, slots_dram, slots_empty, table=None, big_here=None):
    with ExitStack() as stack:
        logits = stack.enter_context(nc.sbuf_tensor(tag + "logits", [P, NT, NE], FP32))
        best = stack.enter_context(nc.sbuf_tensor(tag + "best", [P, NT], FP32))
        isbest = stack.enter_context(nc.sbuf_tensor(tag + "isbest", [P, NT, NE], FP32))
        rankval = stack.enter_context(nc.sbuf_tensor(tag + "rankval", [P, NT, NE], FP32))
        onehot = stack.enter_context(nc.sbuf_tensor(tag + "onehot", [P, NE, NT], BF16))
        tot = stack.enter_context(nc.sbuf_tensor(tag + "tot", [P, NE, NT], FP32))
        cum = stack.enter_context(nc.sbuf_tensor(tag + "cum", [P, NE, NT], FP32))
        cnt = stack.enter_context(nc.sbuf_tensor(tag + "cnt", [P, NE], FP32))
        tiles_a = stack.enter_context(nc.sbuf_tensor(tag + "tiles_a", [P, NE], FP32))
        tiles_e = stack.enter_context(nc.sbuf_tensor(tag + "tiles_e", [P, NE], FP32))
        end_e = stack.enter_context(nc.sbuf_tensor(tag + "end_e", [P, NE], FP32))
        adj = stack.enter_context(nc.sbuf_tensor(tag + "adj", [P, NE], FP32))
        adj2 = stack.enter_context(nc.sbuf_tensor(tag + "adj2", [P, NE], FP32))
        pos = stack.enter_context(nc.sbuf_tensor(tag + "pos", [P, NE, NT], FP32))
        slotf = stack.enter_context(nc.sbuf_tensor(tag + "slotf", [P, NT], FP32))
        past = stack.enter_context(nc.sbuf_tensor(tag + "past", [P, SLOT_TILES, NE], FP32))
        tilef = stack.enter_context(nc.sbuf_tensor(tag + "tilef", [P, SLOT_TILES], FP32))
        tilee = stack.enter_context(nc.sbuf_tensor(tag + "tilee", [P, SLOT_TILES], FP32))
        words = [stack.enter_context(nc.sbuf_tensor(tag + f"words{b}", [P, SLOT_TILES - SIX + 1], FP32)) for b in range(2)]
        pR = stack.enter_context(nc.psum_tensor(tag + "pR", [P, 2, NE * NT], FP32))
        onehot_ready = stack.enter_context(nc.semaphore(tag + "onehot_ready"))
        counts_psum = stack.enter_context(nc.semaphore(tag + "counts_psum"))
        slots_ready = stack.enter_context(nc.semaphore(tag + "slots_ready"))
        scattered = stack.enter_context(nc.semaphore(tag + "scattered"))
        dve_step = stack.enter_context(nc.semaphore(tag + "dve_step"))
        if table is not None:
            dist = stack.enter_context(nc.sbuf_tensor("pt_dist", [P, SEQ], FP32))
            minus_w, ev, top = (stack.enter_context(nc.sbuf_tensor("pt_" + n, [P, NH], FP32))
                                for n in ("minus_w", "ev", "top"))
            grown = stack.enter_context(nc.sbuf_tensor("pt_grown", [P, NH, SEQ], FP32))
            dist_made, dist_ready, grown_made, grown_step, weights, masked = (
                stack.enter_context(nc.semaphore("pt_" + n))
                for n in ("dist_made", "dist_ready", "grown_made", "grown_step", "weights", "masked"))
        block = stack.enter_context(nc.Block())

        @block.vector
        def _(dve):
            done = [0]

            def step(ins):
                done[0] += 1
                ins.then_inc(dve_step, 1)
                dve.wait_ge(dve_step, done[0])

            step(nc.vector.tensor_tensor(logits[:, :, :], const["logits_bank"][:, :].rearrange("p (t e) -> p t e", e=NE),
                                         const["bg"][:, :].unsqueeze(1).broadcast_to((P, NT, NE)), ALU.add))
            step(nc.vector.tensor_reduce(best[:, :], logits[:, :, :], AX.X, ALU.max))
            step(nc.vector.tensor_tensor(isbest[:, :, :], logits[:, :, :],
                                         best[:, :].unsqueeze(2).broadcast_to((P, NT, NE)), ALU.is_equal))
            order = const["order"][:, :].unsqueeze(1).broadcast_to((P, NT, NE))
            step(nc.vector.tensor_tensor(rankval[:, :, :], isbest[:, :, :], order, ALU.mult))
            step(nc.vector.tensor_reduce(best[:, :], rankval[:, :, :], AX.X, ALU.max))
            nc.vector.tensor_tensor(onehot[:, :, :].rearrange("p e t -> p t e"), order,
                                    best[:, :].unsqueeze(2).broadcast_to((P, NT, NE)),
                                    ALU.is_equal).then_inc(onehot_ready, 1)
            if table is not None:
                nc.vector.tensor_scalar(minus_w[:, :], const["w"][:, :], -1.0, None, ALU.mult)
                dve.wait_ge(dist_made, 1)
                nc.vector.tensor_scalar(dist[:, :], dist[:, :], 0.0, None, ALU.max).then_inc(dist_ready, 1)
            dve.wait_ge(counts_psum, 1)
            step(nc.vector.tensor_copy(tot[:, :, :], pR[:, 1, :].rearrange("p (e t) -> p e t", e=NE)))
            flat = "p e t -> p (e t)"
            nc.vector.tensor_tensor_scan(cum[:, :, :].rearrange(flat), tot[:, :, :].rearrange(flat),
                                         const["zero"][:, 0:NE * NT], 0.0, ALU.add, ALU.add)
            step(nc.vector.tensor_reduce(cnt[:, :], tot[:, :, :], AX.X, ALU.add))
            step(nc.vector.tensor_scalar(tiles_a[:, :], cnt[:, :], 1.0 / P, (P - 1) / (2.0 * P), ALU.mult, ALU.add))
            step(nc.vector.tensor_scalar(tiles_e[:, :], tiles_a[:, :], ROUND, ROUND, ALU.add, ALU.subtract))
            step(nc.vector.tensor_tensor_scan(end_e[:, :], tiles_e[:, :], const["zero"][:, 0:NE], 0.0,
                                              ALU.add, ALU.add))
            step(nc.vector.tensor_tensor(adj[:, :], end_e[:, :], tiles_e[:, :], ALU.subtract))
            step(nc.vector.scalar_tensor_tensor(out=adj2[:, :], in0=adj[:, :], scalar=float(P), in1=tot[:, :, 0],
                                                op0=ALU.mult, op1=ALU.add))
            step(nc.vector.tensor_tensor(adj[:, :], adj2[:, :], cum[:, :, 0], ALU.subtract))
            step(nc.vector.tensor_tensor(pos[:, :, :], cum[:, :, :], tot[:, :, :], ALU.subtract))
            step(nc.vector.tensor_tensor(cum[:, :, :], pos[:, :, :], pR[:, 0, :].rearrange("p (e t) -> p e t", e=NE),
                                         ALU.add))
            step(nc.vector.tensor_tensor(pos[:, :, :], cum[:, :, :],
                                         adj[:, :].unsqueeze(2).broadcast_to((P, NE, NT)), ALU.add))
            step(nc.vector.tensor_tensor(cum[:, :, :], pos[:, :, :], onehot[:, :, :], ALU.mult))
            step(nc.vector.tensor_reduce(slotf[:, :], cum[:, :, :].rearrange("p e t -> p t e"), AX.X, ALU.add))
            nc.vector.tensor_copy(const["slot"][:, :], slotf[:, :]).then_inc(slots_ready, 1)
            step(nc.vector.tensor_tensor(past[:, :, :], end_e[:, :].unsqueeze(1).broadcast_to((P, SLOT_TILES, NE)),
                                         const["tileno"][:, :].unsqueeze(2).broadcast_to((P, SLOT_TILES, NE)),
                                         ALU.is_le))
            step(nc.vector.tensor_reduce(tilef[:, :], past[:, :, :], AX.X, ALU.add))
            step(nc.vector.tensor_scalar(tilee[:, :], tilef[:, :], float(NE - 1), None, ALU.min))
            step(nc.vector.tensor_copy(const["tile_expert"][:, :], tilee[:, :]))
            firsts = SLOT_TILES - SIX + 1
            for n in range(SIX - 2, -1, -1):
                word = tilee[:, SIX - 1:] if n == SIX - 2 else words[n % 2][:, :]
                to = const["six_experts"] if n == 0 else words[(n + 1) % 2]
                step(nc.vector.scalar_tensor_tensor(out=to[:, 0:firsts], in0=word, scalar=float(NE),
                                                    in1=tilee[:, n:n + firsts], op0=ALU.mult, op1=ALU.add))
            if table is not None:
                dve.wait_ge(grown_made, 1 + NH)
                nc.vector.tensor_scalar(top[:, :], ev[:, :], 1.0, float(1.0 / np.sqrt(HD)), ALU.add, ALU.mult)
                nc.vector.tensor_scalar(grown[:, :, :], grown[:, :, :], 1.0, None, ALU.add).then_inc(grown_step, 1)
                dve.wait_ge(grown_step, 1)
                nc.vector.reciprocal(grown[:, :, :], grown[:, :, :]).then_inc(grown_step, 1)
                dve.wait_ge(grown_step, 2)
                nc.vector.tensor_tensor(table[:, :, :], grown[:, :, :],
                                        top[:, :].unsqueeze(2).broadcast_to((P, NH, SEQ)), ALU.mult).then_inc(weights, 1)

        if table is not None:
            @block.scalar
            def _(act):
                nc.scalar.activation(ev[:, :], const["v"][:, :], ACT.Exp).then_inc(grown_made, 1)
                act.wait_ge(dist_ready, 1)
                for h in range(NH):
                    nc.scalar.activation(grown[:, h, :], dist[:, :], ACT.Exp, bias=const["v"][:, h:h + 1],
                                         scale=minus_w[:, h:h + 1]).then_inc(grown_made, 1)

            @block.sync
            def _(sp):
                sp.wait_ge(big_here, BIG_LOADS)

        @block.gpsimd
        def _(pool):
            if table is not None:
                nc.gpsimd.iota(dist[:, :], pattern=[[-1, SEQ]], base=P, channel_multiplier=1,
                               allow_small_or_imprecise_dtypes=True).then_inc(dist_made, 1)
            pool.wait_ge(slots_empty, SLOTS_EMPTY)
            pool.wait_ge(slots_ready, 1)
            for t in range(NT):
                nc.gpsimd.indirect_dma_start(
                    out=slots_dram[:, :], out_offset=bass.IndirectOffsetOnAxis(ap=const["slot"][:, t:t + 1], axis=0),
                    in_=routed[:, t, :], in_offset=None).then_inc(scattered, 16)
            if table is not None:
                pool.wait_ge(weights, 1)
                nc.gpsimd.affine_select(out=table[:, :, :], in_=table[:, :, :], compare_op=ALU.is_ge, fill=-1.0,
                                        base=P, pattern=[[0, NH], [-1, SEQ]], channel_multiplier=1).then_inc(masked, 1)
                pool.wait_ge(masked, 1)
            pool.wait_ge(scattered, 16 * NT)

        @block.tensor
        def _(pe):
            pe.wait_ge(onehot_ready, 1)
            oh = onehot[:, :, :].rearrange("p e t -> p (e t)")
            nc.tensor.matmul(pR[:, 0, :], const["before"][:, :], oh, start=True, stop=True)
            nc.tensor.matmul(pR[:, 1, :], const["ones"][:, :], oh, start=True, stop=True).then_inc(counts_psum, 1)


def expert_tiles(nc, tag, w, const, slots_dram, y_dram):
    U = 4
    with ExitStack() as stack:
        xt = stack.enter_context(nc.sbuf_tensor(tag + "xt", [P, U, ROW], FP32))
        gate = stack.enter_context(nc.sbuf_tensor(tag + "gate", [P, U], FP32))
        number = stack.enter_context(nc.sbuf_tensor(tag + "number", [P, U], U32))
        yt = stack.enter_context(nc.sbuf_tensor(tag + "yt", [P, U, C], FP32))
        xT = stack.enter_context(nc.sbuf_tensor(tag + "xT", [P, 2, P], FP32))
        hid = stack.enter_context(nc.sbuf_tensor(tag + "hid", [P, 2, HID], FP32))
        hidT = stack.enter_context(nc.sbuf_tensor(tag + "hidT", [P, 2, HID], FP32))
        xT_bank = [stack.enter_context(nc.psum_tensor(tag + f"xT_bank{b}", [P, 512], FP32)) for b in range(2)]
        hid_bank = [stack.enter_context(nc.psum_tensor(tag + f"hid_bank{b}", [P, HID], FP32)) for b in range(2)]
        hidT_bank = [stack.enter_context(nc.psum_tensor(tag + f"hidT_bank{b}", [P, HID], FP32)) for b in range(2)]
        y_bank = [stack.enter_context(nc.psum_tensor(tag + f"y_bank{b}", [P, 512], FP32)) for b in range(2)]
        loaded = [stack.enter_context(nc.semaphore(tag + f"loaded{u}")) for u in range(U)]
        stored = [stack.enter_context(nc.semaphore(tag + f"stored{u}")) for u in range(U)]
        xT_psum = stack.enter_context(nc.semaphore(tag + "xT_psum"))
        xT_sbuf = stack.enter_context(nc.semaphore(tag + "xT_sbuf"))
        hid_psum = stack.enter_context(nc.semaphore(tag + "hid_psum"))
        hid_sbuf = stack.enter_context(nc.semaphore(tag + "hid_sbuf"))
        hidT_psum = stack.enter_context(nc.semaphore(tag + "hidT_psum"))
        passed = stack.enter_context(nc.semaphore(tag + "passed"))
        hidT_sbuf = stack.enter_context(nc.semaphore(tag + "hidT_sbuf"))
        y_psum = stack.enter_context(nc.semaphore(tag + "y_psum"))
        y_sbuf = stack.enter_context(nc.semaphore(tag + "y_sbuf"))
        block = stack.enter_context(nc.Block())

        TURNS = SLOT_TILES // U
        FIRST = U + 3
        LOOPED = (SLOT_TILES - FIRST) // U * U

        def in_steps(eng, stages, begin=None):

            def one(s):
                for f, lag in stages:
                    if 0 <= s - lag < SLOT_TILES:
                        f(s - lag, (s - lag) % U, (s - lag) // U)

            for s in range(FIRST):
                one(s)
            with eng.Fori(0, LOOPED // U) as i:
                if begin is not None:
                    begin(i)
                for k in range(U):
                    for f, lag in stages:
                        j = FIRST + k - lag
                        f(i * U + j, j % U, i + j // U)
            for s in range(FIRST + LOOPED, SLOT_TILES + 3):
                one(s)

        def later(j, n):
            return not isinstance(j, int) or j >= n

        @block.sync
        def _(sp):
            for u in range(U):
                sp.dma_start(xt[:, u, :], slots_dram[u * P:(u + 1) * P, :]).then_inc(loaded[u], 16)

            def load_next(i, u):
                sp.wait_ge(xT_sbuf, i * U + (u + 2))
                sp.dma_start(xt[:, u, :], slots_dram[bass.ds(i * (U * P) + (U + u) * P, P), :]).then_inc(loaded[u], 16)

            with nc.sync.Fori(0, TURNS - 1) as i:
                for u in range(U):
                    load_next(i, u)
            for u in range(SLOT_TILES - TURNS * U):
                load_next(TURNS - 1, u)

        @block.scalar
        def _(act):
            def gelu(j, u, turn):
                act.wait_ge(hid_psum, j + 1)
                if later(j, 2):
                    act.wait_ge(hidT_psum, j - 1)
                nc.scalar.activation(hid[:, u % 2, :], hid_bank[u % 2][:, :], ACT.Gelu_apprx_tanh).then_inc(hid_sbuf, 1)

            def copy_y(j, u, turn):
                act.wait_ge(y_psum, j + 1)
                if later(j, U):
                    act.wait_ge(passed, j - (U - 1))
                    act.wait_ge(stored[u], turn * 16)
                nc.scalar.copy(yt[:, u, :], y_bank[u % 2][:, 0:C]).then_inc(y_sbuf, 1)

            in_steps(nc.scalar, ((gelu, 1), (copy_y, 3)))

        @block.gpsimd
        def _(pool):
            def store(i, u):
                pool.wait_ge(y_sbuf, i * U + (u + 1))
                nc.gpsimd.tensor_tensor(gate[:, u:u + 1], const["zero"][:, 0:1], const["zero"][:, 0:1],
                                        ALU.add).then_inc(passed, 1)
                nc.gpsimd.indirect_dma_start(
                    out=y_dram[:, :], out_offset=bass.IndirectOffsetOnAxis(ap=number[:, u:u + 1], axis=0),
                    in_=yt[:, u, :], in_offset=None).then_inc(stored[u], 16)

            with nc.gpsimd.Fori(0, TURNS) as i:
                for u in range(U):
                    store(i, u)
            for u in range(SLOT_TILES - TURNS * U):
                store(TURNS, u)
            for u in range(U):
                pool.wait_ge(stored[u], 16 * len(range(u, SLOT_TILES, U)))

        @block.vector
        def _(dve):
            def copy_x(j, u, turn):
                dve.wait_ge(xT_psum, j + 1)
                if later(j, 2):
                    dve.wait_ge(hid_psum, j - 1)
                nc.vector.tensor_copy(xT[:, u % 2, :], xT_bank[u % 2][:, 0:P]).then_inc(xT_sbuf, 1)

            def copy_number(j, u, turn):
                if later(j, U):
                    dve.wait_ge(stored[u], turn * 16)
                nc.vector.tensor_copy(number[:, u:u + 1], xt[:, u, C:ROW])

            def copy_hidden(j, u, turn):
                dve.wait_ge(hidT_psum, j + 1)
                if later(j, 2):
                    dve.wait_ge(y_psum, j - 1)
                nc.vector.tensor_copy(hidT[:, u % 2, :], hidT_bank[u % 2][:, :]).then_inc(hidT_sbuf, 1)

            in_steps(nc.vector, ((copy_number, 1), (copy_x, 0), (copy_hidden, 2)))

        @block.tensor
        def _(pe):
            experts = {}

            def load_experts(i):
                word = nc.tensor.value_load(const["six_experts"][0:1, bass.ds(i * U + (FIRST - 3), 1)],
                                            min_val=0, max_val=NE ** (U + 2) - 1)
                for n in range(U + 2):
                    experts[n] = (word >> (3 * n)) & (NE - 1)

            def expert(j, u):
                if isinstance(j, int):
                    return nc.tensor.value_load(const["tile_expert"][0:1, bass.ds(j, 1)], min_val=0, max_val=NE - 1)
                return experts[u]

            def turn_x(j, u, turn):
                pe.wait_ge(loaded[u], turn * 16 + 16)
                if later(j, 2):
                    pe.wait_ge(xT_sbuf, j - 1)
                nc.tensor.transpose(xT_bank[u % 2][:, 0:P], xt[:, u, 0:C], const["ident"][:, :]).then_inc(xT_psum, 1)

            def up(j, u, turn):
                e = expert(j, 2 + (u - (FIRST - 1)) % U)
                pe.wait_ge(xT_sbuf, j + 1)
                if later(j, 2):
                    pe.wait_ge(hid_sbuf, j - 1)
                nc.tensor.matmul(hid_bank[u % 2][:, :], xT[:, u % 2, :], w["w1"][:, bass.ds(e * HID, HID)],
                                 start=True, stop=True).then_inc(hid_psum, 1)

            def turn_hidden(j, u, turn):
                pe.wait_ge(hid_sbuf, j + 1)
                if later(j, 2):
                    pe.wait_ge(hidT_sbuf, j - 1)
                for k in range(NHC):
                    last = nc.tensor.transpose(hidT_bank[u % 2][:, k * P:(k + 1) * P],
                                               hid[:, u % 2, k * P:(k + 1) * P], const["ident"][:, :])
                last.then_inc(hidT_psum, 1)

            def down(j, u, turn):
                e = expert(j, (u - (FIRST - 3)) % U)
                pe.wait_ge(hidT_sbuf, j + 1)
                if later(j, 2):
                    pe.wait_ge(y_sbuf, j - 1)
                for k in range(NHC):
                    last = nc.tensor.matmul(y_bank[u % 2][:, 0:C], hidT[:, u % 2, k * P:(k + 1) * P],
                                            w["w2"][:, bass.ds(e * (NHC * C) + k * C, C)],
                                            start=(k == 0), stop=(k == NHC - 1))
                last.then_inc(y_psum, 1)

            in_steps(nc.tensor, ((turn_x, 0), (up, 1), (turn_hidden, 2), (down, 3)), load_experts)


def combine_and_store(nc, x, y, y_rows, outputs_here, out_rows):
    with ExitStack() as stack:
        added = stack.enter_context(nc.semaphore("c_added"))
        stored = stack.enter_context(nc.semaphore("c_stored"))
        block = stack.enter_context(nc.Block())

        @block.scalar
        def _(act):
            load_outputs(act, y, y_rows, outputs_here)

        @block.vector
        def _(dve):
            for c in range(NCH):
                tiles = slice(c * CT, (c + 1) * CT)
                dve.wait_ge(outputs_here[c], 2 * 16)
                nc.vector.tensor_tensor(x[:, tiles, :], x[:, tiles, :], y[:, tiles, :], ALU.add).then_inc(added, 1)

        @block.sync
        def _(sp):
            for c in range(NCH):
                tiles = slice(c * CT, (c + 1) * CT)
                sp.wait_ge(added, c + 1)
                sp.dma_start(out_rows[:, tiles, :], x[:, tiles, :]).then_inc(stored, 16)
            sp.wait_ge(stored, 16 * NCH)


def load_outputs(eng, y, y_rows, outputs_here):
    for c in range(NCH):
        tiles = slice(c * CT, (c + 1) * CT)
        eng.dma_start(y[:, tiles, :], y_rows[:, tiles, :]).then_inc(outputs_here[c], 16)


PARTS = 3
STACK = PARTS * PARTS * HD
BIG = 1e30


def staged(stages):
    for s in range(NCH + max(lag for _, lag in stages)):
        for f, lag in stages:
            if 0 <= s - lag < NCH:
                f(s - lag)


def part(a, c, k=None):
    first, n = (c * CT, CT) if k is None else (c * CT + k, 1)
    return a[:, first * C:(first + n) * C]


def layer_norm_stats(nc, stats, mv, vare, src, c, step, moments):
    for k in range(CT):
        last = nc.vector.bn_stats(stats[:, k, :], part(src, c, k))
    step(last)
    for k in range(CT):
        last = nc.vector.bn_aggr(mv[:, k, :], stats[:, k, :])
    step(last)
    nc.vector.tensor_scalar(vare[:, :], mv[:, :, 1], EPS, None, ALU.add).then_inc(moments, 1)


def load_stack(eng, b, n, qs, ks, stacked, q_dram, k_dram, pairs=range(PARTS * PARTS)):
    for c in pairs:
        rows = slice(c * HD, (c + 1) * HD)
        for dst, dram, r in ((qs[b], q_dram, c // PARTS), (ks[b], k_dram, c % PARTS)):
            eng.dma_start(dst[rows, :, :], dram[r, :, bass.ds(n * SEQ, SEQ)].rearrange("(h d) n -> d h n", d=HD)
                          ).then_inc(stacked[b], 16)


def load_values(eng, b, n, values, v_ones, values_here):
    wide = 2 * NH * (HD + 1)
    eng.dma_start(values[b][:, :], v_ones[:, bass.ds(n * wide, wide)]).then_inc(values_here[b], 16)


def project(nc, x, y, const, y_rows, outputs_here, v_ones, q_dram, k_dram, places):
    with ExitStack() as stack:
        def sb(name, shape, dt=FP32, n=2):
            return [stack.enter_context(nc.sbuf_tensor(f"p_{name}{p}", shape, dt)) for p in range(n)]

        def banks(name):
            return [stack.enter_context(nc.psum_tensor(f"p_{name}{p}", [P, CT * P], FP32)) for p in range(2)]

        def sem(name):
            return stack.enter_context(nc.semaphore("p_" + name))

        stats, mv = sb("stats", [P, CT, 6]), sb("mv", [P, CT, 2])
        vare, rstd = sb("vare", [P, CT]), sb("rstd", [P, CT])
        fresh = sb("fresh", [P, CT * C])
        xnT = sb("xnT", [P, CT * P])
        rest = {s: sb("rest_" + s, [P, CT * P]) for s in "qk"}
        split = {s: sb("split_" + s, [P, PARTS, CT * P], BF16, 3) for s in "qk"}
        xnT_bank, v_bank = banks("xnT_bank"), banks("v_bank")
        qk_bank = {s: banks("bank_" + s) for s in "qk"}
        moments, rstd_ready, dve_step = sem("moments"), sem("rstd"), sem("dve_step")
        xn_ready, xnT_psum, xnT_sbuf = sem("xn_ready"), sem("xnT_psum"), sem("xnT_sbuf")
        qk_psum, part0_ready, rest_ready, part1_ready, split_ready = (
            sem(n) for n in ("qk_psum", "part0", "rest", "part1", "split_ready"))
        kept = [sem(f"kept{p}") for p in range(3)]
        v_psum, v_sbuf, ones_set = sem("v_psum"), sem("v_sbuf"), sem("ones_set")
        block = stack.enter_context(nc.Block())

        @block.gpsimd
        def _(pool):
            nc.gpsimd.memset(v_ones[:, :, HD:HD + 1], 1.0).then_inc(ones_set, 1)

            def power(c):
                pool.wait_ge(moments, c + 1)
                nc.gpsimd.tensor_tensor(rstd[c % 2][:, :], vare[c % 2][:, :], const["minus_half"][:, 0:CT],
                                        ALU.pow).then_inc(rstd_ready, 1)

            def part2_of(c):
                for n, s in enumerate("qk"):
                    pool.wait_ge(part1_ready, 2 * c + 1 + n)
                    nc.gpsimd.tensor_tensor(split[s][c % 3][:, 2, :], rest[s][c % 2][:, :], split[s][c % 3][:, 1, :],
                                            ALU.subtract).then_inc(split_ready, 1)

            staged(((power, 0), (part2_of, 3)))

        @block.vector
        def _(dve):
            def add_and_norm(c):
                step = Steps(dve, dve_step, c, 3)
                dve.wait_ge(outputs_here[c], 16)
                step(nc.vector.tensor_tensor(part(x, c), part(x, c),
                                             y[:, c * CT:(c + 1) * CT, :].rearrange("p t c -> p (t c)"), ALU.add))
                layer_norm_stats(nc, stats[c % 2], mv[c % 2], vare[c % 2], x, c, step, moments)
                step.end()

            def xn_of(c):
                dve.wait_ge(rstd_ready, c + 1)
                if c >= 2:
                    dve.wait_ge(xnT_psum, c - 1)
                for k in range(CT):
                    last = nc.vector.tensor_scalar(fresh[c % 2][:, k * C:(k + 1) * C], part(x, c, k),
                                                   mv[c % 2][:, k, 0:1], rstd[c % 2][:, k:k + 1],
                                                   ALU.subtract, ALU.mult)
                last.then_inc(xn_ready, 1)

            def rest_of(c):
                for n, s in enumerate("qk"):
                    dve.wait_ge(part0_ready, 2 * c + 1 + n)
                    if c >= 2:
                        dve.wait_ge(split_ready, 2 * (c - 2) + 1 + n)
                    nc.vector.tensor_tensor(rest[s][c % 2][:, :], qk_bank[s][c % 2][:, :], split[s][c % 3][:, 0, :],
                                            ALU.subtract).then_inc(rest_ready, 1)

            staged(((rest_of, 3), (add_and_norm, 0), (xn_of, 1)))

        @block.scalar
        def _(act):
            def part1_of(c):
                for n, s in enumerate("qk"):
                    act.wait_ge(rest_ready, 2 * c + 1 + n)
                    nc.scalar.copy(split[s][c % 3][:, 1, :], rest[s][c % 2][:, :]).then_inc(part1_ready, 1)

            def keep_values(c):
                act.wait_ge(v_psum, c + 1)
                act.wait_ge(ones_set, 1)
                nc.scalar.copy(v_ones[:, c * CT * NH:(c + 1) * CT * NH, 0:HD],
                               v_bank[c % 2][:, :].rearrange("p (g d) -> p g d", d=HD)).then_inc(v_sbuf, 1)

            def xn_turned(c):
                act.wait_ge(xnT_psum, c + 1)
                if c >= 2:
                    act.wait_ge(v_psum, c - 1)
                nc.scalar.copy(xnT[c % 2][:, :], xnT_bank[c % 2][:, :]).then_inc(xnT_sbuf, 1)

            def part0_of(c):
                for n, s in enumerate("qk"):
                    act.wait_ge(qk_psum, 2 * c + 1 + n)
                    if c >= 3:
                        act.wait_ge(kept[c % 3], 2 * 16 * (c // 3))
                    nc.scalar.copy(split[s][c % 3][:, 0, :], qk_bank[s][c % 2][:, :]).then_inc(part0_ready, 1)

            staged(((part1_of, 3), (keep_values, 2), (xn_turned, 1), (part0_of, 1)))

        @block.sync
        def _(sp):
            RETURNS = NCH - 3
            load_outputs(sp, y, y_rows, outputs_here)
            for c in range(NCH):
                for n, (s, dram) in enumerate((("q", q_dram), ("k", k_dram))):
                    sp.wait_ge(split_ready, 2 * c + 1 + n)
                    sp.dma_start(dram[:, :, c * CT * P:(c + 1) * CT * P].rearrange("r p n -> p r n"),
                                 split[s][c % 3][:, :, :]).then_inc(kept[c % 3], 16)
                if c == 1:
                    sp.wait_ge(kept[0], 2 * 16)
                    sp.wait_ge(v_sbuf, 1)
                    for b in range(2):
                        load_values(sp, b, b, places["values"], places["v_flat"], places["values_here"])
                if 1 <= c <= RETURNS:
                    for n in range((c - 1) * 2 * PARTS * PARTS // RETURNS, c * 2 * PARTS * PARTS // RETURNS):
                        b, pair = divmod(n, PARTS * PARTS)
                        load_stack(sp, b, b, places["qs"], places["ks"], places["stacked"], q_dram, k_dram, [pair])
            for p in range(3):
                sp.wait_ge(kept[p], 2 * 16 * len(range(p, NCH, 3)))

        @block.tensor
        def _(pe):
            def turn(c):
                pe.wait_ge(xn_ready, c + 1)
                if c >= 2:
                    pe.wait_ge(xnT_sbuf, c - 1)
                for k in range(CT):
                    last = nc.tensor.transpose(xnT_bank[c % 2][:, k * P:(k + 1) * P], fresh[c % 2][:, k * C:(k + 1) * C],
                                               const["ident"][:, :])
                last.then_inc(xnT_psum, 1)

            def products(c):
                pe.wait_ge(xnT_sbuf, c + 1)
                for n, s in enumerate("qk"):
                    if c >= 2:
                        pe.wait_ge(rest_ready, 2 * (c - 2) + 1 + n)
                    nc.tensor.matmul(qk_bank[s][c % 2][:, :], const["w" + s][:, :], xnT[c % 2][:, :],
                                     start=True, stop=True).then_inc(qk_psum, 1)
                if c >= 2:
                    pe.wait_ge(v_sbuf, c - 1)
                for k in range(CT):
                    last = nc.tensor.matmul(v_bank[c % 2][:, k * C:(k + 1) * C], xnT[c % 2][:, k * P:(k + 1) * P],
                                            const["wv"][:, :], start=True, stop=True)
                last.then_inc(v_psum, 1)

            staged(((turn, 1), (products, 1)))


def attend(nc, const, v_ones, table, q_dram, k_dram, places, ctx_out):
    GAP = 32
    PER = P // GAP
    W = 4
    UNIT = 8 * P
    per_batch = [(0, 8 * g, 8) for g in range(2)] + [(1, 4 * g, 4) for g in range(4)]
    UNITS = [(b, tile, head, heads) for b in range(2) for tile, head, heads in per_batch]
    NU = len(UNITS)
    TOTAL = NU * BATCH // 2
    with ExitStack() as stack:
        def sb(name, shape, dt=FP32):
            return stack.enter_context(nc.sbuf_tensor("t_" + name, shape, dt))

        def bank(name, n=1):
            return stack.enter_context(nc.psum_tensor("t_" + name, [P, 512 * n], FP32))

        def sem(name):
            return stack.enter_context(nc.semaphore("t_" + name))

        qs, ks, values = places["qs"], places["ks"], places["values"]
        stacked, values_here = places["stacked"], places["values_here"]
        relus = [sb(f"relu{p}", [P, UNIT]) for p in range(2)]
        weighted = [sb(f"weighted{p}", [P, UNIT]) for p in range(W)]
        tops = [sb(f"top{p}", [P, 8]) for p in range(W)]
        gate = sb("gate", [P, W])
        ctxT = [sb(f"ctxT{p}", [P, NH // PER * P]) for p in range(2)]
        probs = [sb(f"probs{p}", [P, UNIT]) for p in range(2)]
        recs = [sb(f"rec{p}", [P, NH]) for p in range(2)]
        score_banks = [bank(f"score{p}", 2) for p in range(2)]
        turned_bank = [bank(f"turned{p}") for p in range(2)]
        ctxT_bank, ctx_bank = bank("ctxT_bank"), bank("ctx_bank")
        scored, relu_done, weighted_done, shifted, turned, exped, averaged = (sem(n) for n in (
            "scored", "relu_done", "weighted_done", "shifted", "turned", "exped", "averaged"))
        bank_blank, ctxT_sbuf, turned_back, rec_done, ctx_done = (sem(n) for n in (
            "bank_blank", "ctxT_sbuf", "turned_back", "rec_done", "ctx_done"))
        block = stack.enter_context(nc.Block())

        def in_steps(eng, stages):
            lags = max(lag for _, lag in stages)
            for s in range(NU):
                for f, lag in stages:
                    if s >= lag:
                        f(s - lag, s - lag, 0)
            with eng.Fori(1, BATCH // 2) as i:
                for s in range(NU):
                    for f, lag in stages:
                        f(i * NU + (s - lag), (s - lag) % NU, i if s >= lag else i - 1)
            for s in range(TOTAL, TOTAL + lags):
                for f, lag in stages:
                    if s - lag < TOTAL:
                        f(s - lag, (s - lag) % NU, BATCH // 2 - 1)

        def first(g, n):
            return isinstance(g, int) and g < n

        group = [2 * b + tile for b, tile, _, _ in UNITS]
        ends = [u + 1 == NU or group[u + 1] != group[u] for u in range(NU)]
        begins = [u == 0 or group[u - 1] != group[u] for u in range(NU)]

        @block.sync
        def _(sp):
            with nc.sync.Fori(1, BATCH // 2) as i:
                for b in range(2):
                    sp.wait_ge(scored, i * NU + (NU // 2) * (b - 1))
                    load_stack(sp, b, i * 2 + b, qs, ks, stacked, q_dram, k_dram)
                    sp.wait_ge(averaged, i * NU + (NU // 2) * (b - 1))
                    load_values(sp, b, i * 2 + b, values, v_ones, values_here)

        @block.tensor
        def _(pe):
            def scores(g, u, pair):
                b, tile, head, heads = UNITS[u]
                keys = (tile + 1) * P
                out = score_banks[u % 2]
                if u % (NU // 2) == 0:
                    pe.wait_ge(stacked[b], (pair + 1) * (16 * 2 * PARTS * PARTS))
                if not first(g, 2):
                    pe.wait_ge(relu_done, g - 1)
                for half in range(2):
                    per = heads // 2
                    own = out[:, half * 512:(half + 1) * 512].rearrange("p (h k) -> p h k", h=per)
                    nc.tensor.matmul(own[:, :, keys - P:keys], const["ident16"][:, :],
                                     const["after"][:, :].unsqueeze(1).broadcast_to((P, per, P)),
                                     start=True, stop=False, skip_group_check=True)
                    for k in range(per):
                        h = head + half * per + k
                        last = nc.tensor.matmul(own[:, k, :], qs[b][:, h, tile * P:(tile + 1) * P],
                                                ks[b][:, h, 0:keys], start=False, stop=True, skip_group_check=True)
                last.then_inc(scored, 1)

            def turn(g, u, pair):
                pe.wait_ge(shifted, g + 1)
                for half in range(2):
                    if not first(g, 1):
                        pe.wait_ge(exped, g * 2 + (half - 1))
                    for j in range(4):
                        last = nc.tensor.transpose(turned_bank[half][:, j * P:(j + 1) * P],
                                                   weighted[u % W][:, (half * 4 + j) * P:(half * 4 + j + 1) * P],
                                                   const["ident"][:, :])
                    last.then_inc(turned, 1)

            def average(g, u, pair):
                b, tile, head, heads = UNITS[u]
                blocks = tile + 1
                if u % (NU // 2) == 0:
                    pe.wait_ge(values_here[b], (pair + 1) * 16)
                if first(g, 1):
                    pe.wait_ge(bank_blank, 1)
                elif begins[u]:
                    pe.wait_ge(ctxT_sbuf, pair * 4 + group[u])
                pe.wait_ge(exped, g * 2 + 2)
                for quad in range(heads // PER):
                    for j in range(blocks):
                        for k in range(PER):
                            h = head + quad * PER + k
                            n = (quad * PER + k) * blocks + j
                            last = nc.tensor.matmul(
                                ctxT_bank[k * GAP:k * GAP + HD + 1, h // PER * P:(h // PER + 1) * P],
                                values[b][:, (j * NH + h) * (HD + 1):(j * NH + h + 1) * (HD + 1)],
                                probs[u % 2][:, n * P:(n + 1) * P], start=(j == 0), stop=(j == blocks - 1),
                                skip_group_check=True)
                last.then_inc(averaged, 1)

            def turn_back(g, u, pair):
                if not ends[u]:
                    return
                done = pair * 4 + group[u]
                pe.wait_ge(ctxT_sbuf, done + 1)
                if not first(done, 1):
                    pe.wait_ge(ctx_done, done)
                for n in range(NH // PER):
                    last = nc.tensor.transpose(ctx_bank[:, n * P:(n + 1) * P], ctxT[group[u] % 2][:, n * P:(n + 1) * P],
                                               const["ident"][:, :])
                last.then_inc(turned_back, 1)

            in_steps(nc.tensor, ((scores, 0), (turn, 4), (average, 5), (turn_back, 6)))

        @block.vector
        def _(dve):
            def weigh(g, u, pair):
                b, tile, head, heads = UNITS[u]
                keys = (tile + 1) * P
                dve.wait_ge(relu_done, g + 1)
                if not first(g, W):
                    dve.wait_ge(turned, (g - W) * 2 + 2)
                nc.vector.memset(gate[:, u % W:u % W + 1], 0.0)
                for k in range(heads):
                    own = slice(k * keys, (k + 1) * keys)
                    last = nc.vector.tensor_tensor_reduce(
                        out=weighted[u % W][:, own], in0=relus[u % 2][:, own], in1=table[:, head + k, SEQ - keys:SEQ],
                        scale=1.0, scalar=0.0, op0=ALU.mult, op1=ALU.max, accum_out=tops[u % W][:, k:k + 1])
                last.then_inc(weighted_done, 1)

            def divide(g, u, pair):
                if not ends[u]:
                    return
                done = pair * 4 + group[u]
                ctx = ctx_bank[:, :].rearrange("p (h d) -> p h d", d=GAP)
                rec = recs[group[u] % 2]
                dve.wait_ge(turned_back, done + 1)
                nc.vector.reciprocal(rec[:, :], ctx[:, :, HD]).then_inc(rec_done, 1)
                dve.wait_ge(rec_done, done + 1)
                nc.vector.tensor_tensor(ctx_out[:, bass.ds(done * C, C)].rearrange("p (h d) -> p h d", h=NH),
                                        ctx[:, :, 0:HD], rec[:, :].unsqueeze(2).broadcast_to((P, NH, HD)),
                                        ALU.mult).then_inc(ctx_done, 1)

            nc.vector.memset(ctxT_bank[:, :], 0.0).then_inc(bank_blank, 1)
            in_steps(nc.vector, ((weigh, 0), (divide, 7)))

        @block.gpsimd
        def _(pool):
            def shift(g, u, pair):
                b, tile, head, heads = UNITS[u]
                view = weighted[u % W][:, :].rearrange("p (h k) -> p h k", h=heads)
                pool.wait_ge(weighted_done, g + 1)
                nc.gpsimd.tensor_tensor(view, view, tops[u % W][:, 0:heads].unsqueeze(2).broadcast_to(
                    (P, heads, (tile + 1) * P)), ALU.subtract).then_inc(shifted, 1)

            in_steps(nc.gpsimd, ((shift, 0),))

        @block.scalar
        def _(act):
            def relu(g, u, pair):
                act.wait_ge(scored, g + 1)
                if not first(g, 2):
                    act.wait_ge(weighted_done, g - 1)
                nc.scalar.activation(relus[u % 2][:, :], score_banks[u % 2][:, :], ACT.Relu).then_inc(relu_done, 1)

            def exp(g, u, pair):
                if not first(g, 2):
                    act.wait_ge(averaged, g - 1)
                for half in range(2):
                    act.wait_ge(turned, g * 2 + (half + 1))
                    nc.scalar.activation(probs[u % 2][:, half * 512:(half + 1) * 512], turned_bank[half][:, :],
                                         ACT.Exp).then_inc(exped, 1)

            def keep_ctxT(g, u, pair):
                if not ends[u]:
                    return
                done = pair * 4 + group[u]
                act.wait_ge(averaged, g + 1)
                if not first(done, 2):
                    act.wait_ge(turned_back, done - 1)
                nc.scalar.copy(ctxT[group[u] % 2][:, :], ctxT_bank[:, :]).then_inc(ctxT_sbuf, 1)

            in_steps(nc.scalar, ((relu, 0), (exp, 4), (keep_ctxT, 5)))


def attention_out(nc, x, ctx, routed, w, const, logits_bank):
    with ExitStack() as stack:
        def sb(name, shape, dt=FP32):
            return [stack.enter_context(nc.sbuf_tensor(f"o_{name}{p}", shape, dt)) for p in range(2)]

        def banks(name):
            return [stack.enter_context(nc.psum_tensor(f"o_{name}{p}", [P, CT * P], FP32)) for p in range(2)]

        def sem(name):
            return stack.enter_context(nc.semaphore("o_" + name))

        stats, mv = sb("stats", [P, CT, 6]), sb("mv", [P, CT, 2])
        vare, rstd = sb("vare", [P, CT]), sb("rstd", [P, CT])
        ctxT, xnT = sb("ctxT", [P, CT * P]), sb("xnT", [P, CT * P])
        ctxT_bank, out_bank, xnT_bank = banks("ctxT_bank"), banks("out_bank"), banks("xnT_bank")
        moments, rstd_ready, dve_step, x_plus = sem("moments"), sem("rstd"), sem("dve_step"), sem("x_plus")
        ctxT_psum, ctxT_sbuf, out_psum = sem("ctxT_psum"), sem("ctxT_sbuf"), sem("out_psum")
        xn_ready, xnT_psum, xnT_sbuf, logits_psum = sem("xn_ready"), sem("xnT_psum"), sem("xnT_sbuf"), sem("logits")
        block = stack.enter_context(nc.Block())

        @block.vector
        def _(dve):
            def add_and_norm(c):
                step = Steps(dve, dve_step, c, 3)
                dve.wait_ge(x_plus, c + 1)
                dve.wait_ge(out_psum, c + 1)
                step(nc.vector.tensor_tensor(part(x, c), out_bank[c % 2][:, :], part(x, c), ALU.add))
                layer_norm_stats(nc, stats[c % 2], mv[c % 2], vare[c % 2], x, c, step, moments)
                step.end()

            def xn_of(c):
                dve.wait_ge(rstd_ready, c + 1)
                for k in range(CT):
                    last = nc.vector.tensor_scalar(routed[:, c * CT + k, 0:C], part(x, c, k), mv[c % 2][:, k, 0:1],
                                                   rstd[c % 2][:, k:k + 1], ALU.subtract, ALU.mult)
                last.then_inc(xn_ready, 1)

            staged(((add_and_norm, 1), (xn_of, 2)))

        @block.gpsimd
        def _(pool):
            def add_bo(c):
                xc = part(x, c).rearrange("p (t n) -> p t n", t=CT)
                nc.gpsimd.tensor_tensor(xc, xc, const["bo"][:, :].unsqueeze(1).broadcast_to((P, CT, C)),
                                        ALU.add).then_inc(x_plus, 1)

            def power(c):
                pool.wait_ge(moments, c + 1)
                nc.gpsimd.tensor_tensor(rstd[c % 2][:, :], vare[c % 2][:, :], const["minus_half"][:, 0:CT],
                                        ALU.pow).then_inc(rstd_ready, 1)

            number_tokens(nc, routed)
            staged(((add_bo, 0), (power, 1)))

        @block.scalar
        def _(act):
            def ctx_turned(c):
                act.wait_ge(ctxT_psum, c + 1)
                if c >= 2:
                    act.wait_ge(out_psum, c - 1)
                nc.scalar.copy(ctxT[c % 2][:, :], ctxT_bank[c % 2][:, :]).then_inc(ctxT_sbuf, 1)

            def xn_turned(c):
                act.wait_ge(xnT_psum, c + 1)
                if c >= 2:
                    act.wait_ge(logits_psum, c - 1)
                nc.scalar.copy(xnT[c % 2][:, :], xnT_bank[c % 2][:, :]).then_inc(xnT_sbuf, 1)

            staged(((ctx_turned, 0), (xn_turned, 4)))

        @block.tensor
        def _(pe):
            def turn_ctx(c):
                if c >= 2:
                    pe.wait_ge(ctxT_sbuf, c - 1)
                for k in range(CT):
                    last = nc.tensor.transpose(ctxT_bank[c % 2][:, k * P:(k + 1) * P], part(ctx, c, k),
                                               const["ident"][:, :])
                last.then_inc(ctxT_psum, 1)

            def out(c):
                pe.wait_ge(ctxT_sbuf, c + 1)
                if c >= 2:
                    pe.wait_ge(dve_step, 3 * (c - 2) + 1)
                for k in range(CT):
                    last = nc.tensor.matmul(out_bank[c % 2][:, k * C:(k + 1) * C], ctxT[c % 2][:, k * P:(k + 1) * P],
                                            const["wo"][:, :], start=True, stop=True)
                last.then_inc(out_psum, 1)

            def turn_xn(c):
                pe.wait_ge(xn_ready, c + 1)
                if c >= 2:
                    pe.wait_ge(xnT_sbuf, c - 1)
                for k in range(CT):
                    last = nc.tensor.transpose(xnT_bank[c % 2][:, k * P:(k + 1) * P], routed[:, c * CT + k, 0:C],
                                               const["ident"][:, :])
                last.then_inc(xnT_psum, 1)

            def logits(c):
                pe.wait_ge(xnT_sbuf, c + 1)
                for k in range(CT):
                    t = c * CT + k
                    last = nc.tensor.matmul(logits_bank[:, t * NE:(t + 1) * NE], xnT[c % 2][:, k * P:(k + 1) * P],
                                            w["wg"][:, :], start=True, stop=True)
                last.then_inc(logits_psum, 1)

            staged(((turn_ctx, 0), (turn_xn, 4), (out, 1), (logits, 4)))


INPUTS = ["L0_attn_a_x", "L0_attn_a_w1", "L0_attn_a_b1", "L0_attn_a_w2", "L0_attn_a_b2", "L0_attn_a_gamma1",
          "L0_attn_a_beta1", "L0_attn_a_gamma2", "L0_attn_a_beta2", "L0_attn_b_Wq", "L0_attn_b_Wk", "L0_attn_b_Wv",
          "L0_attn_b_Wo", "L0_attn_b_bo", "L0_attn_b_w", "L0_attn_b_v", "L0_ffn_W1", "L0_ffn_W2", "L0_ffn_Wg",
          "L0_ffn_bg"]


def program(nc, ins, out):
    slots = [nc.dram_tensor(f"slots{n}", [SLOT_TILES * P, ROW], FP32, kind="Internal").ap() for n in range(2)]
    y_dram = nc.dram_tensor("expert_out", [TOK + SLOT_TILES * P, C], FP32, kind="Internal").ap()
    q_dram = nc.dram_tensor("query_parts", [PARTS, P, TOK], BF16, kind="Internal").ap()
    k_dram = nc.dram_tensor("key_parts", [PARTS, P, TOK], BF16, kind="Internal").ap()
    with ExitStack() as stack:
        def sb(name, shape, dt=FP32):
            return stack.enter_context(nc.sbuf_tensor(name, shape, dt))

        x = sb("x", [P, NT * C])
        w = dict(w1=sb("w1", [P, NE * HID]), w2=sb("w2", [P, NE * HID]), wg=sb("wg", [P, NE]))
        const = dict(
            ident=sb("ident", [P, P]), before=sb("before", [P, P], BF16), ones=sb("ones", [P, P], BF16),
            zero=sb("zero", [P, NE * NT]), order=sb("order", [P, NE]), tileno=sb("tileno", [P, SLOT_TILES]),
            minus_half=sb("minus_half", [P, 8]), half_pi=sb("half_pi", [P, 1]),
            slot=sb("slot", [P, NT], U32), tile_expert=sb("tile_expert", [P, SLOT_TILES], I32),
            six_experts=sb("six_experts", [P, SLOT_TILES - SIX + 1], I32),
            ident16=sb("ident16", [P, P], BF16), after=sb("after", [P, P], BF16),
            wq=sb("wq", [P, C]), wk=sb("wk", [P, C]), wv=sb("wv", [P, C]), wo=sb("wo", [P, C]),
            w1T=sb("w1T", [NQ, FFN]), w2T=sb("w2T", [P, NFC, C]), b1=sb("b1", [P, NFC]))
        rows = {"b2": "L0_attn_a_b2", "gamma1": "L0_attn_a_gamma1", "beta1": "L0_attn_a_beta1",
                "gamma2": "L0_attn_a_gamma2", "beta2": "L0_attn_a_beta2", "bo": "L0_attn_b_bo", "bg": "L0_ffn_bg",
                "w": "L0_attn_b_w", "v": "L0_attn_b_v"}
        for name, source in rows.items():
            const[name] = sb(name, [P, ins[source].shape[0]])
        t2 = sb("t2", [P, NT * C])
        table = sb("table", [P, NH, SEQ])
        y_rows, out_rows = (a.rearrange("(t p) c -> p t c", p=P) for a in (y_dram[0:TOK, :], out))
        x_here = [stack.enter_context(nc.semaphore(f"x_here{c}")) for c in range(NCH)]
        outputs_here = [stack.enter_context(nc.semaphore(f"outputs_here{c}")) for c in range(NCH)]
        loads = stack.enter_context(nc.semaphore("loads"))
        slots_empty = stack.enter_context(nc.semaphore("slots_empty"))
        big_here = stack.enter_context(nc.semaphore("big_here"))
        view = "p (t c) -> p t c"
        x3, t23 = x[:, :].rearrange(view, c=C), t2[:, :].rearrange(view, c=C)
        with ExitStack() as inner:
            const["logits_bank"] = inner.enter_context(nc.psum_tensor("logits_bank", [P, NT * NE], FP32))
            routed = inner.enter_context(nc.sbuf_tensor("routed", [P, NT, ROW], FP32))
            blank = inner.enter_context(nc.sbuf_tensor("blank", [P, SLOT_TILES, ROW], FP32))
            setup(nc, ins, x, blank, w, const, rows, x_here, loads)

            def load_later(sp):
                for slots_dram in slots:
                    sp.dma_start(slots_dram.rearrange("(t p) c -> p t c", p=P), blank[:, :, :]).then_inc(slots_empty, 16)
                large = [(const["w" + s][:, :], ins["L0_attn_b_W" + s]) for s in "qkvo"]
                large.append((w["w1"][:, :].rearrange("p (e h) -> p e h", e=NE), ins["L0_ffn_W1"].rearrange("e d h -> d e h")))
                large.append((w["w2"][:, :].rearrange("p (e k c) -> p e k c", e=NE, k=NHC),
                              ins["L0_ffn_W2"].rearrange("e (k p) c -> p e k c", p=P)))
                for dst, src in large:
                    sp.dma_start(dst, src).then_inc(big_here, 16)
                assert BIG_LOADS == 16 * len(large)

            with ExitStack() as scratch:
                y, t1, xb = (scratch.enter_context(nc.sbuf_tensor(n, [P, NT * C], FP32)) for n in ("y", "t1", "xb"))
                block_a(nc, x, y, t1, t2, xb, w, const, x_here, loads, load_later, routed)
            route(nc, "r1_", routed, const, slots[0], slots_empty, table, big_here)
        expert_tiles(nc, "e1_", w, const, slots[0], y_dram)
        with ExitStack() as inner:
            def inner_sb(name, shape, dt=FP32):
                return inner.enter_context(nc.sbuf_tensor(name, shape, dt))

            v_ones = inner_sb("v_ones", [P, NT * NH * (HD + 1)])
            places = dict(qs=[inner_sb(f"qs{b}", [STACK, NH, SEQ], BF16) for b in range(2)],
                          ks=[inner_sb(f"ks{b}", [STACK, NH, SEQ], BF16) for b in range(2)],
                          values=[inner_sb(f"values{b}", [P, 2 * NH * (HD + 1)]) for b in range(2)],
                          v_flat=v_ones,
                          stacked=[inner.enter_context(nc.semaphore(f"stacked{b}")) for b in range(2)],
                          values_here=[inner.enter_context(nc.semaphore(f"values_here{b}")) for b in range(2)])
            project(nc, x, t23, const, y_rows, outputs_here, v_ones[:, :].rearrange("p (g d) -> p g d", d=HD + 1),
                    q_dram, k_dram, places)
            attend(nc, const, v_ones, table, q_dram, k_dram, places, t2)
        with ExitStack() as inner:
            const["logits_bank"] = inner.enter_context(nc.psum_tensor("logits_bank2", [P, NT * NE], FP32))
            routed = inner.enter_context(nc.sbuf_tensor("routed2", [P, NT, ROW], FP32))
            attention_out(nc, x, t2, routed, w, const, const["logits_bank"])
            route(nc, "r2_", routed, const, slots[1], slots_empty)
        expert_tiles(nc, "e2_", w, const, slots[1], y_dram)
        combine_and_store(nc, x3, t23, y_rows, outputs_here, out_rows)


def setup(nc, ins, x, blank, w, const, rows, x_here, loads):
    with ExitStack() as stack:
        pool_made = stack.enter_context(nc.semaphore("pool_made"))
        block = stack.enter_context(nc.Block())
        token_tiles = ins["L0_attn_a_x"].rearrange("b s c -> (b s) c").rearrange("(t p) c -> p t c", p=P)
        xt = x[:, :].rearrange("p (t c) -> p t c", c=C)

        @block.scalar
        def _(act):
            for c in range(NCH):
                tiles = slice(c * CT, (c + 1) * CT)
                act.dma_start(xt[:, tiles, :], token_tiles[:, tiles, :]).then_inc(x_here[c], 16)

        @block.sync
        def _(sp):
            small = [(const["w1T"][:, :], ins["L0_attn_a_w1"]),
                     (const["w2T"][:, :, :], ins["L0_attn_a_w2"].rearrange("(f p) c -> p f c", p=P)),
                     (const["b1"][:, :], ins["L0_attn_a_b1"]), (w["wg"][:, :], ins["L0_ffn_Wg"])]
            for name, source in rows.items():
                src = ins[source]
                small.append((const[name][:, :], src.unsqueeze(0).broadcast_to((P, src.shape[0]))))
            for dst, src in small:
                sp.dma_start(dst, src).then_inc(loads, 16)
            assert SMALL_LOADS == 16 * len(small)

        @block.vector
        def _(dve):
            nc.vector.memset(blank[:, :, 0:C], 0.0)

        @block.gpsimd
        def _(pool):
            nc.gpsimd.iota(blank[:, :, C:ROW], pattern=[[P, SLOT_TILES], [0, 1]], base=TOK, channel_multiplier=1,
                           allow_small_or_imprecise_dtypes=True)
            nc.gpsimd.memset(const["zero"][:, :], 0.0)
            nc.gpsimd.memset(const["ident"][:, :], 0.0)
            nc.gpsimd.memset(const["before"][:, :], 1.0)
            nc.gpsimd.memset(const["ident16"][:, :], 0.0)
            nc.gpsimd.memset(const["after"][:, :], 0.0)
            nc.gpsimd.memset(const["ones"][:, :], 1.0)
            nc.gpsimd.memset(const["minus_half"][:, :], -0.5)
            nc.gpsimd.memset(const["half_pi"][:, :], np.pi / 2)
            nc.gpsimd.iota(const["order"][:, :], pattern=[[-1, NE]], base=NE, channel_multiplier=0,
                           allow_small_or_imprecise_dtypes=True)
            nc.gpsimd.iota(const["tileno"][:, :], pattern=[[1, SLOT_TILES]], base=0, channel_multiplier=0,
                           allow_small_or_imprecise_dtypes=True).then_inc(pool_made, 1)
            pool.wait_ge(pool_made, 1)
            nc.gpsimd.affine_select(out=const["ident"][:, :], in_=const["ident"][:, :], compare_op=ALU.not_equal,
                                    fill=1.0, base=0, pattern=[[-1, P]], channel_multiplier=1)
            nc.gpsimd.affine_select(out=const["ident16"][:, :], in_=const["ident16"][:, :], compare_op=ALU.not_equal,
                                    fill=1.0, base=0, pattern=[[-1, P]], channel_multiplier=1)
            nc.gpsimd.affine_select(out=const["after"][:, :], in_=const["after"][:, :], compare_op=ALU.is_ge,
                                    fill=BIG, base=0, pattern=[[-1, P]], channel_multiplier=1)
            nc.gpsimd.affine_select(out=const["before"][:, :], in_=const["before"][:, :], compare_op=ALU.is_gt,
                                    fill=0.0, base=0, pattern=[[1, P]], channel_multiplier=-1).then_inc(pool_made, 1)
            pool.wait_ge(pool_made, 2)


def kernel(**inputs):
    import numpy as _np
    import concourse.bacc as _bacc
    from concourse import mybir as _mybir
    from concourse.bass_utils import run_bass_kernel_spmd as _run

    nc = _bacc.Bacc("TRN2", target_bir_lowering=False, num_devices=1)
    arrays, args = {}, {}
    for name in INPUTS:
        a = _np.asarray(inputs[name])
        if name in ("L0_attn_a_w1", "L0_attn_a_w2"):
            a = a.T
        if name == "L0_attn_a_b1":
            a = a.reshape(NFC, P).T
        a = _np.ascontiguousarray(a)
        arrays["in_" + name] = a
        args[name] = nc.dram_tensor("in_" + name, a.shape, _mybir.dt.from_np(a.dtype), kind="ExternalInput").ap()
    out = nc.dram_tensor("out_0", (TOK, C), _mybir.dt.float32, kind="ExternalOutput").ap()
    program(nc, args, out)
    r = _run(nc, [arrays], core_ids=[0])
    return _np.asarray(r.results[0]["out_0"]).reshape(BATCH, SEQ, C)
```
